# Optimizing a Trainium2 kernel written in Bass

```python
import numpy as np
import jax
import jax.numpy as jnp

def _softmax(x, axis=-1):
    return jax.nn.softmax(x, axis=axis)
def _gelu(x):
    return jax.nn.gelu(x, approximate=True)
def _silu(x):
    return jax.nn.silu(x)
def _sigmoid(x):
    return jax.nn.sigmoid(x)
def _layernorm(x, axis=-1, eps=1e-5):
    m = jnp.mean(x, axis=axis, keepdims=True)
    v = jnp.var(x, axis=axis, keepdims=True)
    return (x - m) / jnp.sqrt(v + eps)
def _scatter_add(tgt, idx, src, axis=0):
    return tgt.at[idx].add(src)
def _segment_sum(src, seg, n):
    return jax.ops.segment_sum(src, seg, n)

kernel_name = 'mk_conv_preact_d2_conv_nhwc256_b2032e'

def setup_inputs(seed: int = 0):
    np.random.seed(seed)
    _w = jnp.asarray
    def _rec_inputs():
        import jax
        import jax.numpy as jnp
        _gk = jax.random.key(seed)
        x = 7.22e-05 + 1 * jax.random.normal(jax.random.fold_in(_gk, 1), (1, 128, 256, 256), jnp.float32)
        return x
    x = _rec_inputs()
    def _L0_conv_setup():
        import jax, jax.numpy as jnp
        import numpy as np
        C_Z, H_Z, W_Z, NH, C = (128, 256, 256, 4, 64)
        EPS = 1e-05
        key = jax.random.key(seed)
        ks = jax.random.split(key, 8)
        s = 0.02
        return {'pair_rep': jax.random.normal(ks[0], (1, C_Z, H_Z, W_Z), jnp.float32), 'ln_w': jnp.ones((C_Z, H_Z, W_Z), jnp.float32), 'ln_b': jnp.zeros((C_Z, H_Z, W_Z), jnp.float32), 'wq': jax.random.normal(ks[1], (NH * C, C_Z), jnp.float32) * s, 'wk': jax.random.normal(ks[2], (NH * C, C_Z), jnp.float32) * s, 'wv': jax.random.normal(ks[3], (NH * C, C_Z), jnp.float32) * s, 'wb': jax.random.normal(ks[4], (NH, C_Z), jnp.float32) * s, 'wg_w': jax.random.normal(ks[5], (NH * C, C_Z), jnp.float32) * s, 'wg_b': jnp.zeros((NH * C,), jnp.float32), 'wrep_w': jax.random.normal(ks[6], (C_Z, NH * C), jnp.float32) * s, 'wrep_b': jnp.zeros((C_Z,), jnp.float32)}
    _L0_conv_all = _L0_conv_setup()
    _L0_conv_in = {k: v for k, v in _L0_conv_all.items() if k in ('ln_w', 'ln_b', 'wq', 'wk', 'wv', 'wb', 'wg_w', 'wg_b', 'wrep_w', 'wrep_b', )}
    del _L0_conv_all

    def _L1_conv_setup():
        import jax, jax.numpy as jnp
        import numpy as np
        HEAD = 8
        C = 32
        SCALE = 1.0 / C ** 0.5
        key = jax.random.key(seed)
        ks = jax.random.split(key, 6)
        N, S, R, M, Z = (1, 128, 256, 256, 128)
        return {'msa_repr': jax.random.normal(ks[0], (N, S, R, M), jnp.float32), 'pair_repr': jax.random.normal(ks[1], (N, R, R, Z), jnp.float32), 'gate_proj': jax.random.normal(ks[2], (M, M), jnp.float32) * 0.05, 'qkv_proj': jax.random.normal(ks[3], (M, 3 * M), jnp.float32) * 0.05, 'out_proj': jax.random.normal(ks[4], (M, M), jnp.float32) * 0.05, 'bias_proj': jax.random.normal(ks[5], (Z, HEAD), jnp.float32) * 0.05}
    _L1_conv_all = _L1_conv_setup()
    _L1_conv_in = {k: v for k, v in _L1_conv_all.items() if k in ('pair_repr', 'gate_proj', 'qkv_proj', 'out_proj', 'bias_proj', )}
    del _L1_conv_all

    return {
        "x": x,
        "L0_conv_ln_w": _L0_conv_in["ln_w"],
        "L0_conv_ln_b": _L0_conv_in["ln_b"],
        "L0_conv_wq": _L0_conv_in["wq"],
        "L0_conv_wk": _L0_conv_in["wk"],
        "L0_conv_wv": _L0_conv_in["wv"],
        "L0_conv_wb": _L0_conv_in["wb"],
        "L0_conv_wg_w": _L0_conv_in["wg_w"],
        "L0_conv_wg_b": _L0_conv_in["wg_b"],
        "L0_conv_wrep_w": _L0_conv_in["wrep_w"],
        "L0_conv_wrep_b": _L0_conv_in["wrep_b"],
        "L1_conv_pair_repr": _L1_conv_in["pair_repr"],
        "L1_conv_gate_proj": _L1_conv_in["gate_proj"],
        "L1_conv_qkv_proj": _L1_conv_in["qkv_proj"],
        "L1_conv_out_proj": _L1_conv_in["out_proj"],
        "L1_conv_bias_proj": _L1_conv_in["bias_proj"],
    }

def reference(x, L0_conv_ln_w, L0_conv_ln_b, L0_conv_wq, L0_conv_wk, L0_conv_wv, L0_conv_wb, L0_conv_wg_w, L0_conv_wg_b, L0_conv_wrep_w, L0_conv_wrep_b, L1_conv_pair_repr, L1_conv_gate_proj, L1_conv_qkv_proj, L1_conv_out_proj, L1_conv_bias_proj):
    import jax
    import jax.numpy as jnp
    def _L0_conv_ref(pair_rep, ln_w, ln_b, wq, wk, wv, wb, wg_w, wg_b, wrep_w, wrep_b):
        import jax, jax.numpy as jnp
        import numpy as np
        C_Z, H_Z, W_Z, NH, C = (128, 256, 256, 4, 64)
        EPS = 1e-05
        B = pair_rep.shape[0]
        mu = jnp.mean(pair_rep, axis=(1, 2, 3), keepdims=True)
        var = jnp.var(pair_rep, axis=(1, 2, 3), keepdims=True)
        x = (pair_rep - mu) * jax.lax.rsqrt(var + EPS) * ln_w + ln_b

        def proj(w):
            y = jnp.einsum('oc,bcij->boij', w, x)
            return y.reshape(B, NH, C, H_Z, W_Z)
        q = proj(wq)
        k = proj(wk)
        v = proj(wv)
        g = jax.nn.sigmoid(proj(wg_w) + wg_b.reshape(1, NH, C, 1, 1))
        bias = jnp.einsum('hc,bcij->bhij', wb, x)
        scale = 1.0 / jnp.sqrt(jnp.float32(C))
        scores = jnp.einsum('bhcij,bhcik->bhijk', q, k) * scale + bias[:, :, None, :, :]
        a = jax.nn.softmax(scores, axis=-1)
        o = g * jnp.einsum('bhijk,bhcik->bhcij', a, v)
        o = o.transpose(0, 2, 1, 3, 4).reshape(B, C * NH, H_Z, W_Z)
        return jnp.einsum('oc,bcij->boij', wrep_w, o) + wrep_b.reshape(1, C_Z, 1, 1)

    def _L1_conv_ref(msa_repr, pair_repr, gate_proj, qkv_proj, out_proj, bias_proj):
        import jax, jax.numpy as jnp
        import numpy as np
        HEAD = 8
        C = 32
        SCALE = 1.0 / C ** 0.5
        bs, s, r, cm = msa_repr.shape
        head, c, scale = (HEAD, C, SCALE)
        bias = jnp.einsum('nijz,zh->nhij', pair_repr, bias_proj)[:, None]
        gate = jax.nn.sigmoid(msa_repr @ gate_proj).reshape(bs, s, r, head, c)
        q, k, v = jnp.split(msa_repr @ qkv_proj, 3, axis=-1)
        q = q.reshape(bs, s, r, head, c)
        k = k.reshape(bs, s, r, head, c)
        v = v.reshape(bs, s, r, head, c)
        sim = jnp.einsum('nsqhc,nskhc->nshqk', q, k) * scale
        sim = jax.nn.softmax(sim, axis=-1)
        sim = sim + bias
        attend = jnp.einsum('nshqk,nskhc->nsqhc', sim, v) * gate
        out = attend.reshape(bs, s, r, cm) @ out_proj
        return out

    def _gn(v, G=32, eps=1e-5):
        B_, H_, W_, C_ = v.shape
        g = v.reshape(B_, H_, W_, G, C_ // G)
        m = jnp.mean(g, axis=(1, 2, 4), keepdims=True)
        s = jnp.var(g, axis=(1, 2, 4), keepdims=True)
        return ((g - m) / jnp.sqrt(s + eps)).reshape(v.shape)

    def _ln_c(v, eps=1e-6):
        m = jnp.mean(v, axis=-1, keepdims=True)
        s = jnp.var(v, axis=-1, keepdims=True)
        return (v - m) / jnp.sqrt(s + eps)

    def _ln_t(v, eps=1e-5):
        m = jnp.mean(v, axis=-1, keepdims=True)
        s = jnp.var(v, axis=-1, keepdims=True)
        return (v - m) / jnp.sqrt(s + eps)

    def _to_tokens(v):
        B_, H_, W_, C_ = v.shape
        return v.reshape(B_, H_ * W_, C_)
    def _from_tokens(t, like):
        return t.reshape(like.shape)

    x = x + _L0_conv_ref(_gn(x), L0_conv_ln_w, L0_conv_ln_b, L0_conv_wq, L0_conv_wk, L0_conv_wv, L0_conv_wb, L0_conv_wg_w, L0_conv_wg_b, L0_conv_wrep_w, L0_conv_wrep_b)
    x = x + _L1_conv_ref(_gn(x), L1_conv_pair_repr, L1_conv_gate_proj, L1_conv_qkv_proj, L1_conv_out_proj, L1_conv_bias_proj)
    return x


_drawn_inputs = setup_inputs


def setup_inputs(seed=0):
    import zlib

    import numpy as np

    out = dict(_drawn_inputs(seed))
    spreads = {'L0_conv_ln_w': (1.0, 0.6),
     'L0_conv_ln_b': (0.0, 0.8),
     'L0_conv_wg_b': (0.0, 0.8),
     'L0_conv_wrep_b': (0.0, 0.357)}
    factors = {'L0_conv_wq': 8.0,
     'L0_conv_wk': 8.0,
     'L0_conv_wv': 8.0,
     'L0_conv_wb': 8.0,
     'L0_conv_wg_w': 8.0,
     'L0_conv_wrep_w': 8.0}
    for name, (base, spread) in spreads.items():
        noise = np.random.default_rng([zlib.crc32(name.encode()), seed]).standard_normal(out[name].shape)
        drawn = base * np.exp(spread * noise) if base else spread * noise
        out[name] = jnp.asarray(drawn.astype(out[name].dtype))
    for name, factor in factors.items():
        out[name] = (out[name] * factor).astype(out[name].dtype)
    return out
```

```python
import concourse.bass as bass
from concourse import mybir
from contextlib import ExitStack

F32 = mybir.dt.float32
ALU = mybir.AluOpType
ACT = mybir.ActivationFunctionType
AX = mybir.AxisListType

P = 128
C0 = 128
W = 256
KC = W // P
GROUP = 8
NG = W // GROUP
NH0, D0 = 4, 64
NH1, D1 = 8, 32
EPS = 1e-5
HC = 2


def wait(engine, sem, value):
    if not (isinstance(value, int) and value <= 0):
        engine.wait_ge(sem, value)


def loop_first_peeled(engine, count, body):
    body(0)
    with engine.Fori(1, count) as t:
        body(t)


def loop_ends_peeled(engine, count, body):
    body(0, True, False)
    with engine.Fori(1, count - 1) as t:
        body(t, False, False)
    body(count - 1, False, True)


class Chain:

    def __init__(self, engine, sem):
        self.engine, self.sem, self.count = engine, sem, 0

    def __call__(self, instruction):
        self.count += 1
        instruction.then_inc(self.sem, 1)
        self.engine.wait_ge(self.sem, self.count)


def prepare_weights(nc, m, a):
    with ExitStack() as ctx:
        sem = lambda name: ctx.enter_context(nc.semaphore(name))
        sb = lambda name, shape: ctx.enter_context(nc.sbuf_tensor(name, shape, F32))
        wq = sb("wq_raw", [D0, NH0, C0])
        wk = sb("wk_raw", [D0, NH0, C0])
        wv = sb("wv_raw", [P, HC, C0])
        wg = sb("wg_raw", [P, HC, C0])
        wrep = sb("wrep_raw", [C0, D0, NH0])
        wrep_h = sb("wrep_by_head", [C0, NH0, D0])
        wb = sb("wb_raw", [32, C0])
        wgb = sb("wgb_raw", [P, HC])
        loaded, zeroed, ident_step, ident_ready = sem("w_loaded"), sem("w_zeroed"), sem("ident_step"), sem("ident_ready")
        permuted, folded, turned, evacuated, done = sem("w_permuted"), sem("w_folded"), sem("w_turned"), sem("w_evacuated"), sem("w_done")
        wb_loaded = sem("wb_loaded")
        LOADS = 11
        block = ctx.enter_context(nc.Block())

        @block.sync
        def _(sp):
            sp.dma_start(wq[:], a["wq"].rearrange("(h d) c -> d h c", h=NH0)).then_inc(loaded, 16)
            sp.dma_start(wk[:], a["wk"].rearrange("(h d) c -> d h c", h=NH0)).then_inc(loaded, 16)
            sp.dma_start(wv[:], a["wv"].rearrange("(a p) c -> p a c", p=P)).then_inc(loaded, 16)
            sp.dma_start(wg[:], a["wg_w"].rearrange("(a p) c -> p a c", p=P)).then_inc(loaded, 16)
            sp.dma_start(wrep[:], a["wrep_w"].rearrange("o (c h) -> o c h", h=NH0)).then_inc(loaded, 16)
            for c in range(HC):
                sp.dma_start(wgb[:, c:c + 1], a["wg_b"][c * P:(c + 1) * P].rearrange("(p a) -> p a", a=1)).then_inc(loaded, 16)
            sp.dma_start(m.wrep_b[:], a["wrep_b"].rearrange("(p a) -> p a", a=1)).then_inc(loaded, 16)
            sp.dma_start(m.w_gate1[:], a["gate_proj"].rearrange("(a p) n -> p a n", p=P)).then_inc(loaded, 16)
            sp.dma_start(m.w_qkv1[:], a["qkv_proj"].rearrange("(a p) n -> p a n", p=P)).then_inc(loaded, 16)
            sp.dma_start(m.w_out1[:], a["out_proj"].rearrange("(a p) n -> p a n", p=P)).then_inc(loaded, 16)
            sp.wait_ge(zeroed, 1)
            sp.dma_start(wb[0:NH0, :], a["wb"]).then_inc(wb_loaded, 16)
            sp.dma_start(m.w_pair[:, 0:NH1], a["bias_proj"]).then_inc(wb_loaded, 16)
            sp.wait_ge(loaded, 16 * LOADS)
            sp.wait_ge(wb_loaded, 32)

        @block.gpsimd
        def _(pool):
            nc.gpsimd.memset(m.ident[:], 0.0).then_inc(ident_step, 1)
            pool.wait_ge(ident_step, 1)
            nc.gpsimd.affine_select(out=m.ident[:], in_=m.ident[:], compare_op=ALU.not_equal, fill=1.0, base=0,
                                    pattern=[[-1, P]], channel_multiplier=1).then_inc(ident_ready, 1)
            nc.gpsimd.memset(m.q1[:], 0.0).then_inc(done, 1)

        @block.vector
        def _(dve):
            nc.vector.memset(wb[:], 0.0)
            nc.vector.memset(m.w_pair[:], 0.0).then_inc(zeroed, 1)
            nc.vector.memset(m.averager[:], 1.0 / P)
            dve.wait_ge(loaded, 16 * LOADS)
            nc.vector.tensor_copy(wrep_h[:], wrep[:].rearrange("o c h -> o h c")).then_inc(permuted, 1)
            nc.vector.tensor_scalar(m.wg_b_half[:], wgb[:], 0.5, None, ALU.mult)
            nc.vector.tensor_scalar(m.w_out1[:], m.w_out1[:], 0.5, None, ALU.mult).then_inc(done, 1)
            dve.wait_ge(folded, 1)
            nc.vector.tensor_scalar(m.wqk[:], m.psum[0][:].rearrange("p (h c) -> p h c", h=NH0), D0 ** -0.5, None, ALU.mult).then_inc(done, 1)
            dve.wait_ge(turned, 1)
            nc.vector.tensor_copy(m.wv_t[:], m.psum[1][:, 0:256])
            nc.vector.tensor_copy(m.wg_t[:], m.psum[1][:, 256:512])
            nc.vector.tensor_scalar(m.wrep_t[:], m.psum[2][:, 0:256].rearrange("p (a o) -> p a o", a=HC), 0.5, None, ALU.mult)
            nc.vector.tensor_copy(m.wb_t[:], m.psum[2][:, 256:288]).then_inc(done, 1)
            dve.wait_ge(done, 4)

        @block.tensor
        def _(pe):
            pe.wait_ge(loaded, 16 * LOADS)
            for h in range(NH0):
                last = nc.tensor.matmul(m.psum[0][:, h * C0:(h + 1) * C0], wq[:, h, :], wk[:, h, :], start=True, stop=True)
            last.then_inc(folded, 1)
            pe.wait_ge(ident_ready, 1)
            pe.wait_ge(permuted, 1)
            pe.wait_ge(wb_loaded, 32)
            for c in range(HC):
                nc.tensor.transpose(m.psum[1][:, c * P:(c + 1) * P], wv[:, c, :], m.ident[:])
                nc.tensor.transpose(m.psum[1][:, 256 + c * P:256 + (c + 1) * P], wg[:, c, :], m.ident[:])
                nc.tensor.transpose(m.psum[2][:, c * P:(c + 1) * P],
                                    wrep_h[:, 2 * c:2 * c + 2, :].rearrange("o h d -> o (h d)"), m.ident[:])
            nc.tensor.transpose(m.psum[2][:, 256:288], wb[:], m.ident[0:32, 0:32]).then_inc(turned, 1)


def group_statistics(nc, m, tag, source, with_layer_norm):
    ROWS, TILES = 32, W // 32
    with ExitStack() as ctx:
        sem = lambda name: ctx.enter_context(nc.semaphore(f"{tag}_{name}"))
        sb = lambda name, shape: ctx.enter_context(nc.sbuf_tensor(f"{tag}_{name}", shape, F32))
        tiles = [m.stage[:, i * ROWS * W:(i + 1) * ROWS * W].rearrange("p (r c) -> p r c", c=W) for i in range(2)]
        stats = sb("stats", [P, NG, TILES, 6])
        own = sb("own", [P, NG, 2])
        mean_var = sb("mean_var", [P, NG, 2])
        dev = sb("dev", [P, NG])
        var = sb("var", [P, NG])
        ve = sb("ve", [P, NG + 1])
        root = sb("root", [P, NG + 1])
        tmp = sb("tmp", [P, NG + 1])
        inv = sb("inv", [P, NG + 1])
        tile_loaded = [sem("tile_loaded0"), sem("tile_loaded1")]
        tile_read, step, own_ready, mean_mm, dev_ready, dev_mm = sem("tile_read"), sem("step"), sem("own_ready"), sem("mean_mm"), sem("dev_ready"), sem("dev_mm")
        ve_ready, root_ready = sem("ve_ready"), sem("root_ready")
        block = ctx.enter_context(nc.Block())

        @block.sync
        def _(sp):
            def body(t):
                for i in range(2):
                    wait(sp, tile_read, 2 * t + i - 1)
                    sp.dma_start(tiles[i], source[:, bass.ds(ROWS * (2 * t + i), ROWS), :]).then_inc(tile_loaded[i], 16)
            loop_first_peeled(sp, TILES // 2, body)

        @block.vector
        def _(dve):
            for tile in range(TILES):
                i = tile % 2
                dve.wait_ge(tile_loaded[i], 16 * (tile // 2 + 1))
                for g in range(NG):
                    last = nc.vector.bn_stats(stats[:, g, tile, :], tiles[i][:, :, g * GROUP:(g + 1) * GROUP])
                last.then_inc(tile_read, 1)
            dve.wait_ge(tile_read, TILES)
            for g in range(NG):
                last = nc.vector.bn_aggr(own[:, g, :], stats[:, g, :, :])
            last.then_inc(own_ready, 1)
            chain = Chain(dve, step)
            dve.wait_ge(own_ready, 1)
            dve.wait_ge(mean_mm, 1)
            chain(nc.vector.tensor_copy(mean_var[:], m.psum[0][:, 0:2 * NG].rearrange("p (g s) -> p g s", s=2)))
            chain(nc.vector.tensor_tensor(dev[:], own[:, :, 0], mean_var[:, :, 0], ALU.subtract))
            nc.vector.tensor_tensor(dev[:], dev[:], dev[:], ALU.mult).then_inc(dev_ready, 1)
            dve.wait_ge(dev_mm, 1)
            chain(nc.vector.tensor_tensor(var[:], m.psum[1][:, 0:NG], mean_var[:, :, 1], ALU.add))
            nc.vector.tensor_copy(m.mean[:].rearrange("p (g e) -> p g e", e=GROUP),
                                  mean_var[:, :, 0:1].broadcast_to([P, NG, GROUP]))

            def inverse_root(cols, n):
                dve.wait_ge(root_ready, n)
                chain(nc.vector.reciprocal(inv[:, cols], root[:, cols]))
                chain(nc.vector.tensor_tensor(tmp[:, cols], ve[:, cols], inv[:, cols], ALU.mult))
                chain(nc.vector.tensor_tensor(root[:, cols], root[:, cols], tmp[:, cols], ALU.add))
                chain(nc.vector.reciprocal(tmp[:, cols], root[:, cols]))
                chain(nc.vector.tensor_scalar(inv[:, cols], tmp[:, cols], 2.0, None, ALU.mult))

            nc.vector.tensor_scalar(ve[:, 0:NG], var[:], EPS, None, ALU.add).then_inc(ve_ready, 1)
            inverse_root(slice(0, NG), 1)
            if with_layer_norm:
                chain(nc.vector.tensor_tensor(dev[:], var[:], inv[:, 0:NG], ALU.mult))
                chain(nc.vector.tensor_tensor(var[:], dev[:], inv[:, 0:NG], ALU.mult))
                chain(nc.vector.reduce_sum(tmp[:, NG:NG + 1], var[:], AX.X))
                nc.vector.tensor_scalar(ve[:, NG:NG + 1], tmp[:, NG:NG + 1], 1.0 / NG, EPS, ALU.mult, ALU.add).then_inc(ve_ready, 1)
                inverse_root(slice(NG, NG + 1), 2)
                chain(nc.vector.tensor_scalar(tmp[:, 0:NG], inv[:, 0:NG], inv[:, NG:NG + 1], None, ALU.mult))
                chain(nc.vector.tensor_copy(inv[:, 0:NG], tmp[:, 0:NG]))
            chain(nc.vector.tensor_copy(m.rstd[:].rearrange("p (g e) -> p g e", e=GROUP),
                                        inv[:, 0:NG].rearrange("p (g o) -> p g o", o=1).broadcast_to([P, NG, GROUP])))

        @block.scalar
        def _(act):
            act.wait_ge(ve_ready, 1)
            nc.scalar.activation(root[:, 0:NG], ve[:, 0:NG], ACT.Sqrt).then_inc(root_ready, 1)
            if with_layer_norm:
                act.wait_ge(ve_ready, 2)
                nc.scalar.activation(root[:, NG:NG + 1], ve[:, NG:NG + 1], ACT.Sqrt).then_inc(root_ready, 1)

        @block.tensor
        def _(pe):
            pe.wait_ge(own_ready, 1)
            nc.tensor.matmul(m.psum[0][:, 0:2 * NG], m.averager[:], own[:].rearrange("p g s -> p (g s)"), start=True, stop=True).then_inc(mean_mm, 1)
            pe.wait_ge(dev_ready, 1)
            nc.tensor.matmul(m.psum[1][:, 0:NG], m.averager[:], dev[:], start=True, stop=True).then_inc(dev_mm, 1)


ROWS_B = 16
TILES_B = W // ROWS_B


def store_head_rows(sp, tile, evac, scratch, heads, stored):
    for c in range(4):
        sp.dma_start(scratch[:, bass.ds(ROWS_B * tile + 4 * c, 4), :],
                     evac[32 * c:32 * c + heads, :].rearrange("p (r k) -> p r k", k=W)).then_inc(stored, 16)


def project_heads(nc, m, banks, weights, rows):
    for g in range(8):
        c = g // 2
        last = nc.tensor.matmul(banks[g % 2][32 * c:32 * c + 32, :], weights, rows[:, 2 * g:2 * g + 2, :].rearrange("p r c -> p (r c)"),
                                start=True, stop=True, tile_position=(0, 32 * c))
    return last


def project_image_bias(nc, m, x, ln_w, ln_b, scratch):
    with ExitStack() as ctx:
        sem = lambda name: ctx.enter_context(nc.semaphore(f"ib_{name}"))
        size = ROWS_B * W
        view = lambda i: m.stage[:, i * size:(i + 1) * size].rearrange("p (r c) -> p r c", c=W)
        xt, wt, bt = [view(0), view(1)], [view(2), view(3)], [view(4), view(5)]
        evac = [ctx.enter_context(nc.sbuf_tensor(f"ib_evac{i}", [P, 4 * W], F32)) for i in range(2)]
        loaded, stored = [sem("loaded0"), sem("loaded1")], [sem("stored0"), sem("stored1")]
        centred, scaled, weighted, ready, projected, evacuated = (sem(n) for n in ("centred", "scaled", "weighted", "ready", "projected", "evacuated"))
        mean = m.mean[:].rearrange("p (o c) -> p o c", o=1).broadcast_to([P, ROWS_B, W])
        rstd = m.rstd[:].rearrange("p (o c) -> p o c", o=1).broadcast_to([P, ROWS_B, W])
        block = ctx.enter_context(nc.Block())

        @block.sync
        def _(sp):
            def load(tile, i):
                rows = bass.ds(ROWS_B * tile, ROWS_B)
                wait(sp, projected, tile - 1)
                sp.dma_start(xt[i], x[:, rows, :]).then_inc(loaded[i], 16)
                sp.dma_start(wt[i], ln_w[:, rows, :]).then_inc(loaded[i], 16)
                sp.dma_start(bt[i], ln_b[:, rows, :]).then_inc(loaded[i], 16)

            def store(tile, i):
                sp.wait_ge(evacuated, tile + 1)
                store_head_rows(sp, tile, evac[i], scratch, NH0, stored[i])

            load(0, 0)
            load(1, 1)

            def body(t, first, last):
                for i in range(2):
                    store(2 * t + i, i)
                    if not last:
                        load(2 * t + i + 2, i)
            loop_ends_peeled(sp, TILES_B // 2, body)
            for i in range(2):
                sp.wait_ge(stored[i], 16 * 4 * TILES_B // 2)
            for h in range(NH0):
                sp.dma_start(m.bias0[:, :, h, :], scratch[h].rearrange("(a p) k -> p a k", p=P)).then_inc(loaded[0], 16)
            sp.wait_ge(loaded[0], 16 * (3 * TILES_B // 2 + NH0))

        @block.vector
        def _(dve):
            def body(t):
                for i in range(2):
                    tile = 2 * t + i
                    dve.wait_ge(loaded[i], 48 * (t + 1))
                    nc.vector.tensor_tensor(xt[i], xt[i], mean, ALU.subtract).then_inc(centred, 1)
                    dve.wait_ge(centred, tile + 1)
                    nc.vector.tensor_tensor(xt[i], xt[i], rstd, ALU.mult).then_inc(scaled, 1)
                    dve.wait_ge(weighted, tile + 1)
                    nc.vector.tensor_tensor(xt[i], xt[i], bt[i], ALU.add).then_inc(ready, 1)
            loop_first_peeled(dve, TILES_B // 2, body)

        @block.gpsimd
        def _(pool):
            def body(t):
                for i in range(2):
                    pool.wait_ge(scaled, 2 * t + i + 1)
                    nc.gpsimd.tensor_tensor(xt[i], xt[i], wt[i], ALU.mult).then_inc(weighted, 1)
            loop_first_peeled(pool, TILES_B // 2, body)

        @block.tensor
        def _(pe):
            def body(t):
                for i in range(2):
                    tile = 2 * t + i
                    pe.wait_ge(ready, tile + 1)
                    wait(pe, evacuated, tile - 1)
                    project_heads(nc, m, m.psum[2 * i:2 * i + 2], m.wb_t[:], xt[i]).then_inc(projected, 1)
            loop_first_peeled(pe, TILES_B // 2, body)

        @block.scalar
        def _(act):
            def body(t):
                for i in range(2):
                    tile = 2 * t + i
                    act.wait_ge(projected, tile + 1)
                    wait(act, stored[i], 64 * t)
                    view = evac[i][:].rearrange("p (b n) -> p b n", b=2)
                    nc.scalar.activation(view[:, 0, :], m.psum[2 * i][:], ACT.Copy)
                    nc.scalar.activation(view[:, 1, :], m.psum[2 * i + 1][:], ACT.Copy).then_inc(evacuated, 1)
            loop_first_peeled(act, TILES_B // 2, body)


def project_pair_bias(nc, m, pair, scratch):
    with ExitStack() as ctx:
        sem = lambda name: ctx.enter_context(nc.semaphore(f"pb_{name}"))
        size = ROWS_B * W
        raw = [m.stage[:, i * size:(i + 1) * size].rearrange("p (r e z) -> p r e z", e=2, z=P) for i in range(2)]
        turned = [m.stage[:, (2 + i) * size:(3 + i) * size].rearrange("p (r k) -> p r k", k=W) for i in range(2)]
        evac = [ctx.enter_context(nc.sbuf_tensor(f"pb_evac{i}", [P, 4 * W], F32)) for i in range(2)]
        loaded, stored = [sem("loaded0"), sem("loaded1")], [sem("stored0"), sem("stored1")]
        transposed, copied_act, copied_dve, projected, evacuated = (sem(n) for n in ("transposed", "copied_act", "copied_dve", "projected", "evacuated"))
        bank = lambda j: m.psum[4 + j % 4]
        block = ctx.enter_context(nc.Block())
        BANKS = ROWS_B // 2

        @block.sync
        def _(sp):
            def load(tile, i):
                wait(sp, transposed, BANKS * (tile - 1))
                sp.dma_start(raw[i], pair[bass.ds(ROWS_B * tile, ROWS_B)].rearrange("q (p e) z -> p q e z", e=2)).then_inc(loaded[i], 16)

            def store(tile, i):
                sp.wait_ge(evacuated, tile + 1)
                store_head_rows(sp, tile, evac[i], scratch, NH1, stored[i])

            load(0, 0)
            load(1, 1)

            def body(t, first, last):
                for i in range(2):
                    store(2 * t + i, i)
                    if not last:
                        load(2 * t + i + 2, i)
            loop_ends_peeled(sp, TILES_B // 2, body)
            for i in range(2):
                sp.wait_ge(stored[i], 16 * 4 * TILES_B // 2)
            for h in range(NH1):
                sp.dma_start(m.bias1[:, :, h, :], scratch[h].rearrange("(a p) k -> p a k", p=P)).then_inc(loaded[0], 16)
            sp.wait_ge(loaded[0], 16 * (TILES_B // 2 + NH1))

        @block.tensor
        def _(pe):
            def project(tile, i):
                pe.wait_ge(copied_act, BANKS // 2 * (tile + 1))
                pe.wait_ge(copied_dve, BANKS // 2 * (tile + 1))
                wait(pe, evacuated, tile - 1)
                project_heads(nc, m, m.psum[2 * i:2 * i + 2], m.w_pair[:], turned[i]).then_inc(projected, 1)

            def body(t, first, last):
                for i in range(2):
                    tile = 2 * t + i
                    pe.wait_ge(loaded[i], 16 * (t + 1))
                    for j in range(BANKS):
                        wait(pe, copied_act if j % 2 == 0 else copied_dve, BANKS // 2 * tile + j // 2 - 1)
                        for r in range(2):
                            for e in range(2):
                                lastt = nc.tensor.transpose(bank(j)[:, (2 * r + e) * P:(2 * r + e + 1) * P], raw[i][:, 2 * j + r, e, :], m.ident[:])
                        lastt.then_inc(transposed, 1)
                    if not (first and i == 0):
                        project(tile - 1, 1 - i)
            loop_ends_peeled(pe, TILES_B // 2, body)
            project(TILES_B - 1, 1)

        def copies(engine, copy, own, parity):
            def body(t):
                for i in range(2):
                    tile = 2 * t + i
                    wait(engine, projected, tile - 1)
                    for j in range(parity, BANKS, 2):
                        engine.wait_ge(transposed, BANKS * tile + j + 1)
                        copy(turned[i][:, 2 * j:2 * j + 2, :].rearrange("p r (k e) -> p r e k", e=2),
                             bank(j)[:].rearrange("p (r e k) -> p r e k", r=2, e=2)).then_inc(own, 1)
                    if parity == 0:
                        evacuate(tile - 1, 1 - i, t - (1 - i))
            return body

        def evacuate(tile, i, uses):
            if isinstance(tile, int) and tile < 0:
                return
            nc.scalar.wait_ge(projected, tile + 1)
            wait(nc.scalar, stored[i], 64 * uses)
            view = evac[i][:].rearrange("p (b n) -> p b n", b=2)
            nc.scalar.activation(view[:, 0, :], m.psum[2 * i][:], ACT.Copy)
            nc.scalar.activation(view[:, 1, :], m.psum[2 * i + 1][:], ACT.Copy).then_inc(evacuated, 1)

        @block.scalar
        def _(act):
            body = copies(act, lambda out, in_: nc.scalar.activation(out, in_, ACT.Copy), copied_act, 0)
            loop_first_peeled(act, TILES_B // 2, body)
            evacuate(TILES_B - 1, 1, TILES_B // 2 - 1)

        @block.vector
        def _(dve):
            loop_first_peeled(dve, TILES_B // 2, copies(dve, nc.vector.tensor_copy, copied_dve, 1))


def layer0(nc, m, x, ln_w, ln_b, x1):
    UNROLL, TILE = 8, 2
    BUFS = UNROLL // TILE
    with ExitStack() as ctx:
        sem = lambda name: ctx.enter_context(nc.semaphore(f"l0_{name}"))
        sb = lambda name, shape: ctx.enter_context(nc.sbuf_tensor(f"l0_{name}", shape, F32))
        xt = sb("x", [P, BUFS, TILE, W])
        wt = sb("ln_w", [P, BUFS, TILE, W])
        bt = sb("ln_b", [P, BUFS, TILE, W])
        xn = sb("xn", [P, 4, W])
        qk = sb("qk", [P, 2, NH0, W])
        probs = sb("probs", [P, NH0, KC, W])
        probs_t = sb("probs_t", [P, NH0, KC, W])
        v = sb("v", [P, 2, KC, HC * P])
        gate = sb("gate", [P, 2, HC, W])
        o = sb("o", [P, 2, HC, W])
        y = sb("y", [P, 2, TILE, W])
        neg_max = sb("neg_max", [P, NH0, KC])
        total = sb("total", [P, NH0, KC])
        inv = sb("inv", [P, NH0, KC])
        b_qa, b_qb = m.psum[0], m.psum[1]
        b_s, b_t, b_av, b_out = m.psum[2:4], m.psum[4:6], m.psum[6], m.psum[7]
        loaded = [sem(f"loaded{i}") for i in range(BUFS)]
        y_stored = [sem(f"y_stored{i}") for i in range(2)]
        (xn_step, xn_ready, qa_mm, qb_mm, v_mm, g_mm, qa_ready, qb_ready, v_ready, g_ready, s_mm, s_ready, exp_ready, inv_ready,
         p_ready, t_mm, t_act, t_dve, av_mm, o_ready, out_mm, y_ready) = (sem(n) for n in (
            "xn_step", "xn_ready", "qa_mm", "qb_mm", "v_mm", "g_mm", "qa_ready", "qb_ready", "v_ready", "g_ready", "s_mm", "s_ready",
            "exp_ready", "inv_ready", "p_ready", "t_mm", "t_act", "t_dve", "av_mm", "o_ready", "out_mm", "y_ready"))
        block = ctx.enter_context(nc.Block())

        def rows(engine, row):
            def body(t, first, last):
                for k in range(UNROLL):
                    row(UNROLL * t + k, k, first and k == 0, last and k == UNROLL - 1)
            loop_ends_peeled(engine, W // UNROLL, body)

        @block.sync
        def _(sp):
            def load(tile, i):
                at = bass.ds(TILE * tile, TILE)
                sp.dma_start(xt[:, i], x[:, at, :]).then_inc(loaded[i], 16)
                sp.dma_start(wt[:, i], ln_w[:, at, :]).then_inc(loaded[i], 16)
                sp.dma_start(bt[:, i], ln_b[:, at, :]).then_inc(loaded[i], 16)

            for i in range(BUFS):
                load(i, i)

            def body(t, first, last):
                for i in range(BUFS):
                    tile = BUFS * t + i
                    sp.wait_ge(y_ready, TILE * (tile + 1))
                    sp.dma_start(x1[:, bass.ds(TILE * tile, TILE), :], y[:, i % 2]).then_inc(y_stored[i % 2], 16)
                    if not last:
                        load(tile + BUFS, i)
            loop_ends_peeled(sp, W // UNROLL, body)
            for i in range(2):
                sp.wait_ge(y_stored[i], 16 * W // TILE // 2)

        @block.gpsimd
        def _(pool):
            def divide(n, h):
                pool.wait_ge(inv_ready, n + 1)
                pool.nop(nofuse=True)
                for c in range(KC):
                    last = nc.gpsimd.tensor_scalar(probs[:, h, c], probs[:, h, c], inv[:, h, c:c + 1], 1.0, ALU.mult, ALU.mult)
                last.then_inc(p_ready, 1)

            def normalise_ahead(t, k, part):
                r, kk, tt = UNROLL * t + k, k % UNROLL, t + k // UNROLL
                i, j, out = kk // TILE, kk % TILE, xn[:, kk % 4]
                if part == 0:
                    if j == 0:
                        pool.wait_ge(loaded[i], 48 * (tt + 1))
                    wait(pool, s_mm, NH0 * (r - 3))
                    nc.gpsimd.tensor_tensor(out, xt[:, i, j], m.mean[:], ALU.subtract).then_inc(xn_step, 1)
                    return
                pool.wait_ge(xn_step, 3 * r + part)
                if part == 1:
                    nc.gpsimd.tensor_tensor(out, out, m.rstd[:], ALU.mult).then_inc(xn_step, 1)
                elif part == 2:
                    nc.gpsimd.tensor_tensor(out, out, wt[:, i, j], ALU.mult).then_inc(xn_step, 1)
                else:
                    nc.gpsimd.tensor_tensor(out, out, bt[:, i, j], ALU.add).then_inc(xn_ready, 1)

            for r in range(2):
                for part in range(4):
                    normalise_ahead(0, r, part)
            divide(0, 0)
            divide(1, 1)

            def body(t, first, last):
                for k in range(UNROLL):
                    for h in range(NH0):
                        n = NH0 * (UNROLL * t + k) + h
                        if not (last and k == UNROLL - 1 and h >= 2):
                            divide(n + 2, (h + 2) % NH0)
                        if not (last and k >= UNROLL - 2):
                            normalise_ahead(t, k + 2, h)
            loop_ends_peeled(pool, W // UNROLL, body)

        @block.tensor
        def _(pe):
            def queries(r, k, half):
                bank, done, free = ((b_qa, qa_mm, v_ready), (b_qb, qb_mm, g_ready))[half]
                pe.wait_ge(xn_ready, r + 1)
                wait(pe, free, r)
                for j in range(2):
                    last = nc.tensor.matmul(bank[:, j * W:(j + 1) * W], m.wqk[:, 2 * half + j, :], xn[:, k % 4], start=True, stop=True)
                last.then_inc(done, 1)

            def values(r, k):
                pe.wait_ge(qa_ready, r + 1)
                for c in range(KC):
                    last = nc.tensor.matmul(b_qa[:, c * W:(c + 1) * W], xn[:, k % 4, c * P:(c + 1) * P], m.wv_t[:], start=True, stop=True)
                last.then_inc(v_mm, 1)

            def gates(r, k):
                pe.wait_ge(qb_ready, r + 1)
                for c in range(HC):
                    last = nc.tensor.matmul(b_qb[:, c * W:(c + 1) * W], m.wg_t[:, c * P:(c + 1) * P], xn[:, k % 4], start=True, stop=True)
                last.then_inc(g_mm, 1)

            def scores(r, k, h):
                n = NH0 * r + h
                pe.wait_ge(qa_ready if h < 2 else qb_ready, r + 1)
                wait(pe, s_ready, n - 1)
                for c in range(KC):
                    last = nc.tensor.matmul(b_s[h % 2][:, c * W:(c + 1) * W], qk[:, k % 2, h, c * P:(c + 1) * P], xn[:, k % 4], start=True, stop=True)
                last.then_inc(s_mm, 1)

            def transposes(r, h):
                n = NH0 * r + h
                pe.wait_ge(p_ready, n + 1)
                wait(pe, (t_act, t_dve)[h % 2], 2 * r + h // 2)
                for kc in range(KC):
                    for qc in range(KC):
                        last = nc.tensor.transpose(b_t[h % 2][:, kc * W + qc * P:kc * W + (qc + 1) * P], probs[:, h, qc, kc * P:(kc + 1) * P], m.ident[:])
                last.then_inc(t_mm, 1)

            def attend(r, k, pair):
                pe.wait_ge(t_act, 2 * r + pair + 1)
                pe.wait_ge(t_dve, 2 * r + pair + 1)
                pe.wait_ge(v_ready, r + 1)
                wait(pe, o_ready, r)
                for kc in range(KC):
                    for j in range(2):
                        h = 2 * pair + j
                        last = nc.tensor.matmul(b_av[D0 * j:D0 * (j + 1), pair * W:(pair + 1) * W], v[:, k % 2, kc, h * D0:(h + 1) * D0],
                                                probs_t[:, h, kc], start=kc == 0, stop=kc == KC - 1)
                last.then_inc(av_mm, 1)

            def project_out(r, k):
                pe.wait_ge(o_ready, r + 1)
                wait(pe, y_ready, r)
                for c in range(HC):
                    last = nc.tensor.matmul(b_out[:, 0:W], m.wrep_t[:, c, :], o[:, k % 2, c], start=c == 0, stop=c == HC - 1)
                last.then_inc(out_mm, 1)

            queries(0, 0, 0)
            queries(0, 0, 1)
            values(0, 0)
            gates(0, 0)
            scores(0, 0, 0)
            scores(0, 0, 1)

            def row(r, k, first, last):
                scores(r, k, 2)
                transposes(r, 0)
                if not first:
                    attend(r - 1, k + 1, 1)
                if not last:
                    queries(r + 1, k + 1, 0)
                scores(r, k, 3)
                transposes(r, 1)
                if not last:
                    queries(r + 1, k + 1, 1)
                if not first:
                    project_out(r - 1, k + 1)
                if not last:
                    scores(r + 1, k + 1, 0)
                transposes(r, 2)
                attend(r, k, 0)
                if not last:
                    values(r + 1, k + 1)
                    scores(r + 1, k + 1, 1)
                transposes(r, 3)
                if not last:
                    gates(r + 1, k + 1)
            rows(pe, row)
            attend(W - 1, W - 1, 1)
            project_out(W - 1, W - 1)

        @block.scalar
        def _(act):
            def exponents(n, h):
                act.wait_ge(s_ready, n + 1)
                for c in range(KC):
                    last = nc.scalar.activation(probs[:, h, c], probs[:, h, c], ACT.Exp, bias=neg_max[:, h, c:c + 1], scale=-1.0,
                                                accum_out=total[:, h, c:c + 1])
                last.then_inc(exp_ready, 1)

            def queries_out(r, k):
                act.wait_ge(qa_mm, r + 1)
                nc.scalar.activation(qk[:, k % 2, 0:2], b_qa[:].rearrange("p (h c) -> p h c", h=2), ACT.Copy).then_inc(qa_ready, 1)

            def values_out(r, k):
                act.wait_ge(v_mm, r + 1)
                nc.scalar.activation(v[:, k % 2], b_qa[:].rearrange("p (h c) -> p h c", h=2), ACT.Copy).then_inc(v_ready, 1)

            def gates_out(r, k):
                act.wait_ge(g_mm, r + 1)
                for c in range(HC):
                    last = nc.scalar.activation(gate[:, k % 2, c], b_qb[:, c * W:(c + 1) * W], ACT.Tanh, bias=m.wg_b_half[:, c:c + 1], scale=0.5)
                last.then_inc(g_ready, 1)

            def transposed_out(n, h):
                act.wait_ge(t_mm, n + 1)
                nc.scalar.activation(probs_t[:, h], b_t[0][:].rearrange("p (a c) -> p a c", a=KC), ACT.Copy).then_inc(t_act, 1)

            queries_out(0, 0)
            values_out(0, 0)
            gates_out(0, 0)
            exponents(0, 0)
            exponents(1, 1)

            def row(r, k, first, last):
                n = NH0 * r
                transposed_out(n, 0)
                exponents(n + 2, 2)
                if not last:
                    queries_out(r + 1, k + 1)
                exponents(n + 3, 3)
                transposed_out(n + 2, 2)
                if not last:
                    exponents(n + 4, 0)
                    values_out(r + 1, k + 1)
                    exponents(n + 5, 1)
                    gates_out(r + 1, k + 1)
            rows(act, row)

        @block.vector
        def _(dve):
            def biased(n, h):
                dve.wait_ge(s_mm, n + 1)
                dve.nop(nofuse=True)
                for c in range(KC):
                    last = nc.vector.tensor_tensor_reduce(out=probs[:, h, c], in0=b_s[h % 2][:, c * W:(c + 1) * W], in1=m.bias0[:, c, h], scale=-1.0,
                                                          scalar=3.0e38, op0=ALU.add, op1=ALU.min, accum_out=neg_max[:, h, c:c + 1])
                last.then_inc(s_ready, 1)

            def inverse(n, h):
                dve.wait_ge(exp_ready, n + 1)
                nc.vector.reciprocal(inv[:, h], total[:, h]).then_inc(inv_ready, 1)

            def queries_out(r, k):
                dve.wait_ge(qb_mm, r + 1)
                nc.vector.tensor_copy(qk[:, k % 2, 2:4], b_qb[:].rearrange("p (h c) -> p h c", h=2)).then_inc(qb_ready, 1)

            def transposed_out(n, h):
                dve.wait_ge(t_mm, n + 1)
                nc.vector.tensor_copy(probs_t[:, h], b_t[1][:].rearrange("p (a c) -> p a c", a=KC)).then_inc(t_dve, 1)

            def gated(r, k):
                dve.wait_ge(av_mm, 2 * r + 2)
                dve.wait_ge(g_ready, r + 1)
                nc.vector.scalar_tensor_tensor(out=o[:, k % 2], in0=gate[:, k % 2], scalar=1.0, in1=b_av[:].rearrange("p (a c) -> p a c", a=HC),
                                               op0=ALU.add, op1=ALU.mult).then_inc(o_ready, 1)

            def residual(t, k):
                r, kk = UNROLL * t + k, k % UNROLL
                tt = t + (k - kk) // UNROLL
                i, j = kk // TILE, kk % TILE
                dve.wait_ge(out_mm, r + 1)
                if j == 0:
                    wait(dve, y_stored[i % 2], 16 * (BUFS // 2 * tt + i // 2))
                nc.vector.scalar_tensor_tensor(out=y[:, i % 2, j], in0=b_out[:, 0:W], scalar=m.wrep_b[:], in1=xt[:, i, j],
                                               op0=ALU.add, op1=ALU.add).then_inc(y_ready, 1)

            queries_out(0, 0)
            biased(0, 0)
            biased(1, 1)
            inverse(0, 0)
            inverse(1, 1)

            def body(t, first_body, last_body):
                for k in range(UNROLL):
                    r, first, last = UNROLL * t + k, first_body and k == 0, last_body and k == UNROLL - 1
                    n = NH0 * r
                    biased(n + 2, 2)
                    if not first:
                        gated(r - 1, k + 1)
                    inverse(n + 2, 2)
                    biased(n + 3, 3)
                    transposed_out(n + 1, 1)
                    if not last:
                        queries_out(r + 1, k + 1)
                    if not first:
                        residual(t, k - 1)
                    inverse(n + 3, 3)
                    if not last:
                        biased(n + 4, 0)
                        inverse(n + 4, 0)
                        biased(n + 5, 1)
                    transposed_out(n + 3, 3)
                    if not last:
                        inverse(n + 5, 1)
            loop_ends_peeled(dve, W // UNROLL, body)
            gated(W - 1, W - 1)
            residual(W // UNROLL - 1, UNROLL - 1)


def layer1(nc, m, x1, out):
    UNROLL = 4
    SCALE = D1 ** -0.5
    BY_DVE = (3, 7)
    with ExitStack() as ctx:
        sem = lambda name: ctx.enter_context(nc.semaphore(f"l1_{name}"))
        sb = lambda name, shape: ctx.enter_context(nc.sbuf_tensor(f"l1_{name}", shape, F32))
        xt = sb("x", [P, UNROLL, KC, W])
        xn = sb("xn", [P, HC, W])
        kt = sb("k", [P, 2, HC, W])
        probs = sb("probs", [P, 4, KC, W])
        probs_t = sb("probs_t", [P, NH1, KC, W])
        v = sb("v", [P, 2, KC, HC * P])
        gate = sb("gate", [P, 2, HC, W])
        o = sb("o", [P, HC, W])
        y = sb("y", [P, 2, KC, W])
        neg_max = sb("neg_max", [P, 4, KC])
        total = sb("total", [P, 4, KC])
        inv = sb("inv", [P, 4, KC])
        by_channel = sb("by_channel", [P, 2, HC])
        b_q, b_k = m.psum[0], m.psum[1]
        b_s, b_t, b_av, b_out = m.psum[2:4], m.psum[4:6], m.psum[6], m.psum[7]
        loaded = [sem(f"loaded{i}") for i in range(UNROLL)]
        y_stored = [sem(f"y_stored{i}") for i in range(2)]
        (stat_mm, stat_ready, x_mm, x_ready, q_mm, k_mm, v_mm, g_mm, q_ready, k_ready, v_ready, g_ready, s_mm, max_ready, exp_ready, inv_ready,
         p_ready, t_mm, t_act, t_dve, av_mm, o_ready, out_mm, y_ready) = (sem(n) for n in (
            "stat_mm", "stat_ready", "x_mm", "x_ready", "q_mm", "k_mm", "v_mm", "g_mm", "q_ready", "k_ready", "v_ready", "g_ready", "s_mm",
            "max_ready", "exp_ready", "inv_ready", "p_ready", "t_mm", "t_act", "t_dve", "av_mm", "o_ready", "out_mm", "y_ready"))
        block = ctx.enter_context(nc.Block())

        def copies(s, h, dve):
            mine = [g for g in range(NH1) if (g in BY_DVE) == dve]
            return len(mine) * s + len([g for g in mine if g <= h])

        def wait_copied(engine, s, h):
            dve = h in BY_DVE
            wait(engine, t_dve if dve else t_act, copies(s, h, dve))

        def sequences(engine, sequence):
            def body(t, first, last):
                for k in range(UNROLL):
                    sequence(UNROLL * t + k, k, first and k == 0, last and k == UNROLL - 1)
            loop_ends_peeled(engine, C0 // UNROLL, body)

        @block.sync
        def _(sp):
            def load(s, i):
                sp.dma_start(xt[:, i], x1[bass.ds(s, 1)].rearrange("o (a p) c -> p (o a) c", p=P)).then_inc(loaded[i], 16)

            for i in range(UNROLL):
                load(i, i)

            def body(t, first, last):
                for i in range(UNROLL):
                    s = UNROLL * t + i
                    sp.wait_ge(y_ready, s + 1)
                    sp.dma_start(out[bass.ds(s, 1)].rearrange("o (a p) c -> p (o a) c", p=P), y[:, i % 2]).then_inc(y_stored[i % 2], 16)
                    if not last:
                        load(s + UNROLL, i)
            loop_ends_peeled(sp, C0 // UNROLL, body)
            for i in range(2):
                sp.wait_ge(y_stored[i], 16 * C0 // 2)

        @block.tensor
        def _(pe):
            def turn(t, k):
                s, i, tt = UNROLL * t + k, k % UNROLL, t + k // UNROLL
                pe.wait_ge(loaded[i], 16 * (tt + 1))
                wait(pe, y_ready, s - 2)
                for c in range(HC):
                    for a in range(KC):
                        last = nc.tensor.transpose(b_out[:, c * W + a * P:c * W + (a + 1) * P], xt[:, i, a, c * P:(c + 1) * P], m.ident[:])
                last.then_inc(x_mm, 1)

            def by_weights(bank, weights, first_column):
                for j in range(HC):
                    for c in range(HC):
                        at = first_column + j * P
                        last = nc.tensor.matmul(bank[:, j * W:(j + 1) * W], weights[:, c, at:at + P], xn[:, c], start=c == 0, stop=c == HC - 1)
                return last

            def queries(s):
                pe.wait_ge(x_ready, s + 1)
                wait(pe, v_ready, s)
                by_weights(b_q, m.w_qkv1, 0).then_inc(q_mm, 1)

            def keys(s):
                wait(pe, g_ready, s)
                by_weights(b_k, m.w_qkv1, 256).then_inc(k_mm, 1)

            def values(s):
                pe.wait_ge(q_ready, s + 1)
                for a in range(KC):
                    for c in range(HC):
                        last = nc.tensor.matmul(b_q[:, a * W:(a + 1) * W], xn[:, c, a * P:(a + 1) * P], m.w_qkv1[:, c, 512:768], start=c == 0, stop=c == HC - 1)
                last.then_inc(v_mm, 1)

            def gates(s):
                pe.wait_ge(k_ready, s + 1)
                by_weights(b_k, m.w_gate1, 0).then_inc(g_mm, 1)

            def scores(s, k, h):
                n = NH1 * s + h
                pe.wait_ge(q_ready, s + 1)
                pe.wait_ge(k_ready, s + 1)
                wait(pe, exp_ready, n - 1)
                for c in range(KC):
                    last = nc.tensor.matmul(b_s[h % 2][:, c * W:(c + 1) * W], m.q1[:, k % 2, h // 4, h % 4, c * P:(c + 1) * P], kt[:, k % 2, h // 4],
                                            start=True, stop=True)
                last.then_inc(s_mm, 1)

            def transposes(s, h):
                n = NH1 * s + h
                pe.wait_ge(p_ready, n + 1)
                if h >= 2:
                    wait_copied(pe, s, h - 2)
                else:
                    wait_copied(pe, s - 1, h + NH1 - 2)
                for kc in range(KC):
                    for qc in range(KC):
                        last = nc.tensor.transpose(b_t[h % 2][:, kc * W + qc * P:kc * W + (qc + 1) * P], probs[:, h % 4, qc, kc * P:(kc + 1) * P], m.ident[:])
                last.then_inc(t_mm, 1)

            def attend(s, k, half):
                for h in (4 * half + 2, 4 * half + 3):
                    wait_copied(pe, s, h)
                pe.wait_ge(v_ready, s + 1)
                wait(pe, o_ready, s)
                for kc in range(KC):
                    for j in range(4):
                        h = 4 * half + j
                        last = nc.tensor.matmul(b_av[D1 * j:D1 * (j + 1), half * W:(half + 1) * W], v[:, k % 2, kc, h * D1:(h + 1) * D1],
                                                probs_t[:, h, kc], start=kc == 0, stop=kc == KC - 1, tile_position=(0, D1 * j))
                last.then_inc(av_mm, 1)

            def project_out(s):
                pe.wait_ge(o_ready, s + 1)
                wait(pe, x_ready, s + 3 if not isinstance(s, int) or s + 3 <= C0 else C0)
                for a in range(KC):
                    for c in range(HC):
                        last = nc.tensor.matmul(b_out[:, a * W:(a + 1) * W], o[:, c, a * P:(a + 1) * P], m.w_out1[:, c], start=c == 0, stop=c == HC - 1)
                last.then_inc(out_mm, 1)

            for c in range(HC):
                nc.tensor.transpose(b_q[:, c * P:(c + 1) * P], m.mean[:, c * P:(c + 1) * P], m.ident[:])
                last = nc.tensor.transpose(b_k[:, c * P:(c + 1) * P], m.rstd[:, c * P:(c + 1) * P], m.ident[:])
            last.then_inc(stat_mm, 1)
            pe.wait_ge(stat_ready, 1)
            turn(0, 0)
            queries(0)
            keys(0)
            values(0)
            gates(0)
            scores(0, 0, 0)
            scores(0, 0, 1)

            def body(t, first_body, last_body):
                for k in range(UNROLL):
                    s, first, last = UNROLL * t + k, first_body and k == 0, last_body and k == UNROLL - 1
                    for h in range(NH1):
                        if h < NH1 - 2:
                            scores(s, k, h + 2)
                        elif not last:
                            scores(s + 1, k + 1, h + 2 - NH1)
                        transposes(s, h)
                        if h == 1 and not first:
                            attend(s - 1, k + 1, 1)
                        if h == 2 and not last:
                            turn(t, k + 1)
                        if h == 3 and not last:
                            queries(s + 1)
                        if h == 3 and not first:
                            project_out(s - 1) if not last else project_out(s - 1)
                        if h == 4 and not last:
                            keys(s + 1)
                        if h == 5:
                            attend(s, k, 0)
                            if not last:
                                values(s + 1)
                        if h == 6 and not last:
                            gates(s + 1)
            loop_ends_peeled(pe, C0 // UNROLL, body)
            attend(C0 - 1, C0 - 1, 1)
            project_out(C0 - 1)

        @block.scalar
        def _(act):
            def exponents(n, h):
                act.wait_ge(max_ready, n + 1)
                for c in range(KC):
                    last = nc.scalar.activation(probs[:, h % 4, c], b_s[h % 2][:, c * W:(c + 1) * W], ACT.Exp, bias=neg_max[:, h % 4, c:c + 1],
                                                accum_out=total[:, h % 4, c:c + 1])
                last.then_inc(exp_ready, 1)

            def queries_out(s, k):
                act.wait_ge(q_mm, s + 1)
                for j in range(4):
                    at = slice(D1 * j, D1 * (j + 1))
                    last = nc.scalar.activation(m.q1[at, k % 2, :, j, :], b_q[at, :].rearrange("p (a c) -> p a c", a=HC), ACT.Copy, scale=SCALE)
                last.then_inc(q_ready, 1)

            def keys_out(s, k):
                act.wait_ge(k_mm, s + 1)
                nc.scalar.activation(kt[:, k % 2], b_k[:].rearrange("p (a c) -> p a c", a=HC), ACT.Copy).then_inc(k_ready, 1)

            def values_out(s, k):
                act.wait_ge(v_mm, s + 1)
                nc.scalar.activation(v[:, k % 2], b_q[:].rearrange("p (a c) -> p a c", a=KC), ACT.Copy).then_inc(v_ready, 1)

            def gates_out(s, k):
                act.wait_ge(g_mm, s + 1)
                nc.scalar.activation(gate[:, k % 2], b_k[:].rearrange("p (a c) -> p a c", a=HC), ACT.Tanh, scale=0.5).then_inc(g_ready, 1)

            def transposed_out(n, h):
                act.wait_ge(t_mm, n + 1)
                nc.scalar.activation(probs_t[:, h], b_t[h % 2][:].rearrange("p (a c) -> p a c", a=KC), ACT.Copy).then_inc(t_act, 1)

            queries_out(0, 0)
            keys_out(0, 0)
            values_out(0, 0)
            gates_out(0, 0)
            exponents(0, 0)
            exponents(1, 1)

            def sequence(s, k, first, last):
                for h in range(NH1):
                    n = NH1 * s + h
                    if not (last and h >= NH1 - 2):
                        exponents(n + 2, (h + 2) % NH1)
                    if h not in BY_DVE:
                        transposed_out(n, h)
                    if not last:
                        if h == 3:
                            queries_out(s + 1, k + 1)
                        if h == 4:
                            keys_out(s + 1, k + 1)
                        if h == 5:
                            values_out(s + 1, k + 1)
                        if h == 6:
                            gates_out(s + 1, k + 1)
            sequences(act, sequence)

        @block.vector
        def _(dve):
            def maxima(n, h):
                dve.wait_ge(s_mm, n + 1)
                nc.vector.tensor_reduce(neg_max[:, h % 4], b_s[h % 2][:].rearrange("p (a c) -> p a c", a=KC), AX.X, ALU.max, negate=True).then_inc(max_ready, 1)

            def divide(n, h):
                dve.wait_ge(exp_ready, n + 1)
                nc.vector.reciprocal(inv[:, h % 4], total[:, h % 4]).then_inc(inv_ready, 1)
                dve.wait_ge(inv_ready, n + 1)
                for c in range(KC):
                    last = nc.vector.scalar_tensor_tensor(out=probs[:, h % 4, c], in0=probs[:, h % 4, c], scalar=inv[:, h % 4, c:c + 1], in1=m.bias1[:, c, h],
                                                          op0=ALU.mult, op1=ALU.add)
                last.then_inc(p_ready, 1)

            def transposed_out(n, h):
                dve.wait_ge(t_mm, n + 1)
                nc.vector.tensor_copy(probs_t[:, h], b_t[h % 2][:].rearrange("p (a c) -> p a c", a=KC)).then_inc(t_dve, 1)

            def group_norm(s):
                dve.wait_ge(x_mm, s + 1)
                for c in range(HC):
                    last = nc.vector.tensor_scalar(xn[:, c], b_out[:, c * W:(c + 1) * W], by_channel[:, 0, c:c + 1], by_channel[:, 1, c:c + 1],
                                                   ALU.subtract, ALU.mult)
                last.then_inc(x_ready, 1)

            def gated(s, k):
                dve.wait_ge(av_mm, 2 * s + 2)
                dve.wait_ge(g_ready, s + 1)
                nc.vector.scalar_tensor_tensor(out=o[:], in0=gate[:, k % 2], scalar=1.0, in1=b_av[:].rearrange("p (a c) -> p a c", a=HC),
                                               op0=ALU.add, op1=ALU.mult).then_inc(o_ready, 1)

            def residual(t, k):
                s, i = UNROLL * t + k, k % UNROLL
                tt = t + (k - i) // UNROLL
                dve.wait_ge(out_mm, s + 1)
                wait(dve, y_stored[i % 2], 16 * (UNROLL // 2 * tt + i // 2))
                nc.vector.tensor_tensor(y[:, i % 2], b_out[:].rearrange("p (a c) -> p a c", a=KC), xt[:, i], ALU.add).then_inc(y_ready, 1)

            dve.wait_ge(stat_mm, 1)
            nc.vector.tensor_copy(by_channel[:, 0], b_q[:, 0:HC * P].rearrange("p (c n) -> p c n", n=P)[:, :, 0])
            nc.vector.tensor_copy(by_channel[:, 1], b_k[:, 0:HC * P].rearrange("p (c n) -> p c n", n=P)[:, :, 0]).then_inc(stat_ready, 1)
            dve.wait_ge(stat_ready, 1)
            group_norm(0)
            maxima(0, 0)
            maxima(1, 1)
            divide(0, 0)

            def body(t, first_body, last_body):
                for k in range(UNROLL):
                    s, first, last = UNROLL * t + k, first_body and k == 0, last_body and k == UNROLL - 1
                    for h in range(NH1):
                        n = NH1 * s + h
                        if not (last and h >= NH1 - 2):
                            maxima(n + 2, (h + 2) % NH1)
                        if not (last and h >= NH1 - 1):
                            divide(n + 1, (h + 1) % NH1)
                        if h in BY_DVE:
                            transposed_out(n, h)
                        if h == 1 and not first:
                            gated(s - 1, k + 1)
                        if h == 2 and not last:
                            group_norm(s + 1)
                        if h == 3 and not first:
                            residual(t, k - 1)
            loop_ends_peeled(dve, C0 // UNROLL, body)
            gated(C0 - 1, C0 - 1)
            residual(C0 // UNROLL - 1, UNROLL - 1)


class Memory:
    pass


def build(nc, x, ln_w, ln_b, wq, wk, wv, wb, wg_w, wg_b, wrep_w, wrep_b, pair, gate_proj, qkv_proj, out_proj, bias_proj, out, phases=7):
    m = Memory()
    with ExitStack() as ctx:
        sb = lambda name, shape: ctx.enter_context(nc.sbuf_tensor(name, shape, F32))
        m.psum = [ctx.enter_context(nc.psum_tensor(f"bank{i}", [P, 512], F32)) for i in range(8)]
        m.ident = sb("ident", [P, P])
        m.averager = sb("averager", [P, P])
        m.wqk = sb("wqk", [C0, NH0, C0])
        m.wv_t = sb("wv_t", [C0, 256])
        m.wg_t = sb("wg_t", [C0, 256])
        m.wrep_t = sb("wrep_t", [P, HC, C0])
        m.wb_t = sb("wb_t", [C0, 32])
        m.wg_b_half = sb("wg_b_half", [P, HC])
        m.wrep_b = sb("wrep_b", [C0, 1])
        m.w_pair = sb("w_pair", [P, 32])
        m.w_gate1 = sb("w_gate1", [P, HC, 256])
        m.w_qkv1 = sb("w_qkv1", [P, HC, 768])
        m.w_out1 = sb("w_out1", [P, HC, 256])
        m.bias0 = sb("bias0", [P, KC, NH0, W])
        m.bias1 = sb("bias1", [P, KC, NH1, W])
        m.q1 = sb("q1", [P, 2, HC, 4, W])
        m.mean = sb("mean", [P, W])
        m.rstd = sb("rstd", [P, W])
        image_bias = nc.dram_tensor("image_bias", (NH0, W, W), F32).ap()
        pair_bias = nc.dram_tensor("pair_bias", (NH1, W, W), F32).ap()
        x1 = nc.dram_tensor("x1", (C0, W, W), F32).ap()
        x, ln_w, ln_b, pair, out = x[0], ln_w, ln_b, pair[0], out[0]
        args = {"wq": wq, "wk": wk, "wv": wv, "wg_w": wg_w, "wrep_w": wrep_w, "wg_b": wg_b, "wrep_b": wrep_b, "gate_proj": gate_proj,
                "qkv_proj": qkv_proj, "out_proj": out_proj, "wb": wb, "bias_proj": bias_proj}
        prepare_weights(nc, m, args)
        with nc.sbuf_tensor("stage", [P, 6 * ROWS_B * W], F32) as stage:
            m.stage = stage
            group_statistics(nc, m, "gs0", x, True)
            project_image_bias(nc, m, x, ln_w, ln_b, image_bias)
            project_pair_bias(nc, m, pair, pair_bias)
        layer0(nc, m, x, ln_w, ln_b, x1)
        with nc.sbuf_tensor("stage1", [P, 4 * ROWS_B * W], F32) as stage:
            m.stage = stage
            group_statistics(nc, m, "gs1", x1, False)
        layer1(nc, m, x1, out)


_INS = ["x", "L0_conv_ln_w", "L0_conv_ln_b", "L0_conv_wq", "L0_conv_wk", "L0_conv_wv", "L0_conv_wb", "L0_conv_wg_w", "L0_conv_wg_b",
        "L0_conv_wrep_w", "L0_conv_wrep_b", "L1_conv_pair_repr", "L1_conv_gate_proj", "L1_conv_qkv_proj", "L1_conv_out_proj", "L1_conv_bias_proj"]


def kernel(**inputs):
    import numpy as _np
    import concourse.bacc as _bacc
    from concourse import mybir as _mybir
    from concourse.bass_utils import run_bass_kernel_spmd as _run

    nc = _bacc.Bacc("TRN2", target_bir_lowering=False, num_devices=1)
    arrays, args = {}, []
    for name in _INS:
        a = _np.ascontiguousarray(inputs[name])
        arrays[f"in_{name}_dram"] = a
        args.append(nc.dram_tensor(f"in_{name}_dram", a.shape, _mybir.dt.from_np(a.dtype), kind="ExternalInput").ap())
    args.append(nc.dram_tensor("out_dram", (1, 128, 256, 256), _mybir.dt.from_np(_np.dtype("float32")), kind="ExternalOutput").ap())
    build(nc, *args)
    r = _run(nc, [arrays], core_ids=[0])
    return r.results[0]["out_dram"]
```

```python
import concourse.bass as bass
from concourse import mybir
from contextlib import ExitStack

F32 = mybir.dt.float32
F32R = mybir.dt.float32r
ALU = mybir.AluOpType
ACT = mybir.ActivationFunctionType
AX = mybir.AxisListType

P = 128
C0 = 128
W = 256
KC = W // P
GROUP = 8
NG = W // GROUP
NH0, D0 = 4, 64
NH1, D1 = 8, 32
EPS = 1e-5
HC = 2


MOST_AHEAD = 3


def wait(engine, sem, value):
    if not (isinstance(value, int) and value <= 0):
        engine.wait_ge(sem, value)


def loop_first_peeled(engine, count, body):
    body(0)
    with engine.Fori(1, count) as t:
        body(t)


def loop_ends_peeled(engine, count, body):
    body(0, True, False)
    with engine.Fori(1, count - 1) as t:
        body(t, False, False)
    body(count - 1, False, True)


def over_rows(engine, total, unroll, row):
    def body(t, first, last):
        for k in range(-MOST_AHEAD if first else 0, unroll + 1 if last else unroll):
            row(t, k, lambda d, k=k: (not first or k + d >= 0) and (not last or k + d < unroll))
    loop_ends_peeled(engine, total // unroll, body)


class Chain:

    def __init__(self, engine, sem):
        self.engine, self.sem, self.count = engine, sem, 0

    def __call__(self, instruction):
        self.count += 1
        instruction.then_inc(self.sem, 1)
        self.engine.wait_ge(self.sem, self.count)


def matmul_split(nc, out, left, right, start=True, stop=True):
    (lh, ll), (rh, rl) = left, right
    nc.tensor.matmul(out, lh, rh, start=start, stop=False)
    nc.tensor.matmul(out, lh, rl, start=False, stop=False)
    return nc.tensor.matmul(out, ll, rh, start=False, stop=stop)


def prepare_weights(nc, m, a):
    with ExitStack() as ctx:
        sem = lambda name: ctx.enter_context(nc.semaphore(name))
        sb = lambda name, shape: ctx.enter_context(nc.sbuf_tensor(name, shape, F32))
        wq = sb("wq_raw", [D0, NH0, C0])
        wk = sb("wk_raw", [D0, NH0, C0])
        wv = sb("wv_raw", [P, HC, C0])
        wg = sb("wg_raw", [P, HC, C0])
        wrep = sb("wrep_raw", [C0, D0, NH0])
        wrep_h = sb("wrep_by_head", [C0, NH0, D0])
        wb = sb("wb_raw", [32, C0])
        wgb = sb("wgb_raw", [P, HC])
        w_gate1, w_qkv1, w_out1 = sb("gate1_raw", [P, HC, 256]), sb("qkv1_raw", [P, HC, 768]), sb("out1_raw", [P, HC, 256])
        wqk1 = sb("qk1_permuted", [P, HC, 2, HC, P])
        wqk, wv_t, wg_t = sb("wqk_whole", [C0, NH0, C0]), sb("wv_t_whole", [C0, 256]), sb("wg_t_whole", [C0, 256])
        loaded, zeroed, ident_step, ident_ready = sem("w_loaded"), sem("w_zeroed"), sem("ident_step"), sem("ident_ready")
        permuted, folded, turned, step = sem("w_permuted"), sem("w_folded"), sem("w_turned"), sem("w_step")
        wb_loaded = sem("wb_loaded")
        LOADS = 11
        block = ctx.enter_context(nc.Block())

        @block.sync
        def _(sp):
            sp.dma_start(wq[:], a["wq"].rearrange("(h d) c -> d h c", h=NH0)).then_inc(loaded, 16)
            sp.dma_start(wk[:], a["wk"].rearrange("(h d) c -> d h c", h=NH0)).then_inc(loaded, 16)
            sp.dma_start(wv[:], a["wv"].rearrange("(a p) c -> p a c", p=P)).then_inc(loaded, 16)
            sp.dma_start(wg[:], a["wg_w"].rearrange("(a p) c -> p a c", p=P)).then_inc(loaded, 16)
            sp.dma_start(wrep[:], a["wrep_w"].rearrange("o (c h) -> o c h", h=NH0)).then_inc(loaded, 16)
            for c in range(HC):
                sp.dma_start(wgb[:, c:c + 1], a["wg_b"][c * P:(c + 1) * P].rearrange("(p a) -> p a", a=1)).then_inc(loaded, 16)
            sp.dma_start(m.wrep_b[:], a["wrep_b"].rearrange("(p a) -> p a", a=1)).then_inc(loaded, 16)
            sp.dma_start(w_gate1[:], a["gate_proj"].rearrange("(a p) n -> p a n", p=P)).then_inc(loaded, 16)
            sp.dma_start(w_qkv1[:], a["qkv_proj"].rearrange("(a p) n -> p a n", p=P)).then_inc(loaded, 16)
            sp.dma_start(w_out1[:], a["out_proj"].rearrange("(a p) n -> p a n", p=P)).then_inc(loaded, 16)
            sp.wait_ge(zeroed, 1)
            sp.dma_start(wb[0:NH0, :], a["wb"]).then_inc(wb_loaded, 16)
            sp.dma_start(m.w_pair[:, 0:NH1], a["bias_proj"]).then_inc(wb_loaded, 16)
            sp.wait_ge(loaded, 16 * LOADS)
            sp.wait_ge(wb_loaded, 32)

        @block.gpsimd
        def _(pool):
            nc.gpsimd.memset(m.ident[:], 0.0).then_inc(ident_step, 1)
            pool.wait_ge(ident_step, 1)
            nc.gpsimd.affine_select(out=m.ident[:], in_=m.ident[:], compare_op=ALU.not_equal, fill=1.0, base=0,
                                    pattern=[[-1, P]], channel_multiplier=1).then_inc(ident_ready, 1)

        @block.vector
        def _(dve):
            nc.vector.memset(wb[:], 0.0)
            nc.vector.memset(m.w_pair[:], 0.0).then_inc(zeroed, 1)
            nc.vector.memset(m.averager[:], 1.0 / P)
            dve.wait_ge(loaded, 16 * LOADS)
            nc.vector.tensor_copy(wrep_h[:], wrep[:].rearrange("o c h -> o h c")).then_inc(permuted, 1)
            chain = Chain(dve, step)

            def split(parts, whole):
                chain(nc.vector.tensor_copy(parts[0][:], whole))
                chain(nc.vector.tensor_tensor(parts[1][:], whole, parts[0][:].bitcast(F32), ALU.subtract))

            nc.vector.tensor_scalar(m.wg_b_half[:], wgb[:], 0.5, None, ALU.mult)
            for c in range(HC):
                for j in range(HC):
                    columns = lambda at: w_qkv1[:, c, at + j * P:at + (j + 1) * P].rearrange("p (a d) -> p d a", d=D1)
                    nc.vector.tensor_scalar(wqk1[:, c, 0, j].rearrange("p (d a) -> p d a", d=D1), columns(0), D1 ** -0.5, None, ALU.mult)
                    nc.vector.tensor_copy(wqk1[:, c, 1, j].rearrange("p (d a) -> p d a", d=D1), columns(256))
            chain(nc.vector.tensor_scalar(m.w_out1[:], w_out1[:], 0.5, None, ALU.mult))
            split(m.w_qk1, wqk1[:])
            split(m.w_v1, w_qkv1[:, :, 512:768])
            split(m.w_gate1, w_gate1[:])
            dve.wait_ge(folded, 1)
            chain(nc.vector.tensor_scalar(wqk[:], m.psum[0][:].rearrange("p (h c) -> p h c", h=NH0), D0 ** -0.5, None, ALU.mult))
            dve.wait_ge(turned, 1)
            nc.vector.tensor_copy(wv_t[:], m.psum[1][:, 0:256])
            nc.vector.tensor_copy(wg_t[:], m.psum[1][:, 256:512])
            nc.vector.tensor_scalar(m.wrep_t[:], m.psum[2][:, 0:256].rearrange("p (a o) -> p a o", a=HC), 0.5, None, ALU.mult)
            chain(nc.vector.tensor_copy(m.wb_t[:], m.psum[2][:, 256:288]))
            split(m.wqk, wqk[:])
            split(m.wv_t, wv_t[:])
            split(m.wg_t, wg_t[:])

        @block.tensor
        def _(pe):
            pe.wait_ge(loaded, 16 * LOADS)
            for h in range(NH0):
                last = nc.tensor.matmul(m.psum[0][:, h * C0:(h + 1) * C0], wq[:, h, :], wk[:, h, :], start=True, stop=True)
            last.then_inc(folded, 1)
            pe.wait_ge(ident_ready, 1)
            pe.wait_ge(permuted, 1)
            pe.wait_ge(wb_loaded, 32)
            for c in range(HC):
                nc.tensor.transpose(m.psum[1][:, c * P:(c + 1) * P], wv[:, c, :], m.ident[:])
                nc.tensor.transpose(m.psum[1][:, 256 + c * P:256 + (c + 1) * P], wg[:, c, :], m.ident[:])
                nc.tensor.transpose(m.psum[2][:, c * P:(c + 1) * P],
                                    wrep_h[:, 2 * c:2 * c + 2, :].rearrange("o h d -> o (h d)"), m.ident[:])
            nc.tensor.transpose(m.psum[2][:, 256:288], wb[:], m.ident[0:32, 0:32]).then_inc(turned, 1)


def group_statistics(nc, m, tag, source, with_layer_norm):
    ROWS, TILES = 32, W // 32
    with ExitStack() as ctx:
        sem = lambda name: ctx.enter_context(nc.semaphore(f"{tag}_{name}"))
        sb = lambda name, shape: ctx.enter_context(nc.sbuf_tensor(f"{tag}_{name}", shape, F32))
        tiles = [m.stage[:, i * ROWS * W:(i + 1) * ROWS * W].rearrange("p (r c) -> p r c", c=W) for i in range(2)]
        stats = sb("stats", [P, NG, TILES, 6])
        own = sb("own", [P, NG, 2])
        mean_var = sb("mean_var", [P, NG, 2])
        dev = sb("dev", [P, NG])
        var = sb("var", [P, NG])
        ve = sb("ve", [P, NG + 1])
        root = sb("root", [P, NG + 1])
        tmp = sb("tmp", [P, NG + 1])
        inv = sb("inv", [P, NG + 1])
        tile_loaded = [sem("tile_loaded0"), sem("tile_loaded1")]
        tile_read, step, own_ready, mean_mm, dev_ready, dev_mm = sem("tile_read"), sem("step"), sem("own_ready"), sem("mean_mm"), sem("dev_ready"), sem("dev_mm")
        ve_ready, root_ready = sem("ve_ready"), sem("root_ready")
        block = ctx.enter_context(nc.Block())

        @block.sync
        def _(sp):
            def body(t):
                for i in range(2):
                    wait(sp, tile_read, 2 * t + i - 1)
                    sp.dma_start(tiles[i], source[:, bass.ds(ROWS * (2 * t + i), ROWS), :]).then_inc(tile_loaded[i], 16)
            loop_first_peeled(sp, TILES // 2, body)

        @block.vector
        def _(dve):
            for tile in range(TILES):
                i = tile % 2
                dve.wait_ge(tile_loaded[i], 16 * (tile // 2 + 1))
                for g in range(NG):
                    last = nc.vector.bn_stats(stats[:, g, tile, :], tiles[i][:, :, g * GROUP:(g + 1) * GROUP])
                last.then_inc(tile_read, 1)
            dve.wait_ge(tile_read, TILES)
            for g in range(NG):
                last = nc.vector.bn_aggr(own[:, g, :], stats[:, g, :, :])
            last.then_inc(own_ready, 1)
            chain = Chain(dve, step)
            dve.wait_ge(own_ready, 1)
            dve.wait_ge(mean_mm, 1)
            chain(nc.vector.tensor_copy(mean_var[:], m.psum[0][:, 0:2 * NG].rearrange("p (g s) -> p g s", s=2)))
            chain(nc.vector.tensor_tensor(dev[:], own[:, :, 0], mean_var[:, :, 0], ALU.subtract))
            nc.vector.tensor_tensor(dev[:], dev[:], dev[:], ALU.mult).then_inc(dev_ready, 1)
            dve.wait_ge(dev_mm, 1)
            chain(nc.vector.tensor_tensor(var[:], m.psum[1][:, 0:NG], mean_var[:, :, 1], ALU.add))
            nc.vector.tensor_copy(m.mean[:].rearrange("p (g e) -> p g e", e=GROUP),
                                  mean_var[:, :, 0:1].broadcast_to([P, NG, GROUP]))

            def inverse_root(cols, n):
                dve.wait_ge(root_ready, n)
                chain(nc.vector.reciprocal(inv[:, cols], root[:, cols]))
                chain(nc.vector.tensor_tensor(tmp[:, cols], ve[:, cols], inv[:, cols], ALU.mult))
                chain(nc.vector.tensor_tensor(root[:, cols], root[:, cols], tmp[:, cols], ALU.add))
                chain(nc.vector.reciprocal(tmp[:, cols], root[:, cols]))
                chain(nc.vector.tensor_scalar(inv[:, cols], tmp[:, cols], 2.0, None, ALU.mult))

            nc.vector.tensor_scalar(ve[:, 0:NG], var[:], EPS, None, ALU.add).then_inc(ve_ready, 1)
            inverse_root(slice(0, NG), 1)
            if with_layer_norm:
                chain(nc.vector.tensor_tensor(dev[:], var[:], inv[:, 0:NG], ALU.mult))
                chain(nc.vector.tensor_tensor(var[:], dev[:], inv[:, 0:NG], ALU.mult))
                chain(nc.vector.reduce_sum(tmp[:, NG:NG + 1], var[:], AX.X))
                nc.vector.tensor_scalar(ve[:, NG:NG + 1], tmp[:, NG:NG + 1], 1.0 / NG, EPS, ALU.mult, ALU.add).then_inc(ve_ready, 1)
                inverse_root(slice(NG, NG + 1), 2)
                chain(nc.vector.tensor_scalar(tmp[:, 0:NG], inv[:, 0:NG], inv[:, NG:NG + 1], None, ALU.mult))
                chain(nc.vector.tensor_copy(inv[:, 0:NG], tmp[:, 0:NG]))
            chain(nc.vector.tensor_copy(m.rstd[:].rearrange("p (g e) -> p g e", e=GROUP),
                                        inv[:, 0:NG].rearrange("p (g o) -> p g o", o=1).broadcast_to([P, NG, GROUP])))

        @block.scalar
        def _(act):
            act.wait_ge(ve_ready, 1)
            nc.scalar.activation(root[:, 0:NG], ve[:, 0:NG], ACT.Sqrt).then_inc(root_ready, 1)
            if with_layer_norm:
                act.wait_ge(ve_ready, 2)
                nc.scalar.activation(root[:, NG:NG + 1], ve[:, NG:NG + 1], ACT.Sqrt).then_inc(root_ready, 1)

        @block.tensor
        def _(pe):
            pe.wait_ge(own_ready, 1)
            nc.tensor.matmul(m.psum[0][:, 0:2 * NG], m.averager[:], own[:].rearrange("p g s -> p (g s)"), start=True, stop=True).then_inc(mean_mm, 1)
            pe.wait_ge(dev_ready, 1)
            nc.tensor.matmul(m.psum[1][:, 0:NG], m.averager[:], dev[:], start=True, stop=True).then_inc(dev_mm, 1)


ROWS_B = 16
TILES_B = W // ROWS_B


def store_head_rows(sp, tile, evac, scratch, heads, stored):
    for c in range(4):
        sp.dma_start(scratch[:, bass.ds(ROWS_B * tile + 4 * c, 4), :],
                     evac[32 * c:32 * c + heads, :].rearrange("p (r k) -> p r k", k=W)).then_inc(stored, 16)


def project_heads(nc, m, banks, weights, rows):
    for g in range(8):
        c = g // 2
        last = nc.tensor.matmul(banks[g % 2][32 * c:32 * c + 32, :], weights, rows[:, 2 * g:2 * g + 2, :].rearrange("p r c -> p (r c)"),
                                start=True, stop=True, tile_position=(0, 32 * c))
    return last


def project_image_bias(nc, m, x, ln_w, ln_b, scratch):
    with ExitStack() as ctx:
        sem = lambda name: ctx.enter_context(nc.semaphore(f"ib_{name}"))
        size = ROWS_B * W
        view = lambda i: m.stage[:, i * size:(i + 1) * size].rearrange("p (r c) -> p r c", c=W)
        xt, wt, bt = [view(0), view(1)], [view(2), view(3)], [view(4), view(5)]
        evac = [ctx.enter_context(nc.sbuf_tensor(f"ib_evac{i}", [P, 4 * W], F32)) for i in range(2)]
        loaded, stored = [sem("loaded0"), sem("loaded1")], [sem("stored0"), sem("stored1")]
        centred, scaled, weighted, ready, projected, evacuated = (sem(n) for n in ("centred", "scaled", "weighted", "ready", "projected", "evacuated"))
        mean = m.mean[:].rearrange("p (o c) -> p o c", o=1).broadcast_to([P, ROWS_B, W])
        rstd = m.rstd[:].rearrange("p (o c) -> p o c", o=1).broadcast_to([P, ROWS_B, W])
        block = ctx.enter_context(nc.Block())

        @block.sync
        def _(sp):
            def load(tile, i):
                rows = bass.ds(ROWS_B * tile, ROWS_B)
                wait(sp, projected, tile - 1)
                sp.dma_start(xt[i], x[:, rows, :]).then_inc(loaded[i], 16)
                sp.dma_start(wt[i], ln_w[:, rows, :]).then_inc(loaded[i], 16)
                sp.dma_start(bt[i], ln_b[:, rows, :]).then_inc(loaded[i], 16)

            def store(tile, i):
                sp.wait_ge(evacuated, tile + 1)
                store_head_rows(sp, tile, evac[i], scratch, NH0, stored[i])

            load(0, 0)
            load(1, 1)

            def body(t, first, last):
                for i in range(2):
                    store(2 * t + i, i)
                    if not last:
                        load(2 * t + i + 2, i)
            loop_ends_peeled(sp, TILES_B // 2, body)
            for i in range(2):
                sp.wait_ge(stored[i], 16 * 4 * TILES_B // 2)
            for h in range(NH0):
                sp.dma_start(m.bias0[:, :, h, :], scratch[h].rearrange("(a p) k -> p a k", p=P)).then_inc(loaded[0], 16)
            sp.wait_ge(loaded[0], 16 * (3 * TILES_B // 2 + NH0))

        @block.vector
        def _(dve):
            def body(t):
                for i in range(2):
                    tile = 2 * t + i
                    dve.wait_ge(loaded[i], 48 * (t + 1))
                    nc.vector.tensor_tensor(xt[i], xt[i], mean, ALU.subtract).then_inc(centred, 1)
                    dve.wait_ge(centred, tile + 1)
                    nc.vector.tensor_tensor(xt[i], xt[i], rstd, ALU.mult).then_inc(scaled, 1)
                    dve.wait_ge(weighted, tile + 1)
                    nc.vector.tensor_tensor(xt[i], xt[i], bt[i], ALU.add).then_inc(ready, 1)
            loop_first_peeled(dve, TILES_B // 2, body)

        @block.gpsimd
        def _(pool):
            def body(t):
                for i in range(2):
                    pool.wait_ge(scaled, 2 * t + i + 1)
                    nc.gpsimd.tensor_tensor(xt[i], xt[i], wt[i], ALU.mult).then_inc(weighted, 1)
            loop_first_peeled(pool, TILES_B // 2, body)

        @block.tensor
        def _(pe):
            def body(t):
                for i in range(2):
                    tile = 2 * t + i
                    pe.wait_ge(ready, tile + 1)
                    wait(pe, evacuated, tile - 1)
                    project_heads(nc, m, m.psum[2 * i:2 * i + 2], m.wb_t[:], xt[i]).then_inc(projected, 1)
            loop_first_peeled(pe, TILES_B // 2, body)

        @block.scalar
        def _(act):
            def body(t):
                for i in range(2):
                    tile = 2 * t + i
                    act.wait_ge(projected, tile + 1)
                    wait(act, stored[i], 64 * t)
                    view = evac[i][:].rearrange("p (b n) -> p b n", b=2)
                    nc.scalar.activation(view[:, 0, :], m.psum[2 * i][:], ACT.Copy)
                    nc.scalar.activation(view[:, 1, :], m.psum[2 * i + 1][:], ACT.Copy).then_inc(evacuated, 1)
            loop_first_peeled(act, TILES_B // 2, body)


def project_pair_bias(nc, m, pair, scratch):
    with ExitStack() as ctx:
        sem = lambda name: ctx.enter_context(nc.semaphore(f"pb_{name}"))
        size = ROWS_B * W
        raw = [m.stage[:, i * size:(i + 1) * size].rearrange("p (r e z) -> p r e z", e=2, z=P) for i in range(2)]
        turned = [m.stage[:, (2 + i) * size:(3 + i) * size].rearrange("p (r k) -> p r k", k=W) for i in range(2)]
        evac = [ctx.enter_context(nc.sbuf_tensor(f"pb_evac{i}", [P, 4 * W], F32)) for i in range(2)]
        loaded, stored = [sem("loaded0"), sem("loaded1")], [sem("stored0"), sem("stored1")]
        transposed, copied_act, copied_dve, projected, evacuated = (sem(n) for n in ("transposed", "copied_act", "copied_dve", "projected", "evacuated"))
        bank = lambda j: m.psum[4 + j % 4]
        block = ctx.enter_context(nc.Block())
        BANKS = ROWS_B // 2

        @block.sync
        def _(sp):
            def load(tile, i):
                wait(sp, transposed, BANKS * (tile - 1))
                sp.dma_start(raw[i], pair[bass.ds(ROWS_B * tile, ROWS_B)].rearrange("q (p e) z -> p q e z", e=2)).then_inc(loaded[i], 16)

            def store(tile, i):
                sp.wait_ge(evacuated, tile + 1)
                store_head_rows(sp, tile, evac[i], scratch, NH1, stored[i])

            load(0, 0)
            load(1, 1)

            def body(t, first, last):
                for i in range(2):
                    store(2 * t + i, i)
                    if not last:
                        load(2 * t + i + 2, i)
            loop_ends_peeled(sp, TILES_B // 2, body)
            for i in range(2):
                sp.wait_ge(stored[i], 16 * 4 * TILES_B // 2)
            for h in range(NH1):
                sp.dma_start(m.bias1[:, :, h, :], scratch[h].rearrange("(a p) k -> p a k", p=P)).then_inc(loaded[0], 16)
            sp.wait_ge(loaded[0], 16 * (TILES_B // 2 + NH1))

        @block.tensor
        def _(pe):
            def project(tile, i):
                pe.wait_ge(copied_act, BANKS // 2 * (tile + 1))
                pe.wait_ge(copied_dve, BANKS // 2 * (tile + 1))
                wait(pe, evacuated, tile - 1)
                project_heads(nc, m, m.psum[2 * i:2 * i + 2], m.w_pair[:], turned[i]).then_inc(projected, 1)

            def body(t, first, last):
                for i in range(2):
                    tile = 2 * t + i
                    pe.wait_ge(loaded[i], 16 * (t + 1))
                    for j in range(BANKS):
                        wait(pe, copied_act if j % 2 == 0 else copied_dve, BANKS // 2 * tile + j // 2 - 1)
                        for r in range(2):
                            for e in range(2):
                                lastt = nc.tensor.transpose(bank(j)[:, (2 * r + e) * P:(2 * r + e + 1) * P], raw[i][:, 2 * j + r, e, :], m.ident[:])
                        lastt.then_inc(transposed, 1)
                    if not (first and i == 0):
                        project(tile - 1, 1 - i)
            loop_ends_peeled(pe, TILES_B // 2, body)
            project(TILES_B - 1, 1)

        def copies(engine, copy, own, parity):
            def body(t):
                for i in range(2):
                    tile = 2 * t + i
                    wait(engine, projected, tile - 1)
                    for j in range(parity, BANKS, 2):
                        engine.wait_ge(transposed, BANKS * tile + j + 1)
                        copy(turned[i][:, 2 * j:2 * j + 2, :].rearrange("p r (k e) -> p r e k", e=2),
                             bank(j)[:].rearrange("p (r e k) -> p r e k", r=2, e=2)).then_inc(own, 1)
                    if parity == 0:
                        evacuate(tile - 1, 1 - i, t - (1 - i))
            return body

        def evacuate(tile, i, uses):
            if isinstance(tile, int) and tile < 0:
                return
            nc.scalar.wait_ge(projected, tile + 1)
            wait(nc.scalar, stored[i], 64 * uses)
            view = evac[i][:].rearrange("p (b n) -> p b n", b=2)
            nc.scalar.activation(view[:, 0, :], m.psum[2 * i][:], ACT.Copy)
            nc.scalar.activation(view[:, 1, :], m.psum[2 * i + 1][:], ACT.Copy).then_inc(evacuated, 1)

        @block.scalar
        def _(act):
            body = copies(act, lambda out, in_: nc.scalar.activation(out, in_, ACT.Copy), copied_act, 0)
            loop_first_peeled(act, TILES_B // 2, body)
            evacuate(TILES_B - 1, 1, TILES_B // 2 - 1)

        @block.vector
        def _(dve):
            loop_first_peeled(dve, TILES_B // 2, copies(dve, nc.vector.tensor_copy, copied_dve, 1))


def layer0(nc, m, x, ln_w, ln_b, x1):
    UNROLL, TILE = 8, 2
    BUFS = UNROLL // TILE
    with ExitStack() as ctx:
        sem = lambda name: ctx.enter_context(nc.semaphore(f"l0_{name}"))
        sb = lambda name, shape: ctx.enter_context(nc.sbuf_tensor(f"l0_{name}", shape, F32))
        xt = sb("x", [P, BUFS, TILE, W])
        wt = sb("ln_w", [P, BUFS, TILE, W])
        bt = sb("ln_b", [P, BUFS, TILE, W])
        sb_pair = lambda name, shape: [ctx.enter_context(nc.sbuf_tensor(f"l0_{name}_{part}", shape, F32R)) for part in ("high", "low")]
        xf = sb("xf", [P, 2, W])
        xn = sb_pair("xn", [P, 4, W])
        qk = sb_pair("qk", [P, 2, NH0, W])
        probs = sb("probs", [P, NH0, KC, W])
        probs_t = sb("probs_t", [P, NH0, KC, W])
        v = sb("v", [P, 2, KC, HC * P])
        gate = sb("gate", [P, 2, HC, W])
        o = sb("o", [P, 2, HC, W])
        y = sb("y", [P, 2, TILE, W])
        neg_max = sb("neg_max", [P, NH0, KC])
        total = sb("total", [P, NH0, KC])
        inv = sb("inv", [P, NH0, KC])
        b_qa, b_qb = m.psum[0], m.psum[1]
        b_s, b_t, b_av, b_out = m.psum[2:4], m.psum[4:6], m.psum[6], m.psum[7]
        loaded = [sem(f"loaded{i}") for i in range(BUFS)]
        y_stored = [sem(f"y_stored{i}") for i in range(2)]
        (xn_step, xn_ready, qa_mm, qb_mm, v_mm, g_mm, qa_high, qb_high, qa_ready, qb_ready, v_ready, g_ready, s_mm, s_ready, exp_ready, inv_ready,
         p_ready, t_mm, t_act, t_dve, av_mm, o_ready, out_mm, y_ready) = (sem(n) for n in (
            "xn_step", "xn_ready", "qa_mm", "qb_mm", "v_mm", "g_mm", "qa_high", "qb_high", "qa_ready", "qb_ready", "v_ready", "g_ready", "s_mm", "s_ready",
            "exp_ready", "inv_ready", "p_ready", "t_mm", "t_act", "t_dve", "av_mm", "o_ready", "out_mm", "y_ready"))
        block = ctx.enter_context(nc.Block())

        def rows(engine, row):
            over_rows(engine, W, UNROLL, row)

        @block.sync
        def _(sp):
            def load(tile, i):
                at = bass.ds(TILE * tile, TILE)
                sp.dma_start(xt[:, i], x[:, at, :]).then_inc(loaded[i], 16)
                sp.dma_start(wt[:, i], ln_w[:, at, :]).then_inc(loaded[i], 16)
                sp.dma_start(bt[:, i], ln_b[:, at, :]).then_inc(loaded[i], 16)

            for i in range(BUFS):
                load(i, i)

            def body(t, first, last):
                for i in range(BUFS):
                    tile = BUFS * t + i
                    sp.wait_ge(y_ready, TILE * (tile + 1))
                    sp.dma_start(x1[:, bass.ds(TILE * tile, TILE), :], y[:, i % 2]).then_inc(y_stored[i % 2], 16)
                    if not last:
                        load(tile + BUFS, i)
            loop_ends_peeled(sp, W // UNROLL, body)
            for i in range(2):
                sp.wait_ge(y_stored[i], 16 * W // TILE // 2)

        @block.gpsimd
        def _(pool):
            def divide(t, k, h):
                n = NH0 * (UNROLL * t + k) + h
                pool.wait_ge(inv_ready, n + 1)
                pool.nop(nofuse=True)
                for c in range(KC):
                    last = nc.gpsimd.tensor_scalar(probs[:, h, c], probs[:, h, c], inv[:, h, c:c + 1], 1.0, ALU.mult, ALU.mult)
                last.then_inc(p_ready, 1)

            def normalise(t, k, part):
                r, kk, tt = UNROLL * t + k, k % UNROLL, t + k // UNROLL
                i, j, whole = kk // TILE, kk % TILE, xf[:, kk % 2]
                high, low = xn[0][:, kk % 4], xn[1][:, kk % 4]
                if part == 0:
                    if j == 0:
                        pool.wait_ge(loaded[i], 48 * (tt + 1))
                    nc.gpsimd.tensor_tensor(whole, xt[:, i, j], m.mean[:], ALU.subtract).then_inc(xn_step, 1)
                    return
                pool.wait_ge(xn_step, 5 * r + part)
                if part == 1:
                    nc.gpsimd.tensor_tensor(whole, whole, m.rstd[:], ALU.mult).then_inc(xn_step, 1)
                elif part == 2:
                    nc.gpsimd.tensor_tensor(whole, whole, wt[:, i, j], ALU.mult).then_inc(xn_step, 1)
                elif part == 3:
                    nc.gpsimd.tensor_tensor(whole, whole, bt[:, i, j], ALU.add).then_inc(xn_step, 1)
                elif part == 4:
                    wait(pool, s_mm, NH0 * (r - 3))
                    pool.nop(nofuse=True)
                    nc.gpsimd.tensor_scalar(high, whole, 1.0, 1.0, ALU.mult, ALU.mult).then_inc(xn_step, 1)
                else:
                    nc.gpsimd.tensor_tensor(low, whole, high.bitcast(F32), ALU.subtract).then_inc(xn_ready, 1)

            def row(t, k, has):
                if has(2):
                    normalise(t, k + 2, 3)
                if has(-1):
                    divide(t, k - 1, 1)
                if has(2):
                    normalise(t, k + 2, 4)
                    normalise(t, k + 2, 5)
                if has(-1):
                    divide(t, k - 1, 2)
                    divide(t, k - 1, 3)
                if has(3):
                    normalise(t, k + 3, 0)
                if has(0):
                    divide(t, k, 0)
                if has(3):
                    normalise(t, k + 3, 1)
                    normalise(t, k + 3, 2)
            rows(pool, row)

        @block.tensor
        def _(pe):
            def queries(t, k, half):
                r = UNROLL * t + k
                bank, done, free = ((b_qa, qa_mm, v_ready), (b_qb, qb_mm, g_ready))[half]
                pe.wait_ge(xn_ready, r + 1)
                wait(pe, free, r)
                for j in range(2):
                    last = matmul_split(nc, bank[:, j * W:(j + 1) * W], [w[:, 2 * half + j, :] for w in m.wqk], [x_[:, k % 4] for x_ in xn])
                last.then_inc(done, 1)

            def values(t, k):
                r = UNROLL * t + k
                pe.wait_ge(qa_ready, r + 1)
                for c in range(KC):
                    last = matmul_split(nc, b_qa[:, c * W:(c + 1) * W], [x_[:, k % 4, c * P:(c + 1) * P] for x_ in xn], [w[:] for w in m.wv_t])
                last.then_inc(v_mm, 1)

            def gates(t, k):
                r = UNROLL * t + k
                pe.wait_ge(qb_ready, r + 1)
                wait(pe, o_ready, r - 1)
                for c in range(HC):
                    last = matmul_split(nc, b_qb[:, c * W:(c + 1) * W], [w[:, c * P:(c + 1) * P] for w in m.wg_t], [x_[:, k % 4] for x_ in xn])
                last.then_inc(g_mm, 1)

            def scores(t, k, h):
                r = UNROLL * t + k
                n = NH0 * r + h
                pe.wait_ge(qa_ready if h < 2 else qb_ready, r + 1)
                wait(pe, s_ready, n - 1)
                for c in range(KC):
                    last = matmul_split(nc, b_s[h % 2][:, c * W:(c + 1) * W], [q[:, k % 2, h, c * P:(c + 1) * P] for q in qk], [x_[:, k % 4] for x_ in xn])
                last.then_inc(s_mm, 1)

            def transposes(t, k, h):
                r = UNROLL * t + k
                n = NH0 * r + h
                pe.wait_ge(p_ready, n + 1)
                wait(pe, (t_act, t_dve)[h % 2], 2 * r + h // 2)
                for kc in range(KC):
                    for qc in range(KC):
                        last = nc.tensor.transpose(b_t[h % 2][:, kc * W + qc * P:kc * W + (qc + 1) * P], probs[:, h, qc, kc * P:(kc + 1) * P], m.ident[:])
                last.then_inc(t_mm, 1)

            def attend(t, k, pair):
                r = UNROLL * t + k
                pe.wait_ge(t_act, 2 * r + pair + 1)
                pe.wait_ge(t_dve, 2 * r + pair + 1)
                pe.wait_ge(v_ready, r + 1)
                wait(pe, o_ready, r)
                for kc in range(KC):
                    for j in range(2):
                        h = 2 * pair + j
                        last = nc.tensor.matmul(b_av[D0 * j:D0 * (j + 1), pair * W:(pair + 1) * W], v[:, k % 2, kc, h * D0:(h + 1) * D0],
                                                probs_t[:, h, kc], start=kc == 0, stop=kc == KC - 1)
                last.then_inc(av_mm, 1)

            def project_out(t, k):
                r = UNROLL * t + k
                pe.wait_ge(o_ready, r + 1)
                wait(pe, y_ready, r)
                for c in range(HC):
                    last = nc.tensor.matmul(b_out[:, 0:W], m.wrep_t[:, c, :], o[:, k % 2, c], start=c == 0, stop=c == HC - 1)
                last.then_inc(out_mm, 1)

            def row(t, k, has):
                if has(1):
                    values(t, k + 1)
                    scores(t, k + 1, 0)
                if has(0):
                    transposes(t, k, 1)
                if has(1):
                    scores(t, k + 1, 1)
                    gates(t, k + 1)
                if has(2):
                    queries(t, k + 2, 0)
                if has(0):
                    transposes(t, k, 2)
                if has(1):
                    scores(t, k + 1, 2)
                if has(0):
                    attend(t, k, 0)
                    transposes(t, k, 3)
                if has(2):
                    queries(t, k + 2, 1)
                if has(1):
                    scores(t, k + 1, 3)
                if has(-1):
                    project_out(t, k - 1)
                if has(0):
                    attend(t, k, 1)
                if has(1):
                    transposes(t, k + 1, 0)
            rows(pe, row)

        @block.scalar
        def _(act):
            def exponents(t, k, h):
                n = NH0 * (UNROLL * t + k) + h
                act.wait_ge(s_ready, n + 1)
                for c in range(KC):
                    last = nc.scalar.activation(probs[:, h, c], probs[:, h, c], ACT.Exp, bias=neg_max[:, h, c:c + 1], scale=-1.0,
                                                accum_out=total[:, h, c:c + 1])
                last.then_inc(exp_ready, 1)

            def queries_high(t, k, half):
                r = UNROLL * t + k
                bank, done, high = ((b_qa, qa_mm, qa_high), (b_qb, qb_mm, qb_high))[half]
                act.wait_ge(done, r + 1)
                nc.scalar.activation(qk[0][:, k % 2, 2 * half:2 * half + 2], bank[:].rearrange("p (h c) -> p h c", h=2), ACT.Copy).then_inc(high, 1)

            def values_out(t, k):
                r = UNROLL * t + k
                act.wait_ge(v_mm, r + 1)
                nc.scalar.activation(v[:, k % 2], b_qa[:].rearrange("p (h c) -> p h c", h=2), ACT.Copy).then_inc(v_ready, 1)

            def gates_out(t, k):
                r = UNROLL * t + k
                act.wait_ge(g_mm, r + 1)
                for c in range(HC):
                    last = nc.scalar.activation(gate[:, k % 2, c], b_qb[:, c * W:(c + 1) * W], ACT.Tanh, bias=m.wg_b_half[:, c:c + 1], scale=0.5)
                last.then_inc(g_ready, 1)

            def transposed_out(t, k, h):
                n = NH0 * (UNROLL * t + k) + h
                act.wait_ge(t_mm, n + 1)
                nc.scalar.activation(probs_t[:, h], b_t[0][:].rearrange("p (a c) -> p a c", a=KC), ACT.Copy).then_inc(t_act, 1)

            def row(t, k, has):
                if has(1):
                    exponents(t, k + 1, 0)
                    gates_out(t, k + 1)
                if has(0):
                    transposed_out(t, k, 2)
                if has(2):
                    queries_high(t, k + 2, 0)
                if has(1):
                    exponents(t, k + 1, 1)
                    exponents(t, k + 1, 2)
                if has(2):
                    queries_high(t, k + 2, 1)
                if has(1):
                    exponents(t, k + 1, 3)
                if has(2):
                    values_out(t, k + 2)
                if has(1):
                    transposed_out(t, k + 1, 0)
            rows(act, row)

        @block.vector
        def _(dve):
            def biased(t, k, h):
                n = NH0 * (UNROLL * t + k) + h
                dve.wait_ge(s_mm, n + 1)
                dve.nop(nofuse=True)
                for c in range(KC):
                    last = nc.vector.tensor_tensor_reduce(out=probs[:, h, c], in0=b_s[h % 2][:, c * W:(c + 1) * W], in1=m.bias0[:, c, h], scale=-1.0,
                                                          scalar=3.0e38, op0=ALU.add, op1=ALU.min, accum_out=neg_max[:, h, c:c + 1])
                last.then_inc(s_ready, 1)

            def inverse(t, k, h):
                n = NH0 * (UNROLL * t + k) + h
                dve.wait_ge(exp_ready, n + 1)
                nc.vector.reciprocal(inv[:, h], total[:, h]).then_inc(inv_ready, 1)

            def queries_low(t, k, half):
                r = UNROLL * t + k
                bank, high, ready = ((b_qa, qa_high, qa_ready), (b_qb, qb_high, qb_ready))[half]
                at = (slice(None), k % 2, slice(2 * half, 2 * half + 2))
                dve.wait_ge(high, r + 1)
                nc.vector.tensor_tensor(qk[1][at], bank[:].rearrange("p (h c) -> p h c", h=2), qk[0][at].bitcast(F32), ALU.subtract).then_inc(ready, 1)

            def transposed_out(t, k, h):
                n = NH0 * (UNROLL * t + k) + h
                dve.wait_ge(t_mm, n + 1)
                nc.vector.tensor_copy(probs_t[:, h], b_t[1][:].rearrange("p (a c) -> p a c", a=KC)).then_inc(t_dve, 1)

            def gated(t, k):
                r = UNROLL * t + k
                dve.wait_ge(av_mm, 2 * r + 2)
                dve.wait_ge(g_ready, r + 1)
                nc.vector.scalar_tensor_tensor(out=o[:, k % 2], in0=gate[:, k % 2], scalar=1.0, in1=b_av[:].rearrange("p (a c) -> p a c", a=HC),
                                               op0=ALU.add, op1=ALU.mult).then_inc(o_ready, 1)

            def residual(t, k):
                r, kk = UNROLL * t + k, k % UNROLL
                tt = t + (k - kk) // UNROLL
                i, j = kk // TILE, kk % TILE
                dve.wait_ge(out_mm, r + 1)
                if j == 0:
                    wait(dve, y_stored[i % 2], 16 * (BUFS // 2 * tt + i // 2))
                nc.vector.scalar_tensor_tensor(out=y[:, i % 2, j], in0=b_out[:, 0:W], scalar=m.wrep_b[:], in1=xt[:, i, j],
                                               op0=ALU.add, op1=ALU.add).then_inc(y_ready, 1)

            def row(t, k, has):
                if has(1):
                    biased(t, k + 1, 2)
                if has(0):
                    transposed_out(t, k, 3)
                if has(2):
                    queries_low(t, k + 2, 0)
                if has(1):
                    inverse(t, k + 1, 1)
                    biased(t, k + 1, 3)
                    inverse(t, k + 1, 2)
                if has(2):
                    queries_low(t, k + 2, 1)
                if has(0):
                    gated(t, k)
                if has(-1):
                    residual(t, k - 1)
                if has(2):
                    biased(t, k + 2, 0)
                if has(1):
                    inverse(t, k + 1, 3)
                    transposed_out(t, k + 1, 1)
                if has(2):
                    biased(t, k + 2, 1)
                    inverse(t, k + 2, 0)
            rows(dve, row)


def layer1(nc, m, x1, out):
    UNROLL = 4
    BY_DVE = (3,)
    BY_POOL = (1, 3, 5, 7)
    STACK_DMAS = 5
    OUT_BEHIND = 2
    with ExitStack() as ctx:
        sem = lambda name: ctx.enter_context(nc.semaphore(f"l1_{name}"))
        sb = lambda name, shape, dt=F32: ctx.enter_context(nc.sbuf_tensor(f"l1_{name}", shape, dt))
        xt = sb("x", [P, UNROLL, KC, W])
        xf = sb("xf", [P, HC, W])
        xn = [sb("xn_high", [P, HC, W], F32R), sb("xn_low", [P, HC, W], F32R)]
        qk = [sb("qk_high", [P, 2, HC, W], F32R), sb("qk_low", [P, 2, HC, W], F32R)]
        stack = sb("stack", [3 * D1, 2, 4, 2, HC, W], F32R)
        probs = sb("probs", [P, 4, KC, W])
        probs_t = sb("probs_t", [P, NH1, KC, W])
        v = sb("v", [P, 2, KC, HC * P])
        gate = sb("gate", [P, 2, HC, W])
        o = sb("o", [P, HC, W])
        y = sb("y", [P, 2, KC, W])
        neg_max = sb("neg_max", [P, 4, KC])
        total = sb("total", [P, 4, KC])
        inv = sb("inv", [P, 4, KC])
        by_channel = sb("by_channel", [P, 2, HC])
        b_q = m.psum[0]
        b_k = m.psum[1]
        b_s, b_t, b_av = m.psum[2:5], m.psum[5:7], m.psum[7]
        S_BANK = (0, 1, 2, 0, 1, 2, 0, 1)
        S_BACK = (2, 2, 3, 3, 3, 3, 3, 3)
        loaded = [sem(f"loaded{i}") for i in range(UNROLL)]
        y_stored = [sem(f"y_stored{i}") for i in range(2)]
        stacked = [sem(f"stacked{i}") for i in range(2)]
        (stat_mm, stat_ready, x_mm, x_whole, x_high, x_ready, q_mm, k_mm, v_mm, g_mm, q_high, k_high, q_ready, k_ready, v_ready, g_ready,
         s_mm, max_ready, exp_ready, inv_ready, pool_step, p_dve, p_pool, t_mm, t_act, t_dve, av_mm, o_ready, out_mm,
         y_ready) = (sem(n) for n in (
            "stat_mm", "stat_ready", "x_mm", "x_whole", "x_high", "x_ready", "q_mm", "k_mm", "v_mm", "g_mm", "q_high", "k_high", "q_ready",
            "k_ready", "v_ready", "g_ready", "s_mm", "max_ready", "exp_ready", "inv_ready", "pool_step", "p_dve", "p_pool", "t_mm", "t_act",
            "t_dve", "av_mm", "o_ready", "out_mm", "y_ready"))
        block = ctx.enter_context(nc.Block())

        def count(s, h, heads):
            return len(heads) * s + len([g for g in heads if g <= h])

        BY_ACT = tuple(h for h in range(NH1) if h not in BY_DVE)
        NOT_POOL = tuple(h for h in range(NH1) if h not in BY_POOL)

        def wait_copied(engine, s, h):
            if h in BY_DVE:
                wait(engine, t_dve, count(s, h, BY_DVE))
            else:
                wait(engine, t_act, count(s, h, BY_ACT))

        def rows(engine, row):
            over_rows(engine, C0, UNROLL, row)

        @block.sync
        def _(sp):
            def load(s, i):
                sp.dma_start(xt[:, i], x1[bass.ds(s, 1)].rearrange("o (a p) c -> p (o a) c", p=P)).then_inc(loaded[i], 16)

            def lay_out(t, k):
                s = UNROLL * t + k
                wait(sp, s_mm, NH1 * (s - 1))
                sp.nop(nofuse=True)
                sp.wait_ge(q_ready, s + 1)
                sp.wait_ge(k_ready, s + 1)
                sp.nop(nofuse=True)
                flat = lambda ap: ap.bitcast(F32)

                def rows(part, what):
                    to = flat(stack[part * D1:(part + 1) * D1, k % 2])
                    return to.rearrange("p a w c t -> p a (w c t)") if what is None else to[:, :, what].rearrange("p a c t -> p a (c t)")

                def parts(which, what):
                    of = flat(qk[which][:])
                    return of.rearrange("p w c t -> p (w c t)") if what is None else of[:, what].rearrange("p c t -> p (c t)")

                for part, which, what in ((0, 0, None), (1, 1, 0), (1, 0, 1), (2, 0, 0), (2, 1, 1)):
                    sp.dma_start(rows(part, what), parts(which, what)).then_inc(stacked[k % 2], 16)

            for i in range(UNROLL):
                load(i, i)

            def store_and_load(t, k):
                s, i = UNROLL * t + k, k % UNROLL
                tt = t + (k - i) // UNROLL
                sp.wait_ge(y_ready, s + 1)
                sp.nop(nofuse=True)
                sp.dma_start(out[bass.ds(s, 1)].rearrange("o (a p) c -> p (o a) c", p=P), y[:, i % 2]).then_inc(y_stored[i % 2], 16)
                if not isinstance(s, int) or s + UNROLL < C0:
                    load(s + UNROLL, i)

            def row(t, k, has):
                if has(-1):
                    store_and_load(t, k - 1)
                if has(2):
                    lay_out(t, k + 2)
            rows(sp, row)
            for i in range(2):
                sp.wait_ge(y_stored[i], 16 * C0 // 2)

        @block.tensor
        def _(pe):
            def turn(t, k):
                s, i, tt = UNROLL * t + k, k % UNROLL, t + k // UNROLL
                pe.wait_ge(loaded[i], 16 * (tt + 1))
                wait(pe, v_ready, s)
                for c in range(HC):
                    for a in range(KC):
                        last = nc.tensor.transpose(b_q[:, c * W + a * P:c * W + (a + 1) * P], xt[:, i, a, c * P:(c + 1) * P], m.ident[:])
                last.then_inc(x_mm, 1)

            def by_weights(bank, weights):
                for j in range(HC):
                    for c in range(HC):
                        last = matmul_split(nc, bank[:, j * W:(j + 1) * W], [weights(part, c, j) for part in range(2)], [x_[:, c] for x_ in xn],
                                            start=c == 0, stop=c == HC - 1)
                return last

            def queries(t, k):
                s = UNROLL * t + k
                pe.wait_ge(x_ready, s + 1)
                by_weights(b_q, lambda part, c, j: m.w_qk1[part][:, c, 0, j]).then_inc(q_mm, 1)

            def keys(t, k):
                s = UNROLL * t + k
                wait(pe, g_ready, s)
                wait(pe, y_ready, s - OUT_BEHIND)
                by_weights(b_k, lambda part, c, j: m.w_qk1[part][:, c, 1, j]).then_inc(k_mm, 1)

            def values(t, k):
                s = UNROLL * t + k
                pe.wait_ge(q_ready, s + 1)
                for a in range(KC):
                    for c in range(HC):
                        last = matmul_split(nc, b_q[:, a * W:(a + 1) * W], [x_[:, c, a * P:(a + 1) * P] for x_ in xn], [w[:, c] for w in m.w_v1],
                                            start=c == 0, stop=c == HC - 1)
                last.then_inc(v_mm, 1)

            def gates(t, k):
                s = UNROLL * t + k
                pe.wait_ge(k_ready, s + 1)
                wait(pe, o_ready, s - 1)
                by_weights(b_k, lambda part, c, j: m.w_gate1[part][:, c, j * P:(j + 1) * P]).then_inc(g_mm, 1)

            def scores(t, k, h):
                n = NH1 * (UNROLL * t + k) + h
                if h == 0:
                    pe.wait_ge(stacked[k % 2], 16 * STACK_DMAS * (UNROLL // 2 * t + k // 2 + 1))
                wait(pe, exp_ready, n + 1 - S_BACK[h])
                for c in range(KC):
                    last = nc.tensor.matmul(b_s[S_BANK[h]][:, c * W:(c + 1) * W], stack[:, k % 2, h % 4, 0, h // 4, c * P:(c + 1) * P],
                                            stack[:, k % 2, h % 4, 1, h // 4], start=True, stop=True)
                last.then_inc(s_mm, 1)

            def transposes(t, k, h):
                s = UNROLL * t + k
                if h in BY_POOL:
                    pe.wait_ge(p_pool, count(s, h, BY_POOL))
                else:
                    pe.wait_ge(p_dve, count(s, h, NOT_POOL))
                if h >= 2:
                    wait_copied(pe, s, h - 2)
                else:
                    wait_copied(pe, s - 1, h + NH1 - 2)
                for kc in range(KC):
                    for qc in range(KC):
                        last = nc.tensor.transpose(b_t[h % 2][:, kc * W + qc * P:kc * W + (qc + 1) * P], probs[:, h % 4, qc, kc * P:(kc + 1) * P], m.ident[:])
                last.then_inc(t_mm, 1)

            def attend(t, k, half):
                s = UNROLL * t + k
                pe.wait_ge(t_act, count(s, 4 * half + 3, BY_ACT))
                pe.wait_ge(t_dve, count(s, 4 * half + 3, BY_DVE))
                pe.wait_ge(v_ready, s + 1)
                wait(pe, o_ready, s)
                for kc in range(KC):
                    for j in range(4):
                        h = 4 * half + j
                        last = nc.tensor.matmul(b_av[D1 * j:D1 * (j + 1), half * W:(half + 1) * W], v[:, k % 2, kc, h * D1:(h + 1) * D1],
                                                probs_t[:, h, kc], start=kc == 0, stop=kc == KC - 1, tile_position=(0, D1 * j))
                last.then_inc(av_mm, 1)

            def project_out(t, k):
                s = UNROLL * t + k
                gates_before = s + OUT_BEHIND + 1
                pe.wait_ge(o_ready, s + 1)
                pe.wait_ge(g_ready, min(gates_before, C0) if isinstance(s, int) else gates_before)
                for a in range(KC):
                    for c in range(HC):
                        last = nc.tensor.matmul(b_k[:, a * W:(a + 1) * W], o[:, c, a * P:(a + 1) * P], m.w_out1[:, c], start=c == 0, stop=c == HC - 1)
                last.then_inc(out_mm, 1)

            for c in range(HC):
                nc.tensor.transpose(b_q[:, c * P:(c + 1) * P], m.mean[:, c * P:(c + 1) * P], m.ident[:])
                last = nc.tensor.transpose(b_k[:, c * P:(c + 1) * P], m.rstd[:, c * P:(c + 1) * P], m.ident[:])
            last.then_inc(stat_mm, 1)
            pe.wait_ge(stat_ready, 1)
            def row(t, k, has):
                if has(0):
                    scores(t, k, 4)
                if has(-1):
                    attend(t, k - 1, 1)
                if has(0):
                    transposes(t, k, 1)
                    scores(t, k, 5)
                if has(1):
                    values(t, k + 1)
                if has(0):
                    transposes(t, k, 2)
                    scores(t, k, 6)
                if has(1):
                    gates(t, k + 1)
                if has(2):
                    turn(t, k + 2)
                if has(0):
                    transposes(t, k, 3)
                    scores(t, k, 7)
                    transposes(t, k, 4)
                if has(1):
                    scores(t, k + 1, 0)
                if has(-1):
                    project_out(t, k - 1)
                if has(0):
                    transposes(t, k, 5)
                if has(1):
                    scores(t, k + 1, 1)
                if has(0):
                    transposes(t, k, 6)
                if has(2):
                    queries(t, k + 2)
                if has(1):
                    scores(t, k + 1, 2)
                if has(2):
                    keys(t, k + 2)
                if has(0):
                    transposes(t, k, 7)
                if has(1):
                    scores(t, k + 1, 3)
                if has(0):
                    attend(t, k, 0)
                if has(1):
                    transposes(t, k + 1, 0)
            rows(pe, row)

        @block.scalar
        def _(act):
            def exponents(t, k, h):
                n = NH1 * (UNROLL * t + k) + h
                act.wait_ge(max_ready, n + 1)
                for c in range(KC):
                    last = nc.scalar.activation(probs[:, h % 4, c], b_s[S_BANK[h]][:, c * W:(c + 1) * W], ACT.Exp, bias=neg_max[:, h % 4, c:c + 1],
                                                accum_out=total[:, h % 4, c:c + 1])
                last.then_inc(exp_ready, 1)

            def x_high_part(t, k):
                s = UNROLL * t + k
                wait(act, g_mm, s)
                act.wait_ge(x_whole, s + 1)
                nc.scalar.activation(xn[0][:], xf[:], ACT.Copy).then_inc(x_high, 1)

            def high(t, k, what):
                s = UNROLL * t + k
                bank, done, mine = ((b_q, q_mm, q_high), (b_k, k_mm, k_high))[what]
                act.wait_ge(done, s + 1)
                wait(act, stacked[(k - 1) % 2], 16 * STACK_DMAS * (UNROLL // 2 * t + (k + 1) // 2))
                nc.scalar.activation(qk[0][:, what], bank[:].rearrange("p (a c) -> p a c", a=HC), ACT.Copy).then_inc(mine, 1)

            def values_out(t, k):
                s = UNROLL * t + k
                act.wait_ge(v_mm, s + 1)
                nc.scalar.activation(v[:, k % 2], b_q[:].rearrange("p (a c) -> p a c", a=KC), ACT.Copy).then_inc(v_ready, 1)

            def gates_out(t, k):
                s = UNROLL * t + k
                act.wait_ge(g_mm, s + 1)
                nc.scalar.activation(gate[:, k % 2], b_k[:].rearrange("p (a c) -> p a c", a=HC), ACT.Tanh, scale=0.5).then_inc(g_ready, 1)

            def transposed_out(t, k, h):
                n = NH1 * (UNROLL * t + k) + h
                act.wait_ge(t_mm, n + 1)
                nc.scalar.activation(probs_t[:, h], b_t[h % 2][:].rearrange("p (a c) -> p a c", a=KC), ACT.Copy).then_inc(t_act, 1)

            def row(t, k, has):
                if has(0):
                    exponents(t, k, 5)
                    transposed_out(t, k, 2)
                    exponents(t, k, 6)
                if has(1):
                    gates_out(t, k + 1)
                if has(2):
                    x_high_part(t, k + 2)
                if has(0):
                    exponents(t, k, 7)
                    transposed_out(t, k, 4)
                if has(1):
                    exponents(t, k + 1, 0)
                if has(0):
                    transposed_out(t, k, 5)
                if has(1):
                    exponents(t, k + 1, 1)
                if has(0):
                    transposed_out(t, k, 6)
                if has(2):
                    high(t, k + 2, 0)
                    high(t, k + 2, 1)
                if has(0):
                    transposed_out(t, k, 7)
                if has(1):
                    exponents(t, k + 1, 2)
                    exponents(t, k + 1, 3)
                    transposed_out(t, k + 1, 0)
                    exponents(t, k + 1, 4)
                    transposed_out(t, k + 1, 1)
                if has(2):
                    values_out(t, k + 2)
            rows(act, row)

        @block.vector
        def _(dve):
            def maxima(t, k, h):
                n = NH1 * (UNROLL * t + k) + h
                dve.wait_ge(s_mm, n + 1)
                nc.vector.tensor_reduce(neg_max[:, h % 4], b_s[S_BANK[h]][:].rearrange("p (a c) -> p a c", a=KC), AX.X, ALU.max, negate=True).then_inc(max_ready, 1)

            def inverse(t, k, h):
                n = NH1 * (UNROLL * t + k) + h
                dve.wait_ge(exp_ready, n + 1)
                nc.vector.reciprocal(inv[:, h % 4], total[:, h % 4]).then_inc(inv_ready, 1)

            def divide(t, k, h):
                n = NH1 * (UNROLL * t + k) + h
                dve.wait_ge(inv_ready, n + 1)
                for c in range(KC):
                    last = nc.vector.scalar_tensor_tensor(out=probs[:, h % 4, c], in0=probs[:, h % 4, c], scalar=inv[:, h % 4, c:c + 1], in1=m.bias1[:, c, h],
                                                          op0=ALU.mult, op1=ALU.add)
                last.then_inc(p_dve, 1)

            def transposed_out(t, k, h):
                n = NH1 * (UNROLL * t + k) + h
                dve.wait_ge(t_mm, n + 1)
                nc.vector.tensor_copy(probs_t[:, h], b_t[h % 2][:].rearrange("p (a c) -> p a c", a=KC)).then_inc(t_dve, 1)

            def group_norm(t, k):
                s = UNROLL * t + k
                dve.wait_ge(x_mm, s + 1)
                for c in range(HC):
                    last = nc.vector.tensor_scalar(xf[:, c], b_q[:, c * W:(c + 1) * W], by_channel[:, 0, c:c + 1], by_channel[:, 1, c:c + 1],
                                                   ALU.subtract, ALU.mult)
                last.then_inc(x_whole, 1)

            def low(t, k, what):
                s = UNROLL * t + k
                bank, high, ready = ((b_q, q_high, q_ready), (b_k, k_high, k_ready))[what]
                dve.wait_ge(high, s + 1)
                nc.vector.tensor_tensor(qk[1][:, what], bank[:].rearrange("p (a c) -> p a c", a=HC), qk[0][:, what].bitcast(F32), ALU.subtract).then_inc(ready, 1)

            def gated(t, k):
                s = UNROLL * t + k
                dve.wait_ge(av_mm, 2 * s + 2)
                dve.wait_ge(g_ready, s + 1)
                wait(dve, out_mm, s)
                nc.vector.scalar_tensor_tensor(out=o[:], in0=gate[:, k % 2], scalar=1.0, in1=b_av[:].rearrange("p (a c) -> p a c", a=HC),
                                               op0=ALU.add, op1=ALU.mult).then_inc(o_ready, 1)

            def residual(t, k):
                s, i = UNROLL * t + k, k % UNROLL
                tt = t + (k - i) // UNROLL
                dve.wait_ge(out_mm, s + 1)
                wait(dve, y_stored[i % 2], 16 * (UNROLL // 2 * tt + i // 2))
                nc.vector.tensor_tensor(y[:, i % 2], b_k[:].rearrange("p (a c) -> p a c", a=KC), xt[:, i], ALU.add).then_inc(y_ready, 1)

            dve.wait_ge(stat_mm, 1)
            nc.vector.tensor_copy(by_channel[:, 0], b_q[:, 0:HC * P].rearrange("p (c n) -> p c n", n=P)[:, :, 0])
            nc.vector.tensor_copy(by_channel[:, 1], b_k[:, 0:HC * P].rearrange("p (c n) -> p c n", n=P)[:, :, 0]).then_inc(stat_ready, 1)
            dve.wait_ge(stat_ready, 1)
            def row(t, k, has):
                if has(0):
                    inverse(t, k, 0)
                    maxima(t, k, 2)
                    inverse(t, k, 1)
                    divide(t, k, 0)
                if has(1):
                    low(t, k + 1, 0)
                if has(0):
                    maxima(t, k, 3)
                if has(1):
                    low(t, k + 1, 1)
                if has(0):
                    maxima(t, k, 4)
                    inverse(t, k, 2)
                    divide(t, k, 2)
                    inverse(t, k, 3)
                if has(-1):
                    gated(t, k - 1)
                if has(0):
                    maxima(t, k, 5)
                    inverse(t, k, 4)
                    divide(t, k, 4)
                    maxima(t, k, 6)
                    inverse(t, k, 5)
                if has(2):
                    group_norm(t, k + 2)
                if has(0):
                    maxima(t, k, 7)
                    transposed_out(t, k, 3)
                    inverse(t, k, 6)
                    divide(t, k, 6)
                if has(1):
                    maxima(t, k + 1, 0)
                if has(0):
                    inverse(t, k, 7)
                if has(-1):
                    residual(t, k - 1)
                if has(1):
                    maxima(t, k + 1, 1)
            rows(dve, row)

        @block.gpsimd
        def _(pool):
            def x_low_part(t, k):
                s = UNROLL * t + k
                pool.wait_ge(x_high, s + 1)
                nc.gpsimd.tensor_tensor(xn[1][:], xf[:], xn[0][:].bitcast(F32), ALU.subtract).then_inc(x_ready, 1)

            def divide(t, k, h):
                s = UNROLL * t + k
                n = NH1 * s + h
                pool.wait_ge(inv_ready, n + 1)
                pool.nop(nofuse=True)
                for c in range(KC):
                    last = nc.gpsimd.tensor_scalar(probs[:, h % 4, c], probs[:, h % 4, c], inv[:, h % 4, c:c + 1], 1.0, ALU.mult, ALU.mult)
                last.then_inc(pool_step, 1)
                pool.wait_ge(pool_step, count(s, h, BY_POOL))
                nc.gpsimd.tensor_tensor(probs[:, h % 4], probs[:, h % 4], m.bias1[:, :, h], ALU.add).then_inc(p_pool, 1)

            def row(t, k, has):
                if has(0):
                    divide(t, k, 3)
                    divide(t, k, 5)
                if has(2):
                    x_low_part(t, k + 2)
                if has(0):
                    divide(t, k, 7)
                if has(1):
                    divide(t, k + 1, 1)
            rows(pool, row)


class Memory:
    pass


def build(nc, x, ln_w, ln_b, wq, wk, wv, wb, wg_w, wg_b, wrep_w, wrep_b, pair_repr, gate_proj, qkv_proj, out_proj, bias_proj, out):
    m = Memory()
    with ExitStack() as ctx:
        sb = lambda name, shape: ctx.enter_context(nc.sbuf_tensor(name, shape, F32))
        m.psum = [ctx.enter_context(nc.psum_tensor(f"bank{i}", [P, 512], F32)) for i in range(8)]
        m.ident = sb("ident", [P, P])
        m.averager = sb("averager", [P, P])

        def pair(name, shape):
            return [ctx.enter_context(nc.sbuf_tensor(f"{name}_{part}", shape, F32R)) for part in ("high", "low")]

        m.wqk = pair("wqk", [C0, NH0, C0])
        m.wv_t = pair("wv_t", [C0, 256])
        m.wg_t = pair("wg_t", [C0, 256])
        m.wrep_t = sb("wrep_t", [P, HC, C0])
        m.wb_t = sb("wb_t", [C0, 32])
        m.wg_b_half = sb("wg_b_half", [P, HC])
        m.wrep_b = sb("wrep_b", [C0, 1])
        m.w_pair = sb("w_pair", [P, 32])
        m.w_qk1 = pair("w_qk1", [P, HC, 2, HC, P])
        m.w_v1 = pair("w_v1", [P, HC, 256])
        m.w_gate1 = pair("w_gate1", [P, HC, 256])
        m.w_out1 = sb("w_out1", [P, HC, 256])
        m.bias0 = sb("bias0", [P, KC, NH0, W])
        m.bias1 = sb("bias1", [P, KC, NH1, W])
        m.mean = sb("mean", [P, W])
        m.rstd = sb("rstd", [P, W])
        image_bias = nc.dram_tensor("image_bias", (NH0, W, W), F32).ap()
        pair_bias = nc.dram_tensor("pair_bias", (NH1, W, W), F32).ap()
        x1 = nc.dram_tensor("x1", (C0, W, W), F32).ap()
        x, pair_repr, out = x[0], pair_repr[0], out[0]
        args = {"wq": wq, "wk": wk, "wv": wv, "wg_w": wg_w, "wrep_w": wrep_w, "wg_b": wg_b, "wrep_b": wrep_b, "gate_proj": gate_proj,
                "qkv_proj": qkv_proj, "out_proj": out_proj, "wb": wb, "bias_proj": bias_proj}
        prepare_weights(nc, m, args)
        with nc.sbuf_tensor("stage", [P, 6 * ROWS_B * W], F32) as stage:
            m.stage = stage
            group_statistics(nc, m, "gs0", x, True)
            project_image_bias(nc, m, x, ln_w, ln_b, image_bias)
            project_pair_bias(nc, m, pair_repr, pair_bias)
        layer0(nc, m, x, ln_w, ln_b, x1)
        with nc.sbuf_tensor("stage1", [P, 4 * ROWS_B * W], F32) as stage:
            m.stage = stage
            group_statistics(nc, m, "gs1", x1, False)
        layer1(nc, m, x1, out)


_INS = ["x", "L0_conv_ln_w", "L0_conv_ln_b", "L0_conv_wq", "L0_conv_wk", "L0_conv_wv", "L0_conv_wb", "L0_conv_wg_w", "L0_conv_wg_b",
        "L0_conv_wrep_w", "L0_conv_wrep_b", "L1_conv_pair_repr", "L1_conv_gate_proj", "L1_conv_qkv_proj", "L1_conv_out_proj", "L1_conv_bias_proj"]


def kernel(**inputs):
    import numpy as _np
    import concourse.bacc as _bacc
    from concourse import mybir as _mybir
    from concourse.bass_utils import run_bass_kernel_spmd as _run

    nc = _bacc.Bacc("TRN2", target_bir_lowering=False, num_devices=1)
    arrays, args = {}, []
    for name in _INS:
        a = _np.ascontiguousarray(inputs[name])
        arrays[f"in_{name}_dram"] = a
        args.append(nc.dram_tensor(f"in_{name}_dram", a.shape, _mybir.dt.from_np(a.dtype), kind="ExternalInput").ap())
    args.append(nc.dram_tensor("out_dram", (1, 128, 256, 256), _mybir.dt.from_np(_np.dtype("float32")), kind="ExternalOutput").ap())
    build(nc, *args)
    r = _run(nc, [arrays], core_ids=[0])
    return r.results[0]["out_dram"]
```

```python
import concourse.bass as bass
from concourse import mybir
from contextlib import ExitStack

F32 = mybir.dt.float32
F32R = mybir.dt.float32r
ALU = mybir.AluOpType
ACT = mybir.ActivationFunctionType
AX = mybir.AxisListType

P = 128
C0 = 128
W = 256
KC = W // P
GROUP = 8
NG = W // GROUP
NH0, D0 = 4, 64
NH1, D1 = 8, 32
EPS = 1e-5
HC = 2


MOST_AHEAD = 3


def wait(engine, sem, value):
    if not (isinstance(value, int) and value <= 0):
        engine.wait_ge(sem, value)


def loop_first_peeled(engine, count, body):
    body(0)
    with engine.Fori(1, count) as t:
        body(t)


def loop_ends_peeled(engine, count, body):
    body(0, True, False)
    with engine.Fori(1, count - 1) as t:
        body(t, False, False)
    body(count - 1, False, True)


def over_rows(engine, total, unroll, row):
    def body(t, first, last):
        for k in range(-MOST_AHEAD if first else 0, unroll + 1 if last else unroll):
            row(t, k, lambda d, k=k: (not first or k + d >= 0) and (not last or k + d < unroll))
    loop_ends_peeled(engine, total // unroll, body)


class Chain:

    def __init__(self, engine, sem):
        self.engine, self.sem, self.count = engine, sem, 0

    def __call__(self, instruction):
        self.count += 1
        instruction.then_inc(self.sem, 1)
        self.engine.wait_ge(self.sem, self.count)


def matmul_split(nc, out, left, right, start=True, stop=True):
    (lh, ll), (rh, rl) = left, right
    nc.tensor.matmul(out, lh, rh, start=start, stop=False)
    nc.tensor.matmul(out, lh, rl, start=False, stop=False)
    return nc.tensor.matmul(out, ll, rh, start=False, stop=stop)


def prepare_weights(nc, m, a, load_first_tiles):
    with ExitStack() as ctx:
        sem = lambda name: ctx.enter_context(nc.semaphore(name))
        sb = lambda name, shape: ctx.enter_context(nc.sbuf_tensor(name, shape, F32))
        wq = sb("wq_raw", [P, HC, C0])
        wk = sb("wk_raw", [P, HC, C0])
        wv = sb("wv_raw", [P, HC, C0])
        wg = sb("wg_raw", [P, HC, C0])
        wrep = sb("wrep_raw", [C0, D0, NH0])
        wrep_h = sb("wrep_by_head", [C0, NH0, D0])
        wb = sb("wb_raw", [32, C0])
        wgb = sb("wgb_raw", [P, HC])
        w_gate1, w_qkv1, w_out1 = sb("gate1_raw", [P, HC, 256]), sb("qkv1_raw", [P, HC, 768]), sb("out1_raw", [P, HC, 256])
        wqk1 = sb("qk1_permuted", [P, HC, 2, HC, P])
        wqk, wv_t, wg_t = sb("wqk_whole", [C0, 2, HC, P]), sb("wv_t_whole", [C0, 256]), sb("wg_t_whole", [C0, 256])
        wrep_t, wout1 = sb("wrep_t_whole", [P, HC, C0]), sb("out1_half", [P, HC, 256])
        loaded, zeroed, ident_step, ident_ready = sem("w_loaded"), sem("w_zeroed"), sem("ident_step"), sem("ident_ready")
        permuted, turned, step = sem("w_permuted"), sem("w_turned"), sem("w_step")
        wb_loaded = sem("wb_loaded")
        LOADS = 11
        block = ctx.enter_context(nc.Block())

        @block.sync
        def _(sp):
            sp.dma_start(wq[:], a["wq"].rearrange("(a p) c -> p a c", p=P)).then_inc(loaded, 16)
            sp.dma_start(wk[:], a["wk"].rearrange("(a p) c -> p a c", p=P)).then_inc(loaded, 16)
            sp.dma_start(wv[:], a["wv"].rearrange("(a p) c -> p a c", p=P)).then_inc(loaded, 16)
            sp.dma_start(wg[:], a["wg_w"].rearrange("(a p) c -> p a c", p=P)).then_inc(loaded, 16)
            sp.dma_start(wrep[:], a["wrep_w"].rearrange("o (c h) -> o c h", h=NH0)).then_inc(loaded, 16)
            for c in range(HC):
                sp.dma_start(wgb[:, c:c + 1], a["wg_b"][c * P:(c + 1) * P].rearrange("(p a) -> p a", a=1)).then_inc(loaded, 16)
            sp.dma_start(m.wrep_b[:], a["wrep_b"].rearrange("(p a) -> p a", a=1)).then_inc(loaded, 16)
            sp.dma_start(w_gate1[:], a["gate_proj"].rearrange("(a p) n -> p a n", p=P)).then_inc(loaded, 16)
            sp.dma_start(w_qkv1[:], a["qkv_proj"].rearrange("(a p) n -> p a n", p=P)).then_inc(loaded, 16)
            sp.dma_start(w_out1[:], a["out_proj"].rearrange("(a p) n -> p a n", p=P)).then_inc(loaded, 16)
            sp.wait_ge(zeroed, 1)
            sp.dma_start(wb[0:NH0, :], a["wb"]).then_inc(wb_loaded, 16)
            sp.dma_start(m.w_pair[:, 0:NH1], a["bias_proj"]).then_inc(wb_loaded, 16)
            load_first_tiles(sp)
            sp.wait_ge(loaded, 16 * LOADS)
            sp.wait_ge(wb_loaded, 32)

        @block.gpsimd
        def _(pool):
            nc.gpsimd.memset(m.ident[:], 0.0).then_inc(ident_step, 1)
            pool.wait_ge(ident_step, 1)
            nc.gpsimd.affine_select(out=m.ident[:], in_=m.ident[:], compare_op=ALU.not_equal, fill=1.0, base=0,
                                    pattern=[[-1, P]], channel_multiplier=1).then_inc(ident_ready, 1)

        @block.vector
        def _(dve):
            nc.vector.memset(wb[:], 0.0)
            nc.vector.memset(m.w_pair[:], 0.0).then_inc(zeroed, 1)
            nc.vector.memset(m.averager[:], 1.0 / P)
            dve.wait_ge(loaded, 16 * LOADS)
            nc.vector.tensor_copy(wrep_h[:], wrep[:].rearrange("o c h -> o h c")).then_inc(permuted, 1)
            chain = Chain(dve, step)

            def split(parts, whole):
                chain(nc.vector.tensor_copy(parts[0][:], whole))
                chain(nc.vector.tensor_tensor(parts[1][:], whole, parts[0][:].bitcast(F32), ALU.subtract))

            nc.vector.tensor_scalar(m.wg_b_half[:], wgb[:], 0.5, None, ALU.mult)
            for c in range(HC):
                for j in range(HC):
                    columns = lambda at: w_qkv1[:, c, at + j * P:at + (j + 1) * P].rearrange("p (a d) -> p d a", d=D1)
                    nc.vector.tensor_scalar(wqk1[:, c, 0, j].rearrange("p (d a) -> p d a", d=D1), columns(0), D1 ** -0.5, None, ALU.mult)
                    nc.vector.tensor_copy(wqk1[:, c, 1, j].rearrange("p (d a) -> p d a", d=D1), columns(256))
            chain(nc.vector.tensor_scalar(wout1[:], w_out1[:], 0.5, None, ALU.mult))
            split(m.w_out1, wout1[:])
            split(m.w_qk1, wqk1[:])
            split(m.w_v1, w_qkv1[:, :, 512:768])
            split(m.w_gate1, w_gate1[:])
            dve.wait_ge(turned, 1)
            for c in range(HC):
                columns = lambda at: m.psum[0][:, at + c * P:at + (c + 1) * P].rearrange("p (a d) -> p d a", d=D0)
                nc.vector.tensor_scalar(wqk[:, 0, c].rearrange("p (d a) -> p d a", d=D0), columns(0), D0 ** -0.5, None, ALU.mult)
                nc.vector.tensor_copy(wqk[:, 1, c].rearrange("p (d a) -> p d a", d=D0), columns(256))
            nc.vector.tensor_copy(wv_t[:], m.psum[1][:, 0:256])
            nc.vector.tensor_copy(wg_t[:], m.psum[1][:, 256:512])
            nc.vector.tensor_scalar(wrep_t[:], m.psum[2][:, 0:256].rearrange("p (a o) -> p a o", a=HC), 0.5, None, ALU.mult)
            chain(nc.vector.tensor_copy(m.wb_t[:], m.psum[2][:, 256:288]))
            split(m.wqk, wqk[:])
            split(m.wv_t, wv_t[:])
            split(m.wg_t, wg_t[:])
            split(m.wrep_t, wrep_t[:])

        @block.tensor
        def _(pe):
            pe.wait_ge(loaded, 16 * LOADS)
            pe.wait_ge(ident_ready, 1)
            pe.wait_ge(permuted, 1)
            pe.wait_ge(wb_loaded, 32)
            for c in range(HC):
                nc.tensor.transpose(m.psum[0][:, c * P:(c + 1) * P], wq[:, c, :], m.ident[:])
                nc.tensor.transpose(m.psum[0][:, 256 + c * P:256 + (c + 1) * P], wk[:, c, :], m.ident[:])
                nc.tensor.transpose(m.psum[1][:, c * P:(c + 1) * P], wv[:, c, :], m.ident[:])
                nc.tensor.transpose(m.psum[1][:, 256 + c * P:256 + (c + 1) * P], wg[:, c, :], m.ident[:])
                nc.tensor.transpose(m.psum[2][:, c * P:(c + 1) * P],
                                    wrep_h[:, 2 * c:2 * c + 2, :].rearrange("o h d -> o (h d)"), m.ident[:])
            nc.tensor.transpose(m.psum[2][:, 256:288], wb[:], m.ident[0:32, 0:32]).then_inc(turned, 1)


TILE_ROWS = 8


class ImageTiles:

    def __init__(self, nc, ctx, x, ln_w, ln_b):
        sources = {"x": x, "ln_w": ln_w, "ln_b": ln_b}
        self.buffers = {name: [ctx.enter_context(nc.sbuf_tensor(f"fp_{name}{i}", [P, TILE_ROWS, W], F32)) for i in range(2)] for name in sources}
        self.loaded = [ctx.enter_context(nc.semaphore(f"fp_loaded{i}")) for i in range(2)]
        self.sources = sources

    def load(self, sp, tile, i):
        for name, source in self.sources.items():
            sp.dma_start(self.buffers[name][i][:], source[:, bass.ds(TILE_ROWS * tile, TILE_ROWS), :]).then_inc(self.loaded[i], 16)


def first_pass(nc, m, image, pair, image_parts, pair_bias, stats):
    ROWS, TILES = TILE_ROWS, W // TILE_ROWS
    PAIRS = ROWS // 2
    STORES = 2 * PAIRS
    X_PART, W_PART, B_PART, PAIR_PART = range(4)
    with ExitStack() as ctx:
        sem = lambda name: ctx.enter_context(nc.semaphore(f"fp_{name}"))
        sb = lambda name, shape: [ctx.enter_context(nc.sbuf_tensor(f"fp_{name}{i}", shape, F32)) for i in range(2)]
        xt, wt, bt = (image.buffers[name] for name in ("x", "ln_w", "ln_b"))
        loaded = image.loaded
        raw = sb("pair", [P, ROWS, 2, P])
        turned = sb("pair_t", [P, ROWS, W])
        evac = sb("evac", [P, 4, 2 * W])
        pair_loaded, stored = ([sem(f"{name}{i}") for i in range(2)] for name in ("pair_loaded", "stored"))
        measured, weighted, transposed, copied_act, copied_dve, evacuated = (sem(n) for n in (
            "measured", "weighted", "transposed", "copied_act", "copied_dve", "evacuated"))
        projected = [sem(f"projected_{part}") for part in ("x", "w", "b", "pair")]
        bank = lambda j: m.psum[4 + j]
        block = ctx.enter_context(nc.Block())

        @block.sync
        def _(sp):
            def load_pair(tile, i):
                wait(sp, transposed, PAIRS * (tile - 1))
                sp.dma_start(raw[i][:], pair[bass.ds(ROWS * tile, ROWS)].rearrange("q (p e) z -> p q e z", e=2)).then_inc(pair_loaded[i], 16)

            def load(tile, i):
                for part in (X_PART, W_PART, B_PART):
                    wait(sp, projected[part], tile - 1)
                image.load(sp, tile, i)
                load_pair(tile, i)

            def store(tile, i):
                sp.wait_ge(evacuated, tile + 1)
                for c in range(PAIRS):
                    rows, mine = bass.ds(ROWS * tile + 2 * c, 2), evac[i][32 * c:32 * c + NH1]
                    sp.dma_start(image_parts[:, :, rows, :].rearrange("s h r k -> h s (r k)"), mine[0:NH0, 0:3]).then_inc(stored[i], 16)
                    sp.dma_start(pair_bias[:, rows, :].rearrange("h r k -> h (r k)"), mine[:, PAIR_PART]).then_inc(stored[i], 16)

            load_pair(0, 0)
            load_pair(1, 1)

            def body(t, first, last):
                for i in range(2):
                    if not last:
                        load(2 * t + i + 2, i)
                    store(2 * t + i, i)
            loop_ends_peeled(sp, TILES // 2, body)
            for i in range(2):
                sp.wait_ge(stored[i], 16 * STORES * TILES // 2)

        @block.tensor
        def _(pe):
            def project(part, tile, weights, rows):
                wait(pe, evacuated, tile)
                for c in range(PAIRS):
                    last = nc.tensor.matmul(m.psum[part][32 * c:32 * c + 32, :], weights, rows[:, 2 * c:2 * c + 2, :].rearrange("p r k -> p (r k)"),
                                            start=True, stop=True, tile_position=(0, 32 * c))
                last.then_inc(projected[part], 1)

            def body(t):
                for i in range(2):
                    tile = 2 * t + i
                    pe.wait_ge(pair_loaded[i], 16 * (t + 1))
                    for j in range(PAIRS):
                        wait(pe, copied_act if j % 2 == 0 else copied_dve, PAIRS // 2 * (tile - 1) + j // 2 + 1)
                        for r in range(2):
                            for e in range(2):
                                last = nc.tensor.transpose(bank(j)[:, (2 * r + e) * P:(2 * r + e + 1) * P], raw[i][:, 2 * j + r, e, :], m.ident[:])
                        last.then_inc(transposed, 1)
                    pe.wait_ge(loaded[i], 48 * (t + 1))
                    project(W_PART, tile, m.wb_t[:], wt[i])
                    project(B_PART, tile, m.wb_t[:], bt[i])
                    pe.wait_ge(copied_act, PAIRS // 2 * (tile + 1))
                    pe.wait_ge(copied_dve, PAIRS // 2 * (tile + 1))
                    project(PAIR_PART, tile, m.w_pair[:], turned[i])
                    pe.wait_ge(weighted, tile + 1)
                    project(X_PART, tile, m.wb_t[:], xt[i])
            loop_first_peeled(pe, TILES // 2, body)

        def copy_turned(copy, i, j):
            return copy(turned[i][:, 2 * j:2 * j + 2, :].rearrange("p r (k e) -> p r e k", e=2), bank(j)[:].rearrange("p (r e k) -> p r e k", r=2, e=2))

        @block.scalar
        def _(act):
            def body(t):
                for i in range(2):
                    tile = 2 * t + i
                    wait(act, projected[PAIR_PART], tile - 1)
                    for j in range(0, PAIRS, 2):
                        act.wait_ge(transposed, PAIRS * tile + j + 1)
                        copy_turned(lambda to, of: nc.scalar.activation(to, of, ACT.Copy), i, j).then_inc(copied_act, 1)
                    wait(act, stored[i], 16 * STORES * t)
                    for part in (W_PART, B_PART, PAIR_PART, X_PART):
                        act.wait_ge(projected[part], tile + 1)
                        last = nc.scalar.activation(evac[i][:, part], m.psum[part][:], ACT.Copy)
                    last.then_inc(evacuated, 1)
            loop_first_peeled(act, TILES // 2, body)

        @block.vector
        def _(dve):
            def body(t):
                for i in range(2):
                    tile = 2 * t + i
                    dve.wait_ge(loaded[i], 48 * (t + 1))
                    for g in range(NG):
                        last = nc.vector.bn_stats(stats[:, g, tile, :], xt[i][:, :, g * GROUP:(g + 1) * GROUP])
                    last.then_inc(measured, 1)
                    wait(dve, projected[PAIR_PART], tile - 1)
                    for j in range(1, PAIRS, 2):
                        dve.wait_ge(transposed, PAIRS * tile + j + 1)
                        copy_turned(nc.vector.tensor_copy, i, j).then_inc(copied_dve, 1)
            loop_first_peeled(dve, TILES // 2, body)

        @block.gpsimd
        def _(pool):
            def body(t):
                for i in range(2):
                    pool.wait_ge(measured, 2 * t + i + 1)
                    nc.gpsimd.tensor_tensor(xt[i][:], xt[i][:], wt[i][:], ALU.mult).then_inc(weighted, 1)
            loop_first_peeled(pool, TILES // 2, body)


def finish_statistics(nc, m, tag, stats, chunks, with_layer_norm, biases=None):
    with ExitStack() as ctx:
        sem = lambda name: ctx.enter_context(nc.semaphore(f"{tag}_{name}"))
        sb = lambda name, shape: ctx.enter_context(nc.sbuf_tensor(f"{tag}_{name}", shape, F32))
        own = sb("own", [P, NG, 2])
        mean_var = sb("mean_var", [P, NG, 2])
        dev = sb("dev", [P, NG])
        var = sb("var", [P, NG])
        ve = sb("ve", [P, NG + 1])
        root = sb("root", [P, NG + 1])
        tmp = sb("tmp", [P, NG + 1])
        inv = sb("inv", [P, NG + 1])
        step, own_ready, mean_mm, dev_ready, dev_mm = sem("step"), sem("own_ready"), sem("mean_mm"), sem("dev_ready"), sem("dev_mm")
        ve_ready, root_ready = sem("ve_ready"), sem("root_ready")
        loaded, pair_loaded = sem("loaded"), sem("pair_loaded")
        if biases:
            w_part, b_part = sb("w_part", [P, KC, NH0, W]), sb("b_part", [P, KC, NH0, W])
        block = ctx.enter_context(nc.Block())

        @block.sync
        def _(sp):
            if biases:
                for part, to in ((1, w_part), (0, m.bias0), (2, b_part)):
                    for a in range(KC):
                        sp.dma_start(to[:, a], biases[0][part, :, a * P:(a + 1) * P, :].rearrange("h p k -> p h k")).then_inc(loaded, 16)
                for a in range(KC):
                    sp.dma_start(m.bias1[:, a], biases[1][:, a * P:(a + 1) * P, :].rearrange("h p k -> p h k")).then_inc(pair_loaded, 16)
                sp.wait_ge(pair_loaded, 16 * KC)

        @block.vector
        def _(dve):
            for g in range(NG):
                last = nc.vector.bn_aggr(own[:, g, :], stats[:, g, 0:chunks(g), :])
            last.then_inc(own_ready, 1)
            chain = Chain(dve, step)
            dve.wait_ge(own_ready, 1)
            dve.wait_ge(mean_mm, 1)
            chain(nc.vector.tensor_copy(mean_var[:], m.psum[0][:, 0:2 * NG].rearrange("p (g s) -> p g s", s=2)))
            chain(nc.vector.tensor_tensor(dev[:], own[:, :, 0], mean_var[:, :, 0], ALU.subtract))
            nc.vector.tensor_tensor(dev[:], dev[:], dev[:], ALU.mult).then_inc(dev_ready, 1)
            dve.wait_ge(dev_mm, 1)
            chain(nc.vector.tensor_tensor(var[:], m.psum[1][:, 0:NG], mean_var[:, :, 1], ALU.add))
            nc.vector.tensor_copy(m.mean[:].rearrange("p (g e) -> p g e", e=GROUP),
                                  mean_var[:, :, 0:1].broadcast_to([P, NG, GROUP]))

            def inverse_root(cols, n):
                dve.wait_ge(root_ready, n)
                chain(nc.vector.reciprocal(inv[:, cols], root[:, cols]))
                chain(nc.vector.tensor_tensor(tmp[:, cols], ve[:, cols], inv[:, cols], ALU.mult))
                chain(nc.vector.tensor_tensor(root[:, cols], root[:, cols], tmp[:, cols], ALU.add))
                chain(nc.vector.reciprocal(tmp[:, cols], root[:, cols]))
                chain(nc.vector.tensor_scalar(inv[:, cols], tmp[:, cols], 2.0, None, ALU.mult))

            nc.vector.tensor_scalar(ve[:, 0:NG], var[:], EPS, None, ALU.add).then_inc(ve_ready, 1)
            inverse_root(slice(0, NG), 1)
            if with_layer_norm:
                chain(nc.vector.tensor_tensor(dev[:], var[:], inv[:, 0:NG], ALU.mult))
                chain(nc.vector.tensor_tensor(var[:], dev[:], inv[:, 0:NG], ALU.mult))
                chain(nc.vector.reduce_sum(tmp[:, NG:NG + 1], var[:], AX.X))
                nc.vector.tensor_scalar(ve[:, NG:NG + 1], tmp[:, NG:NG + 1], 1.0 / NG, EPS, ALU.mult, ALU.add).then_inc(ve_ready, 1)
                inverse_root(slice(NG, NG + 1), 2)
                chain(nc.vector.tensor_scalar(tmp[:, 0:NG], inv[:, 0:NG], inv[:, NG:NG + 1], None, ALU.mult))
                chain(nc.vector.tensor_copy(inv[:, 0:NG], tmp[:, 0:NG]))
            chain(nc.vector.tensor_copy(m.rstd[:].rearrange("p (g e) -> p g e", e=GROUP),
                                        inv[:, 0:NG].rearrange("p (g o) -> p g o", o=1).broadcast_to([P, NG, GROUP])))
            if biases:
                by_column = lambda of: of[:].rearrange("p (o k) -> p o k", o=1).broadcast_to([P, KC * NH0, W])
                flat = lambda of: of[:].rearrange("p a h k -> p (a h) k")
                dve.wait_ge(loaded, 16 * 3 * KC)
                chain(nc.vector.tensor_tensor(flat(w_part), flat(w_part), by_column(m.mean), ALU.mult))
                chain(nc.vector.tensor_tensor(flat(m.bias0), flat(m.bias0), flat(w_part), ALU.subtract))
                chain(nc.vector.tensor_tensor(flat(m.bias0), flat(m.bias0), by_column(m.rstd), ALU.mult))
                chain(nc.vector.tensor_tensor(flat(m.bias0), flat(m.bias0), flat(b_part), ALU.add))

        @block.scalar
        def _(act):
            act.wait_ge(ve_ready, 1)
            nc.scalar.activation(root[:, 0:NG], ve[:, 0:NG], ACT.Sqrt).then_inc(root_ready, 1)
            if with_layer_norm:
                act.wait_ge(ve_ready, 2)
                nc.scalar.activation(root[:, NG:NG + 1], ve[:, NG:NG + 1], ACT.Sqrt).then_inc(root_ready, 1)

        @block.tensor
        def _(pe):
            pe.wait_ge(own_ready, 1)
            nc.tensor.matmul(m.psum[0][:, 0:2 * NG], m.averager[:], own[:].rearrange("p g s -> p (g s)"), start=True, stop=True).then_inc(mean_mm, 1)
            pe.wait_ge(dev_ready, 1)
            nc.tensor.matmul(m.psum[1][:, 0:NG], m.averager[:], dev[:], start=True, stop=True).then_inc(dev_mm, 1)


def layer0(nc, m, x, ln_w, ln_b, x1, stats):
    UNROLL, TILE = 8, 2
    STACK_DMAS = (3, 2)
    Q_HIGH, Q_LOW, K_PARTS = range(3)
    BUFS = UNROLL // TILE
    with ExitStack() as ctx:
        sem = lambda name: ctx.enter_context(nc.semaphore(f"l0_{name}"))
        sb = lambda name, shape: ctx.enter_context(nc.sbuf_tensor(f"l0_{name}", shape, F32))
        xt = sb("x", [P, BUFS, TILE, W])
        wt = sb("ln_w", [P, BUFS, TILE, W])
        bt = sb("ln_b", [P, BUFS, TILE, W])
        sb_pair = lambda name, shape: [ctx.enter_context(nc.sbuf_tensor(f"l0_{name}_{part}", shape, F32R)) for part in ("high", "low")]
        xf = sb("xf", [P, 2, W])
        xn = sb_pair("xn", [P, 4, W])
        qk = sb_pair("qk", [P, 2, HC, W])
        stack = ctx.enter_context(nc.sbuf_tensor("l0_stack", [P, 2, 3, 2, HC, W], F32R))
        probs = sb("probs", [P, NH0, KC, W])
        probs_t = sb("probs_t", [P, NH0, KC, W])
        v = sb("v", [P, 2, KC, HC * P])
        gate = sb("gate", [P, 2, HC, W])
        o = sb("o", [P, HC, W])
        o_parts = sb_pair("o", [P, HC, W])
        y = sb("y", [P, UNROLL, W])
        neg_max = sb("neg_max", [P, NH0, KC])
        total = sb("total", [P, NH0, KC])
        inv = sb("inv", [P, NH0, KC])
        b_qa, b_qb = m.psum[0], m.psum[1]
        b_s, b_t, b_av, b_out = m.psum[2:4], m.psum[4:6], m.psum[6], m.psum[7]
        loaded = [sem(f"loaded{i}") for i in range(BUFS)]
        stacked = [[sem(f"stacked_{name}{i}") for i in range(2)] for name in ("q", "k")]
        y_stored = [sem(f"y_stored{i}") for i in range(BUFS)]
        (xn_step, xn_ready, qa_mm, qb_mm, v_mm, g_mm, qa_high, qb_high, qa_ready, qb_ready, v_ready, g_ready, s_mm, s_ready, exp_ready, inv_ready,
         p_ready, t_mm, t_act, t_dve, av_mm, o_ready, out_mm, y_ready, measured, o_high, o_split, zeroed) = (sem(n) for n in (
            "xn_step", "xn_ready", "qa_mm", "qb_mm", "v_mm", "g_mm", "qa_high", "qb_high", "qa_ready", "qb_ready", "v_ready", "g_ready", "s_mm", "s_ready",
            "exp_ready", "inv_ready", "p_ready", "t_mm", "t_act", "t_dve", "av_mm", "o_ready", "out_mm", "y_ready", "measured", "o_high", "o_split", "zeroed"))
        block = ctx.enter_context(nc.Block())

        def rows(engine, row):
            over_rows(engine, W, UNROLL, row)

        @block.sync
        def _(sp):
            def load(tile, i):
                at = bass.ds(TILE * tile, TILE)
                sp.dma_start(xt[:, i], x[:, at, :]).then_inc(loaded[i], 16)
                sp.dma_start(wt[:, i], ln_w[:, at, :]).then_inc(loaded[i], 16)
                sp.dma_start(bt[:, i], ln_b[:, at, :]).then_inc(loaded[i], 16)

            for i in range(BUFS):
                load(i, i)

            def lay_out(t, k, side):
                r = UNROLL * t + k
                wait(sp, s_mm, NH0 * (r - 1))
                sp.nop(nofuse=True)
                sp.wait_ge((qa_ready, qb_ready)[side], r + 1)
                sp.nop(nofuse=True)
                for half, what, part in (((0, Q_HIGH, 0), (1, Q_HIGH, 0), (0, Q_LOW, 1)), ((0, K_PARTS, 0), (1, K_PARTS, 1)))[side]:
                    to = stack[half * D0:(half + 1) * D0, k % 2, what].bitcast(F32)
                    of = qk[part][:, side].bitcast(F32)
                    sp.dma_start(to.rearrange("p a c t -> p a (c t)"), of.rearrange("p c t -> p (c t)")).then_inc(stacked[side][k % 2], 16)

            def store_and_load(t, k):
                kk = k % UNROLL
                if kk % TILE < TILE - 1:
                    return
                i, tt = kk // TILE, t + (k - kk) // UNROLL
                tile = BUFS * tt + i
                sp.wait_ge(y_ready, TILE * (tile + 1))
                sp.nop(nofuse=True)
                sp.dma_start(x1[:, bass.ds(TILE * tile, TILE), :], y[:, TILE * i:TILE * (i + 1)]).then_inc(y_stored[i], 16)
                if not isinstance(tile, int) or tile + BUFS < W // TILE:
                    load(tile + BUFS, i)

            def row(t, k, has):
                if has(3):
                    lay_out(t, k + 3, 0)
                    lay_out(t, k + 3, 1)
                if has(-1):
                    store_and_load(t, k - 1)
            rows(sp, row)
            for i in range(BUFS):
                sp.wait_ge(y_stored[i], 16 * W // UNROLL)

        @block.gpsimd
        def _(pool):
            def divide(t, k, h):
                n = NH0 * (UNROLL * t + k) + h
                pool.wait_ge(inv_ready, n + 1)
                pool.nop(nofuse=True)
                for c in range(KC):
                    last = nc.gpsimd.tensor_scalar(probs[:, h, c], probs[:, h, c], inv[:, h, c:c + 1], 1.0, ALU.mult, ALU.mult)
                last.then_inc(p_ready, 1)

            def normalise(t, k, part):
                r, kk, tt = UNROLL * t + k, k % UNROLL, t + k // UNROLL
                i, j, whole = kk // TILE, kk % TILE, xf[:, kk % 2]
                high, low = xn[0][:, kk % 4], xn[1][:, kk % 4]
                if part == 0:
                    if j == 0:
                        pool.wait_ge(loaded[i], 48 * (tt + 1))
                    nc.gpsimd.tensor_tensor(whole, xt[:, i, j], m.mean[:], ALU.subtract).then_inc(xn_step, 1)
                    return
                pool.wait_ge(xn_step, 5 * r + part)
                if part == 1:
                    nc.gpsimd.tensor_tensor(whole, whole, m.rstd[:], ALU.mult).then_inc(xn_step, 1)
                elif part == 2:
                    nc.gpsimd.tensor_tensor(whole, whole, wt[:, i, j], ALU.mult).then_inc(xn_step, 1)
                elif part == 3:
                    nc.gpsimd.tensor_tensor(whole, whole, bt[:, i, j], ALU.add).then_inc(xn_step, 1)
                elif part == 4:
                    wait(pool, v_mm, r - 3)
                    wait(pool, g_mm, r - 3)
                    pool.nop(nofuse=True)
                    nc.gpsimd.tensor_scalar(high, whole, 1.0, 1.0, ALU.mult, ALU.mult).then_inc(xn_step, 1)
                else:
                    nc.gpsimd.tensor_tensor(low, whole, high.bitcast(F32), ALU.subtract).then_inc(xn_ready, 1)

            def row(t, k, has):
                if has(2):
                    normalise(t, k + 2, 1)
                    normalise(t, k + 2, 2)
                if has(-1):
                    divide(t, k - 1, 0)
                    divide(t, k - 1, 1)
                    divide(t, k - 1, 2)
                if has(2):
                    normalise(t, k + 2, 3)
                    normalise(t, k + 2, 4)
                if has(-1):
                    divide(t, k - 1, 3)
                if has(2):
                    normalise(t, k + 2, 5)
                if has(3):
                    normalise(t, k + 3, 0)
            rows(pool, row)

        @block.tensor
        def _(pe):
            pe.wait_ge(zeroed, 1)

            def queries(t, k, half):
                r = UNROLL * t + k
                bank, done, free = ((b_qa, qa_mm, v_ready), (b_qb, qb_mm, g_ready))[half]
                pe.wait_ge(xn_ready, r + 1)
                wait(pe, free, r)
                for j in range(2):
                    last = matmul_split(nc, bank[:, j * W:(j + 1) * W], [w[:, half, j] for w in m.wqk], [x_[:, k % 4] for x_ in xn])
                last.then_inc(done, 1)

            def values(t, k):
                r = UNROLL * t + k
                pe.wait_ge(qa_ready, r + 1)
                for c in range(KC):
                    last = matmul_split(nc, b_qa[:, c * W:(c + 1) * W], [x_[:, k % 4, c * P:(c + 1) * P] for x_ in xn], [w[:] for w in m.wv_t])
                last.then_inc(v_mm, 1)

            def gates(t, k):
                r = UNROLL * t + k
                pe.wait_ge(qb_ready, r + 1)
                wait(pe, o_ready, r - 1)
                for c in range(HC):
                    last = matmul_split(nc, b_qb[:, c * W:(c + 1) * W], [w[:, c * P:(c + 1) * P] for w in m.wg_t], [x_[:, k % 4] for x_ in xn])
                last.then_inc(g_mm, 1)

            def scores(t, k, h):
                r = UNROLL * t + k
                n = NH0 * r + h
                if h == 0:
                    for side in range(2):
                        pe.wait_ge(stacked[side][k % 2], 16 * STACK_DMAS[side] * (UNROLL // 2 * t + k // 2 + 1))
                wait(pe, s_ready, n - 1)
                for c in range(KC):
                    for what in (Q_HIGH, Q_LOW):
                        last = nc.tensor.matmul(b_s[h % 2][:, c * W:(c + 1) * W], stack[:, k % 2, what, h % 2, h // 2, c * P:(c + 1) * P],
                                                stack[:, k % 2, K_PARTS, h % 2, h // 2], start=what == Q_HIGH, stop=what == Q_LOW)
                last.then_inc(s_mm, 1)

            def transposes(t, k, h):
                r = UNROLL * t + k
                n = NH0 * r + h
                pe.wait_ge(p_ready, n + 1)
                wait(pe, (t_act, t_dve)[h % 2], 2 * r + h // 2)
                for kc in range(KC):
                    for qc in range(KC):
                        last = nc.tensor.transpose(b_t[h % 2][:, kc * W + qc * P:kc * W + (qc + 1) * P], probs[:, h, qc, kc * P:(kc + 1) * P], m.ident[:])
                last.then_inc(t_mm, 1)

            def attend(t, k, pair):
                r = UNROLL * t + k
                pe.wait_ge(t_act, 2 * r + pair + 1)
                pe.wait_ge(t_dve, 2 * r + pair + 1)
                pe.wait_ge(v_ready, r + 1)
                wait(pe, o_ready, r)
                for kc in range(KC):
                    for j in range(2):
                        h = 2 * pair + j
                        last = nc.tensor.matmul(b_av[D0 * j:D0 * (j + 1), pair * W:(pair + 1) * W], v[:, k % 2, kc, h * D0:(h + 1) * D0],
                                                probs_t[:, h, kc], start=kc == 0, stop=kc == KC - 1)
                last.then_inc(av_mm, 1)

            def project_out(t, k):
                r = UNROLL * t + k
                pe.wait_ge(o_split, r + 1)
                wait(pe, y_ready, r)
                for c in range(HC):
                    last = matmul_split(nc, b_out[:, 0:W], [w[:, c, :] for w in m.wrep_t], [part[:, c] for part in o_parts], start=c == 0, stop=c == HC - 1)
                last.then_inc(out_mm, 1)

            def row(t, k, has):
                if has(-1):
                    project_out(t, k - 1)
                if has(1):
                    transposes(t, k + 1, 0)
                if has(3):
                    queries(t, k + 3, 0)
                if has(1):
                    transposes(t, k + 1, 1)
                if has(2):
                    gates(t, k + 2)
                if has(1):
                    transposes(t, k + 1, 2)
                if has(2):
                    scores(t, k + 2, 0)
                    scores(t, k + 2, 1)
                if has(3):
                    queries(t, k + 3, 1)
                if has(1):
                    transposes(t, k + 1, 3)
                if has(2):
                    scores(t, k + 2, 2)
                if has(1):
                    attend(t, k + 1, 0)
                if has(2):
                    scores(t, k + 2, 3)
                if has(1):
                    attend(t, k + 1, 1)
                if has(3):
                    values(t, k + 3)
            rows(pe, row)

        @block.scalar
        def _(act):
            def exponents(t, k, h):
                n = NH0 * (UNROLL * t + k) + h
                act.wait_ge(s_ready, n + 1)
                for c in range(KC):
                    last = nc.scalar.activation(probs[:, h, c], probs[:, h, c], ACT.Exp, bias=neg_max[:, h, c:c + 1], scale=-1.0,
                                                accum_out=total[:, h, c:c + 1])
                last.then_inc(exp_ready, 1)

            def queries_high(t, k, half):
                r = UNROLL * t + k
                bank, done, high = ((b_qa, qa_mm, qa_high), (b_qb, qb_mm, qb_high))[half]
                act.wait_ge(done, r + 1)
                wait(act, stacked[half][(k - 1) % 2], 16 * STACK_DMAS[half] * (UNROLL // 2 * t + (k + 1) // 2))
                nc.scalar.activation(qk[0][:, half], bank[:].rearrange("p (h c) -> p h c", h=2), ACT.Copy).then_inc(high, 1)

            def output_high(t, k):
                r = UNROLL * t + k
                act.wait_ge(o_ready, r + 1)
                wait(act, out_mm, r)
                nc.scalar.activation(o_parts[0][:], o[:], ACT.Copy).then_inc(o_high, 1)

            def values_out(t, k):
                r = UNROLL * t + k
                act.wait_ge(v_mm, r + 1)
                nc.scalar.activation(v[:, k % 2], b_qa[:].rearrange("p (h c) -> p h c", h=2), ACT.Copy).then_inc(v_ready, 1)

            def gates_out(t, k):
                r = UNROLL * t + k
                act.wait_ge(g_mm, r + 1)
                for c in range(HC):
                    last = nc.scalar.activation(gate[:, k % 2, c], b_qb[:, c * W:(c + 1) * W], ACT.Tanh, bias=m.wg_b_half[:, c:c + 1], scale=0.5)
                last.then_inc(g_ready, 1)

            def transposed_out(t, k, h):
                n = NH0 * (UNROLL * t + k) + h
                act.wait_ge(t_mm, n + 1)
                nc.scalar.activation(probs_t[:, h], b_t[0][:].rearrange("p (a c) -> p a c", a=KC), ACT.Copy).then_inc(t_act, 1)

            def row(t, k, has):
                if has(1):
                    exponents(t, k + 1, 2)
                if has(2):
                    values_out(t, k + 2)
                if has(1):
                    exponents(t, k + 1, 3)
                    transposed_out(t, k + 1, 0)
                if has(3):
                    queries_high(t, k + 3, 0)
                if has(2):
                    gates_out(t, k + 2)
                if has(0):
                    output_high(t, k)
                if has(1):
                    transposed_out(t, k + 1, 2)
                if has(3):
                    queries_high(t, k + 3, 1)
                if has(2):
                    exponents(t, k + 2, 0)
                    exponents(t, k + 2, 1)
            rows(act, row)

        @block.vector
        def _(dve):
            for i in range(2):
                last = nc.vector.memset(stack[D0:P, i, Q_LOW].bitcast(F32), 0.0)
            last.then_inc(zeroed, 1)

            def biased(t, k, h):
                n = NH0 * (UNROLL * t + k) + h
                dve.wait_ge(s_mm, n + 1)
                dve.nop(nofuse=True)
                for c in range(KC):
                    last = nc.vector.tensor_tensor_reduce(out=probs[:, h, c], in0=b_s[h % 2][:, c * W:(c + 1) * W], in1=m.bias0[:, c, h], scale=-1.0,
                                                          scalar=3.0e38, op0=ALU.add, op1=ALU.min, accum_out=neg_max[:, h, c:c + 1])
                last.then_inc(s_ready, 1)

            def inverse(t, k, h):
                n = NH0 * (UNROLL * t + k) + h
                dve.wait_ge(exp_ready, n + 1)
                nc.vector.reciprocal(inv[:, h], total[:, h]).then_inc(inv_ready, 1)

            def queries_low(t, k, half):
                r = UNROLL * t + k
                bank, high, ready = ((b_qa, qa_high, qa_ready), (b_qb, qb_high, qb_ready))[half]
                dve.wait_ge(high, r + 1)
                nc.vector.tensor_tensor(qk[1][:, half], bank[:].rearrange("p (h c) -> p h c", h=2), qk[0][:, half].bitcast(F32), ALU.subtract).then_inc(ready, 1)

            def transposed_out(t, k, h):
                n = NH0 * (UNROLL * t + k) + h
                dve.wait_ge(t_mm, n + 1)
                nc.vector.tensor_copy(probs_t[:, h], b_t[1][:].rearrange("p (a c) -> p a c", a=KC)).then_inc(t_dve, 1)

            def gated(t, k):
                r = UNROLL * t + k
                dve.wait_ge(av_mm, 2 * r + 2)
                dve.wait_ge(g_ready, r + 1)
                wait(dve, o_split, r)
                nc.vector.scalar_tensor_tensor(out=o[:], in0=gate[:, k % 2], scalar=1.0, in1=b_av[:].rearrange("p (a c) -> p a c", a=HC),
                                               op0=ALU.add, op1=ALU.mult).then_inc(o_ready, 1)

            def output_low(t, k):
                dve.wait_ge(o_high, UNROLL * t + k + 1)
                nc.vector.tensor_tensor(o_parts[1][:], o[:], o_parts[0][:].bitcast(F32), ALU.subtract).then_inc(o_split, 1)

            def residual(t, k):
                r, kk = UNROLL * t + k, k % UNROLL
                tt = t + (k - kk) // UNROLL
                i, j = kk // TILE, kk % TILE
                dve.wait_ge(out_mm, r + 1)
                wait(dve, measured, r)
                if j == 0:
                    wait(dve, y_stored[i], 16 * tt)
                nc.vector.scalar_tensor_tensor(out=y[:, kk], in0=b_out[:, 0:W], scalar=m.wrep_b[:], in1=xt[:, i, j],
                                               op0=ALU.add, op1=ALU.add).then_inc(y_ready, 1)
                dve.wait_ge(y_ready, r + 1)
                for g in range(NG // UNROLL * kk, NG // UNROLL * (kk + 1)):
                    columns = slice(g * GROUP, (g + 1) * GROUP)
                    if isinstance(tt, int) and tt == 0:
                        last = nc.vector.bn_stats(stats[:, g, 0, :], y[:, 0:kk + 1, columns])
                    else:
                        last = nc.vector.bn_stats(stats[:, g, tt, :], y[:, :, columns])
                last.then_inc(measured, 1)

            def row(t, k, has):
                if has(1):
                    biased(t, k + 1, 1)
                if has(0):
                    transposed_out(t, k, 3)
                if has(2):
                    queries_low(t, k + 2, 1)
                if has(1):
                    biased(t, k + 1, 2)
                    inverse(t, k + 1, 0)
                if has(-1):
                    output_low(t, k - 1)
                if has(1):
                    inverse(t, k + 1, 1)
                    biased(t, k + 1, 3)
                if has(0):
                    gated(t, k)
                if has(1):
                    inverse(t, k + 1, 2)
                if has(-1):
                    residual(t, k - 1)
                if has(1):
                    inverse(t, k + 1, 3)
                    transposed_out(t, k + 1, 1)
                if has(3):
                    queries_low(t, k + 3, 0)
                if has(2):
                    biased(t, k + 2, 0)
            rows(dve, row)
            for g in range(NG - NG // UNROLL):
                nc.vector.bn_stats(stats[:, g, W // UNROLL, :], y[:, g // (NG // UNROLL) + 1:UNROLL, g * GROUP:(g + 1) * GROUP])


def layer1(nc, m, x1, out):
    UNROLL = 4
    BY_DVE = (3,)
    BY_POOL = (1, 3, 5, 7)
    STACK_DMAS = 3
    OUT_BEHIND = 2
    with ExitStack() as ctx:
        sem = lambda name: ctx.enter_context(nc.semaphore(f"l1_{name}"))
        sb = lambda name, shape, dt=F32: ctx.enter_context(nc.sbuf_tensor(f"l1_{name}", shape, dt))
        xt = sb("x", [P, UNROLL, KC, W])
        xf = sb("xf", [P, HC, W])
        xn = [sb("xn_high", [P, HC, W], F32R), sb("xn_low", [P, HC, W], F32R)]
        qk = [sb("qk_high", [P, 2, HC, W], F32R), sb("qk_low", [P, 2, HC, W], F32R)]
        stack = sb("stack", [3 * D1, 2, 4, 2, HC, W], F32R)
        probs = sb("probs", [P, 4, KC, W])
        probs_t = sb("probs_t", [P, NH1, KC, W])
        v = sb("v", [P, 2, KC, HC * P])
        gate = sb("gate", [P, 2, HC, W])
        o = sb("o", [P, HC, W])
        o_parts = [sb("o_high", [P, HC, W], F32R), sb("o_low", [P, HC, W], F32R)]
        y = sb("y", [P, 2, KC, W])
        neg_max = sb("neg_max", [P, 4, KC])
        total = sb("total", [P, 4, KC])
        inv = sb("inv", [P, 4, KC])
        by_channel = sb("by_channel", [P, 2, HC])
        b_q = m.psum[0]
        b_k = m.psum[1]
        b_s, b_t, b_av = m.psum[2:5], m.psum[5:7], m.psum[7]
        S_BANK = (0, 1, 2, 0, 1, 2, 0, 1)
        S_BACK = (2, 2, 3, 3, 3, 3, 3, 3)
        loaded = [sem(f"loaded{i}") for i in range(UNROLL)]
        y_stored = [sem(f"y_stored{i}") for i in range(2)]
        stacked = [[sem(f"stacked_{name}{i}") for i in range(2)] for name in ("q", "k")]
        (stat_mm, stat_ready, x_mm, x_whole, x_high, x_ready, q_mm, k_mm, v_mm, g_mm, q_high, k_high, q_ready, k_ready, v_ready, g_ready,
         s_mm, max_ready, exp_ready, inv_ready, pool_step, p_dve, p_pool, t_mm, t_act, t_dve, av_mm, o_ready, out_mm,
         y_ready, o_high, o_split) = (sem(n) for n in (
            "stat_mm", "stat_ready", "x_mm", "x_whole", "x_high", "x_ready", "q_mm", "k_mm", "v_mm", "g_mm", "q_high", "k_high", "q_ready",
            "k_ready", "v_ready", "g_ready", "s_mm", "max_ready", "exp_ready", "inv_ready", "pool_step", "p_dve", "p_pool", "t_mm", "t_act",
            "t_dve", "av_mm", "o_ready", "out_mm", "y_ready", "o_high", "o_split"))
        block = ctx.enter_context(nc.Block())

        def count(s, h, heads):
            return len(heads) * s + len([g for g in heads if g <= h])

        BY_ACT = tuple(h for h in range(NH1) if h not in BY_DVE)
        NOT_POOL = tuple(h for h in range(NH1) if h not in BY_POOL)

        def wait_copied(engine, s, h):
            if h in BY_DVE:
                wait(engine, t_dve, count(s, h, BY_DVE))
            else:
                wait(engine, t_act, count(s, h, BY_ACT))

        def rows(engine, row):
            over_rows(engine, C0, UNROLL, row)

        @block.sync
        def _(sp):
            def load(s, i):
                sp.dma_start(xt[:, i], x1[bass.ds(s, 1)].rearrange("o (a p) c -> p (o a) c", p=P)).then_inc(loaded[i], 16)

            def lay_out(t, k, side):
                s = UNROLL * t + k
                wait(sp, s_mm, NH1 * (s - 1))
                sp.nop(nofuse=True)
                sp.wait_ge((q_ready, k_ready)[side], s + 1)
                sp.nop(nofuse=True)
                for third, part in enumerate(((0, 1, 0), (0, 0, 1))[side]):
                    to = stack[third * D1:(third + 1) * D1, k % 2, :, side].bitcast(F32)
                    of = qk[part][:, side].bitcast(F32)
                    sp.dma_start(to.rearrange("p a c t -> p a (c t)"), of.rearrange("p c t -> p (c t)")).then_inc(stacked[side][k % 2], 16)

            for i in range(UNROLL):
                load(i, i)

            def store_and_load(t, k):
                s, i = UNROLL * t + k, k % UNROLL
                tt = t + (k - i) // UNROLL
                sp.wait_ge(y_ready, s + 1)
                sp.nop(nofuse=True)
                sp.dma_start(out[bass.ds(s, 1)].rearrange("o (a p) c -> p (o a) c", p=P), y[:, i % 2]).then_inc(y_stored[i % 2], 16)
                if not isinstance(s, int) or s + UNROLL < C0:
                    load(s + UNROLL, i)

            def row(t, k, has):
                if has(-1):
                    store_and_load(t, k - 1)
                if has(2):
                    lay_out(t, k + 2, 0)
                    lay_out(t, k + 2, 1)
            rows(sp, row)
            for i in range(2):
                sp.wait_ge(y_stored[i], 16 * C0 // 2)

        @block.tensor
        def _(pe):
            def turn(t, k):
                s, i, tt = UNROLL * t + k, k % UNROLL, t + k // UNROLL
                pe.wait_ge(loaded[i], 16 * (tt + 1))
                wait(pe, v_ready, s)
                for c in range(HC):
                    for a in range(KC):
                        last = nc.tensor.transpose(b_q[:, c * W + a * P:c * W + (a + 1) * P], xt[:, i, a, c * P:(c + 1) * P], m.ident[:])
                last.then_inc(x_mm, 1)

            def by_weights(bank, weights):
                for j in range(HC):
                    for c in range(HC):
                        last = matmul_split(nc, bank[:, j * W:(j + 1) * W], [weights(part, c, j) for part in range(2)], [x_[:, c] for x_ in xn],
                                            start=c == 0, stop=c == HC - 1)
                return last

            def queries(t, k):
                s = UNROLL * t + k
                pe.wait_ge(x_ready, s + 1)
                by_weights(b_q, lambda part, c, j: m.w_qk1[part][:, c, 0, j]).then_inc(q_mm, 1)

            def keys(t, k):
                s = UNROLL * t + k
                wait(pe, g_ready, s)
                wait(pe, y_ready, s - OUT_BEHIND)
                by_weights(b_k, lambda part, c, j: m.w_qk1[part][:, c, 1, j]).then_inc(k_mm, 1)

            def values(t, k):
                s = UNROLL * t + k
                pe.wait_ge(q_ready, s + 1)
                for a in range(KC):
                    for c in range(HC):
                        last = matmul_split(nc, b_q[:, a * W:(a + 1) * W], [x_[:, c, a * P:(a + 1) * P] for x_ in xn], [w[:, c] for w in m.w_v1],
                                            start=c == 0, stop=c == HC - 1)
                last.then_inc(v_mm, 1)

            def gates(t, k):
                s = UNROLL * t + k
                pe.wait_ge(k_ready, s + 1)
                wait(pe, o_ready, s - 1)
                by_weights(b_k, lambda part, c, j: m.w_gate1[part][:, c, j * P:(j + 1) * P]).then_inc(g_mm, 1)

            def scores(t, k, h):
                n = NH1 * (UNROLL * t + k) + h
                if h == 0:
                    for side in range(2):
                        pe.wait_ge(stacked[side][k % 2], 16 * STACK_DMAS * (UNROLL // 2 * t + k // 2 + 1))
                wait(pe, exp_ready, n + 1 - S_BACK[h])
                for c in range(KC):
                    last = nc.tensor.matmul(b_s[S_BANK[h]][:, c * W:(c + 1) * W], stack[:, k % 2, h % 4, 0, h // 4, c * P:(c + 1) * P],
                                            stack[:, k % 2, h % 4, 1, h // 4], start=True, stop=True)
                last.then_inc(s_mm, 1)

            def transposes(t, k, h):
                s = UNROLL * t + k
                if h in BY_POOL:
                    pe.wait_ge(p_pool, count(s, h, BY_POOL))
                else:
                    pe.wait_ge(p_dve, count(s, h, NOT_POOL))
                if h >= 2:
                    wait_copied(pe, s, h - 2)
                else:
                    wait_copied(pe, s - 1, h + NH1 - 2)
                for kc in range(KC):
                    for qc in range(KC):
                        last = nc.tensor.transpose(b_t[h % 2][:, kc * W + qc * P:kc * W + (qc + 1) * P], probs[:, h % 4, qc, kc * P:(kc + 1) * P], m.ident[:])
                last.then_inc(t_mm, 1)

            def attend(t, k, half):
                s = UNROLL * t + k
                pe.wait_ge(t_act, count(s, 4 * half + 3, BY_ACT))
                pe.wait_ge(t_dve, count(s, 4 * half + 3, BY_DVE))
                pe.wait_ge(v_ready, s + 1)
                wait(pe, o_ready, s)
                for kc in range(KC):
                    for j in range(4):
                        h = 4 * half + j
                        last = nc.tensor.matmul(b_av[D1 * j:D1 * (j + 1), half * W:(half + 1) * W], v[:, k % 2, kc, h * D1:(h + 1) * D1],
                                                probs_t[:, h, kc], start=kc == 0, stop=kc == KC - 1, tile_position=(0, D1 * j))
                last.then_inc(av_mm, 1)

            def project_out(t, k):
                s = UNROLL * t + k
                gates_before = s + OUT_BEHIND + 1
                pe.wait_ge(o_split, s + 1)
                pe.wait_ge(g_ready, min(gates_before, C0) if isinstance(s, int) else gates_before)
                for a in range(KC):
                    for c in range(HC):
                        last = matmul_split(nc, b_k[:, a * W:(a + 1) * W], [part[:, c, a * P:(a + 1) * P] for part in o_parts], [w[:, c] for w in m.w_out1],
                                            start=c == 0, stop=c == HC - 1)
                last.then_inc(out_mm, 1)

            for c in range(HC):
                nc.tensor.transpose(b_q[:, c * P:(c + 1) * P], m.mean[:, c * P:(c + 1) * P], m.ident[:])
                last = nc.tensor.transpose(b_k[:, c * P:(c + 1) * P], m.rstd[:, c * P:(c + 1) * P], m.ident[:])
            last.then_inc(stat_mm, 1)
            pe.wait_ge(stat_ready, 1)
            def row(t, k, has):
                if has(0):
                    scores(t, k, 3)
                if has(1):
                    queries(t, k + 1)
                    keys(t, k + 1)
                if has(0):
                    transposes(t, k, 0)
                    scores(t, k, 4)
                    transposes(t, k, 1)
                if has(-1):
                    attend(t, k - 1, 1)
                if has(0):
                    transposes(t, k, 2)
                    scores(t, k, 5)
                    scores(t, k, 6)
                if has(1):
                    values(t, k + 1)
                if has(0):
                    transposes(t, k, 3)
                    scores(t, k, 7)
                if has(1):
                    gates(t, k + 1)
                if has(0):
                    transposes(t, k, 4)
                if has(2):
                    turn(t, k + 2)
                if has(0):
                    attend(t, k, 0)
                if has(1):
                    scores(t, k + 1, 0)
                if has(0):
                    transposes(t, k, 5)
                if has(1):
                    scores(t, k + 1, 1)
                if has(0):
                    transposes(t, k, 6)
                if has(1):
                    scores(t, k + 1, 2)
                if has(-1):
                    project_out(t, k - 1)
                if has(0):
                    transposes(t, k, 7)
            rows(pe, row)

        @block.scalar
        def _(act):
            def exponents(t, k, h):
                n = NH1 * (UNROLL * t + k) + h
                act.wait_ge(max_ready, n + 1)
                for c in range(KC):
                    last = nc.scalar.activation(probs[:, h % 4, c], b_s[S_BANK[h]][:, c * W:(c + 1) * W], ACT.Exp, bias=neg_max[:, h % 4, c:c + 1],
                                                accum_out=total[:, h % 4, c:c + 1])
                last.then_inc(exp_ready, 1)

            def x_high_part(t, k):
                s = UNROLL * t + k
                wait(act, g_mm, s)
                act.wait_ge(x_whole, s + 1)
                nc.scalar.activation(xn[0][:], xf[:], ACT.Copy).then_inc(x_high, 1)

            def high(t, k, what):
                s = UNROLL * t + k
                bank, done, mine = ((b_q, q_mm, q_high), (b_k, k_mm, k_high))[what]
                act.wait_ge(done, s + 1)
                wait(act, stacked[what][(k - 1) % 2], 16 * STACK_DMAS * (UNROLL // 2 * t + (k + 1) // 2))
                nc.scalar.activation(qk[0][:, what], bank[:].rearrange("p (a c) -> p a c", a=HC), ACT.Copy).then_inc(mine, 1)

            def output_high(t, k):
                s = UNROLL * t + k
                act.wait_ge(o_ready, s + 1)
                wait(act, out_mm, s)
                nc.scalar.activation(o_parts[0][:], o[:], ACT.Copy).then_inc(o_high, 1)

            def values_out(t, k):
                s = UNROLL * t + k
                act.wait_ge(v_mm, s + 1)
                nc.scalar.activation(v[:, k % 2], b_q[:].rearrange("p (a c) -> p a c", a=KC), ACT.Copy).then_inc(v_ready, 1)

            def gates_out(t, k):
                s = UNROLL * t + k
                act.wait_ge(g_mm, s + 1)
                nc.scalar.activation(gate[:, k % 2], b_k[:].rearrange("p (a c) -> p a c", a=HC), ACT.Tanh, scale=0.5).then_inc(g_ready, 1)

            def transposed_out(t, k, h):
                n = NH1 * (UNROLL * t + k) + h
                act.wait_ge(t_mm, n + 1)
                nc.scalar.activation(probs_t[:, h], b_t[h % 2][:].rearrange("p (a c) -> p a c", a=KC), ACT.Copy).then_inc(t_act, 1)

            def row(t, k, has):
                if has(0):
                    exponents(t, k, 0)
                    exponents(t, k, 1)
                if has(-1):
                    transposed_out(t, k - 1, 6)
                if has(0):
                    exponents(t, k, 2)
                if has(-1):
                    transposed_out(t, k - 1, 7)
                if has(1):
                    high(t, k + 1, 0)
                if has(0):
                    exponents(t, k, 3)
                if has(1):
                    high(t, k + 1, 1)
                if has(0):
                    transposed_out(t, k, 0)
                    transposed_out(t, k, 1)
                    exponents(t, k, 4)
                    transposed_out(t, k, 2)
                if has(-1):
                    output_high(t, k - 1)
                if has(0):
                    exponents(t, k, 5)
                    exponents(t, k, 6)
                if has(1):
                    values_out(t, k + 1)
                if has(0):
                    exponents(t, k, 7)
                if has(1):
                    gates_out(t, k + 1)
                if has(0):
                    transposed_out(t, k, 4)
                if has(2):
                    x_high_part(t, k + 2)
                if has(0):
                    transposed_out(t, k, 5)
            rows(act, row)

        @block.vector
        def _(dve):
            def maxima(t, k, h):
                n = NH1 * (UNROLL * t + k) + h
                dve.wait_ge(s_mm, n + 1)
                nc.vector.tensor_reduce(neg_max[:, h % 4], b_s[S_BANK[h]][:].rearrange("p (a c) -> p a c", a=KC), AX.X, ALU.max, negate=True).then_inc(max_ready, 1)

            def inverse(t, k, h):
                n = NH1 * (UNROLL * t + k) + h
                dve.wait_ge(exp_ready, n + 1)
                nc.vector.reciprocal(inv[:, h % 4], total[:, h % 4]).then_inc(inv_ready, 1)

            def divide(t, k, h):
                n = NH1 * (UNROLL * t + k) + h
                dve.wait_ge(inv_ready, n + 1)
                for c in range(KC):
                    last = nc.vector.scalar_tensor_tensor(out=probs[:, h % 4, c], in0=probs[:, h % 4, c], scalar=inv[:, h % 4, c:c + 1], in1=m.bias1[:, c, h],
                                                          op0=ALU.mult, op1=ALU.add)
                last.then_inc(p_dve, 1)

            def transposed_out(t, k, h):
                n = NH1 * (UNROLL * t + k) + h
                dve.wait_ge(t_mm, n + 1)
                nc.vector.tensor_copy(probs_t[:, h], b_t[h % 2][:].rearrange("p (a c) -> p a c", a=KC)).then_inc(t_dve, 1)

            def group_norm(t, k):
                s = UNROLL * t + k
                dve.wait_ge(x_mm, s + 1)
                for c in range(HC):
                    last = nc.vector.tensor_scalar(xf[:, c], b_q[:, c * W:(c + 1) * W], by_channel[:, 0, c:c + 1], by_channel[:, 1, c:c + 1],
                                                   ALU.subtract, ALU.mult)
                last.then_inc(x_whole, 1)

            def low(t, k, what):
                s = UNROLL * t + k
                bank, high, ready = ((b_q, q_high, q_ready), (b_k, k_high, k_ready))[what]
                dve.wait_ge(high, s + 1)
                nc.vector.tensor_tensor(qk[1][:, what], bank[:].rearrange("p (a c) -> p a c", a=HC), qk[0][:, what].bitcast(F32), ALU.subtract).then_inc(ready, 1)

            def gated(t, k):
                s = UNROLL * t + k
                dve.wait_ge(av_mm, 2 * s + 2)
                dve.wait_ge(g_ready, s + 1)
                wait(dve, o_split, s)
                nc.vector.scalar_tensor_tensor(out=o[:], in0=gate[:, k % 2], scalar=1.0, in1=b_av[:].rearrange("p (a c) -> p a c", a=HC),
                                               op0=ALU.add, op1=ALU.mult).then_inc(o_ready, 1)

            def residual(t, k):
                s, i = UNROLL * t + k, k % UNROLL
                tt = t + (k - i) // UNROLL
                dve.wait_ge(out_mm, s + 1)
                wait(dve, y_stored[i % 2], 16 * (UNROLL // 2 * tt + i // 2))
                nc.vector.tensor_tensor(y[:, i % 2], b_k[:].rearrange("p (a c) -> p a c", a=KC), xt[:, i], ALU.add).then_inc(y_ready, 1)

            dve.wait_ge(stat_mm, 1)
            nc.vector.tensor_copy(by_channel[:, 0], b_q[:, 0:HC * P].rearrange("p (c n) -> p c n", n=P)[:, :, 0])
            nc.vector.tensor_copy(by_channel[:, 1], b_k[:, 0:HC * P].rearrange("p (c n) -> p c n", n=P)[:, :, 0]).then_inc(stat_ready, 1)
            dve.wait_ge(stat_ready, 1)
            def row(t, k, has):
                if has(1):
                    low(t, k + 1, 1)
                if has(-1):
                    gated(t, k - 1)
                if has(0):
                    maxima(t, k, 5)
                    maxima(t, k, 6)
                    inverse(t, k, 4)
                    divide(t, k, 4)
                    inverse(t, k, 5)
                    maxima(t, k, 7)
                    transposed_out(t, k, 3)
                    inverse(t, k, 6)
                    divide(t, k, 6)
                    inverse(t, k, 7)
                if has(2):
                    group_norm(t, k + 2)
                if has(1):
                    maxima(t, k + 1, 0)
                    maxima(t, k + 1, 1)
                    maxima(t, k + 1, 2)
                    inverse(t, k + 1, 0)
                    divide(t, k + 1, 0)
                    inverse(t, k + 1, 1)
                if has(-1):
                    residual(t, k - 1)
                if has(1):
                    maxima(t, k + 1, 3)
                    inverse(t, k + 1, 2)
                    divide(t, k + 1, 2)
                if has(2):
                    low(t, k + 2, 0)
                if has(1):
                    inverse(t, k + 1, 3)
                    maxima(t, k + 1, 4)
            rows(dve, row)

        @block.gpsimd
        def _(pool):
            def x_low_part(t, k):
                s = UNROLL * t + k
                pool.wait_ge(x_high, s + 1)
                nc.gpsimd.tensor_tensor(xn[1][:], xf[:], xn[0][:].bitcast(F32), ALU.subtract).then_inc(x_ready, 1)

            def output_low(t, k):
                pool.wait_ge(o_high, UNROLL * t + k + 1)
                nc.gpsimd.tensor_tensor(o_parts[1][:], o[:], o_parts[0][:].bitcast(F32), ALU.subtract).then_inc(o_split, 1)

            def divide(t, k, h):
                s = UNROLL * t + k
                n = NH1 * s + h
                pool.wait_ge(inv_ready, n + 1)
                pool.nop(nofuse=True)
                for c in range(KC):
                    last = nc.gpsimd.tensor_scalar(probs[:, h % 4, c], probs[:, h % 4, c], inv[:, h % 4, c:c + 1], 1.0, ALU.mult, ALU.mult)
                last.then_inc(pool_step, 1)
                pool.wait_ge(pool_step, count(s, h, BY_POOL))
                nc.gpsimd.tensor_tensor(probs[:, h % 4], probs[:, h % 4], m.bias1[:, :, h], ALU.add).then_inc(p_pool, 1)

            def row(t, k, has):
                if has(0):
                    divide(t, k, 3)
                if has(-1):
                    output_low(t, k - 1)
                if has(0):
                    divide(t, k, 5)
                    divide(t, k, 7)
                if has(2):
                    x_low_part(t, k + 2)
                if has(1):
                    divide(t, k + 1, 1)
            rows(pool, row)


class Memory:
    pass


def build(nc, x, ln_w, ln_b, wq, wk, wv, wb, wg_w, wg_b, wrep_w, wrep_b, pair_repr, gate_proj, qkv_proj, out_proj, bias_proj, out):
    m = Memory()
    with ExitStack() as ctx:
        sb = lambda name, shape: ctx.enter_context(nc.sbuf_tensor(name, shape, F32))
        m.psum = [ctx.enter_context(nc.psum_tensor(f"bank{i}", [P, 512], F32)) for i in range(8)]
        m.ident = sb("ident", [P, P])
        m.averager = sb("averager", [P, P])

        def pair(name, shape):
            return [ctx.enter_context(nc.sbuf_tensor(f"{name}_{part}", shape, F32R)) for part in ("high", "low")]

        m.wqk = pair("wqk", [C0, 2, HC, P])
        m.wv_t = pair("wv_t", [C0, 256])
        m.wg_t = pair("wg_t", [C0, 256])
        m.wrep_t = pair("wrep_t", [P, HC, C0])
        m.wb_t = sb("wb_t", [C0, 32])
        m.wg_b_half = sb("wg_b_half", [P, HC])
        m.wrep_b = sb("wrep_b", [C0, 1])
        m.w_pair = sb("w_pair", [P, 32])
        m.w_qk1 = pair("w_qk1", [P, HC, 2, HC, P])
        m.w_v1 = pair("w_v1", [P, HC, 256])
        m.w_gate1 = pair("w_gate1", [P, HC, 256])
        m.w_out1 = pair("w_out1", [P, HC, 256])
        m.bias0 = sb("bias0", [P, KC, NH0, W])
        m.bias1 = sb("bias1", [P, KC, NH1, W])
        m.mean = sb("mean", [P, W])
        m.rstd = sb("rstd", [P, W])
        stats = sb("chunk_stats", [P, NG, W // 8 + 1, 6])
        image_parts = nc.dram_tensor("image_bias_parts", (3, NH0, W, W), F32).ap()
        pair_bias = nc.dram_tensor("pair_bias", (NH1, W, W), F32).ap()
        x1 = nc.dram_tensor("x1", (C0, W, W), F32).ap()
        x, pair_repr, out = x[0], pair_repr[0], out[0]
        args = {"wq": wq, "wk": wk, "wv": wv, "wg_w": wg_w, "wrep_w": wrep_w, "wg_b": wg_b, "wrep_b": wrep_b, "gate_proj": gate_proj,
                "qkv_proj": qkv_proj, "out_proj": out_proj, "wb": wb, "bias_proj": bias_proj}
        with ExitStack() as tiles:
            image = ImageTiles(nc, tiles, x, ln_w, ln_b)

            def load_first_tiles(sp):
                for i in range(2):
                    image.load(sp, i, i)

            prepare_weights(nc, m, args, load_first_tiles)
            first_pass(nc, m, image, pair_repr, image_parts, pair_bias, stats)
        finish_statistics(nc, m, "gs0", stats, lambda g: W // 8, True, (image_parts, pair_bias))
        layer0(nc, m, x, ln_w, ln_b, x1, stats)
        finish_statistics(nc, m, "gs1", stats, lambda g: W // 8 + (g < NG - 4), False)
        layer1(nc, m, x1, out)


_INS = ["x", "L0_conv_ln_w", "L0_conv_ln_b", "L0_conv_wq", "L0_conv_wk", "L0_conv_wv", "L0_conv_wb", "L0_conv_wg_w", "L0_conv_wg_b",
        "L0_conv_wrep_w", "L0_conv_wrep_b", "L1_conv_pair_repr", "L1_conv_gate_proj", "L1_conv_qkv_proj", "L1_conv_out_proj", "L1_conv_bias_proj"]


def kernel(**inputs):
    import numpy as _np
    import concourse.bacc as _bacc
    from concourse import mybir as _mybir
    from concourse.bass_utils import run_bass_kernel_spmd as _run

    nc = _bacc.Bacc("TRN2", target_bir_lowering=False, num_devices=1)
    arrays, args = {}, []
    for name in _INS:
        a = _np.ascontiguousarray(inputs[name])
        arrays[f"in_{name}_dram"] = a
        args.append(nc.dram_tensor(f"in_{name}_dram", a.shape, _mybir.dt.from_np(a.dtype), kind="ExternalInput").ap())
    args.append(nc.dram_tensor("out_dram", (1, 128, 256, 256), _mybir.dt.from_np(_np.dtype("float32")), kind="ExternalOutput").ap())
    build(nc, *args)
    r = _run(nc, [arrays], core_ids=[0])
    return r.results[0]["out_dram"]
```
